# Optimizing a Trainium2 kernel written in Bass

```python
import numpy as np
import jax
import jax.numpy as jnp

def _softmax(x, axis=-1):
    return jax.nn.softmax(x, axis=axis)

def _gelu(x):
    return jax.nn.gelu(x, approximate=True)

def _silu(x):
    return jax.nn.silu(x)

def _sigmoid(x):
    return jax.nn.sigmoid(x)

def _layernorm(x, axis=-1, eps=1e-05):
    m = jnp.mean(x, axis=axis, keepdims=True)
    v = jnp.var(x, axis=axis, keepdims=True)
    return (x - m) / jnp.sqrt(v + eps)

def _scatter_add(tgt, idx, src, axis=0):
    return tgt.at[idx].add(src)

def _segment_sum(src, seg, n):
    return jax.ops.segment_sum(src, seg, n)
kernel_name = 'mk_decoder_preln_d2_seqx_r4_8694d9'

def setup_inputs(seed: int=0):
    np.random.seed(seed)
    _w = jnp.asarray

    def _rec_inputs():
        import jax
        import jax.numpy as jnp
        _rk = jax.random.key(seed)
        x = 2.818e-05 + 1 * jax.random.normal(jax.random.fold_in(_rk, 1), (8, 256, 256), jnp.float32)
        _lenS = 256 - jax.random.randint(jax.random.fold_in(_rk, 7), (8,), 0, max(1, 256 // 4) + 1, jnp.int32)
        _lenS2 = 256 - jax.random.randint(jax.random.fold_in(_rk, 8), (8,), 0, max(1, 256 // 4) + 1, jnp.int32)
        _ctx_2048P = jax.random.normal(jax.random.fold_in(_rk, 11), (8, 16, 512), jnp.float32)
        _ctx_2048c = jax.random.dirichlet(jax.random.fold_in(_rk, 511), 0.3 * jnp.ones((16,), jnp.float32), (8, 256))
        _ctx_2048t = jnp.einsum('bsk,bkd->bsd', _ctx_2048c, _ctx_2048P)
        _ctx_2048t = _ctx_2048t * jax.lax.rsqrt(jnp.mean(jnp.square(_ctx_2048t)) + 1e-12) * 0.953939
        ctx_2048 = -0.000125008 + 0.999885 * (_ctx_2048t + 0.3 * jax.random.normal(jax.random.fold_in(_rk, 611), (8, 256, 512), jnp.float32))
        _validS = jnp.arange(256)[None, :] < _lenS[:, None]
        _validS2 = jnp.arange(256)[None, :] < _lenS2[:, None]
        _causal = jnp.tril(jnp.ones((256, 256), dtype=bool))
        mask_BxS2_fk1 = jnp.where(jnp.broadcast_to(_validS2[:, :], (8, 256)), 1.0, 0.0).astype(jnp.float32)
        mask_BxS2_if0 = jnp.where(jnp.ones((8, 256), dtype=bool), 4, 0).astype(jnp.int32)
        return (x, ctx_2048, mask_BxS2_fk1, mask_BxS2_if0)
    x, ctx_2048, mask_BxS2_fk1, mask_BxS2_if0 = _rec_inputs()

    def _L0_attn_setup():
        import jax, jax.numpy as jnp
        import numpy as np
        B, N, D_IN, D_OUT, HEADS = (4, 1024, 256, 256, 16)
        D_HEAD = D_OUT // HEADS
        key = jax.random.key(seed)
        ks = jax.random.split(key, 5)
        x = jax.random.normal(ks[0], (B, N, D_IN), dtype=jnp.float32)
        s_in = 1.0 / np.sqrt(D_IN)
        s_out = 1.0 / np.sqrt(D_OUT)
        Wq = jax.random.normal(ks[1], (D_IN, D_OUT), dtype=jnp.float32) * s_in
        Wk = jax.random.normal(ks[2], (D_IN, D_OUT), dtype=jnp.float32) * s_in
        Wv = jax.random.normal(ks[3], (D_IN, D_OUT), dtype=jnp.float32) * s_in
        Wo = jax.random.normal(ks[4], (D_OUT, D_OUT), dtype=jnp.float32) * s_out
        bo = jnp.zeros((D_OUT,), dtype=jnp.float32)
        return {'x': x, 'Wq': Wq, 'Wk': Wk, 'Wv': Wv, 'Wo': Wo, 'bo': bo}
    _L0_attn_all = _L0_attn_setup()
    _L0_attn_in = {k: v for k, v in _L0_attn_all.items() if k in ('Wq', 'Wk', 'Wv', 'Wo', 'bo')}
    del _L0_attn_all

    def _L0_xattn_setup():
        import jax, jax.numpy as jnp
        import numpy as np
        B, S, T = (32, 128, 128)
        SRC_SIZE, TGT_SIZE, OUT_SIZE, NUM_HEAD = (512, 256, 256, 8)
        HEAD_DIM = OUT_SIZE // NUM_HEAD
        key = jax.random.key(seed)
        ks = jax.random.split(key, 12)
        src = jax.random.normal(ks[0], (B, S, SRC_SIZE), dtype=jnp.float32)
        tgt = jax.random.normal(ks[1], (B, T, TGT_SIZE), dtype=jnp.float32)
        src_mask = (jax.random.uniform(ks[2], (B, S)) > 0.3).astype(jnp.float32)
        src_mask = src_mask.at[:, 0].set(1.0)
        tgt_mask = (jax.random.uniform(ks[3], (B, T)) > 0.3).astype(jnp.float32)
        tgt_mask = tgt_mask.at[:, 0].set(1.0)

        def lin(k, out_f, in_f):
            return jax.random.normal(k, (out_f, in_f), dtype=jnp.float32) / np.sqrt(in_f)
        W_src = lin(ks[4], 2 * OUT_SIZE, SRC_SIZE)
        b_src = jnp.zeros((2 * OUT_SIZE,), jnp.float32)
        W_tgt = lin(ks[5], OUT_SIZE, TGT_SIZE)
        b_tgt = jnp.zeros((OUT_SIZE,), jnp.float32)
        W_out = lin(ks[6], OUT_SIZE, OUT_SIZE + TGT_SIZE)
        b_out = jnp.zeros((OUT_SIZE,), jnp.float32)
        return {'src': src, 'tgt': tgt, 'src_mask': src_mask, 'tgt_mask': tgt_mask, 'W_src': W_src, 'b_src': b_src, 'W_tgt': W_tgt, 'b_tgt': b_tgt, 'W_out': W_out, 'b_out': b_out}
    _L0_xattn_all = _L0_xattn_setup()
    _L0_xattn_in = {k: v for k, v in _L0_xattn_all.items() if k in ('W_src', 'b_src', 'W_tgt', 'b_tgt', 'W_out', 'b_out')}
    del _L0_xattn_all

    def _L0_ffn_setup():
        import jax, jax.numpy as jnp
        import numpy as np
        B, T, D, F_FF, E, TOP_K = (8, 512, 256, 1024, 8, 2)
        CAP_FACTOR = 1.25
        key = jax.random.key(seed)
        ks = jax.random.split(key, 7)
        s = 0.02
        return {'x': jax.random.normal(ks[0], (B, T, D), dtype=jnp.float32), 'w_router': jax.random.normal(ks[1], (D, E), dtype=jnp.float32) * s, 'b_router': jnp.zeros((E,), dtype=jnp.float32), 'w1': jax.random.normal(ks[2], (E, D, F_FF), dtype=jnp.float32) * s, 'b1': jnp.zeros((E, F_FF), dtype=jnp.float32), 'w2': jax.random.normal(ks[3], (E, F_FF, D), dtype=jnp.float32) * s, 'b2': jnp.zeros((E, D), dtype=jnp.float32)}
    _L0_ffn_all = _L0_ffn_setup()
    _L0_ffn_in = {k: v for k, v in _L0_ffn_all.items() if k in ('w_router', 'b_router', 'w1', 'b1', 'w2', 'b2')}
    del _L0_ffn_all

    def _L1_attn_setup():
        import math
        import jax, jax.numpy as jnp
        import numpy as np
        D_MODEL = 256
        N_HEADS = 16
        BLOCK = 512
        EPS2 = 0.0487
        ROPE_BASE = 10000.0

        def _riemann_zeros(K):
            n = np.arange(1, K + 1, dtype=np.float64)
            t = 10.0 + 6.0 * n
            for _ in range(60):
                f = t / (2 * np.pi) * np.log(t / (2 * np.pi * np.e)) - (n - 0.875)
                fp = np.log(t / (2 * np.pi)) / (2 * np.pi)
                t = t - f / fp
            return t

        def _constants(N, K):
            g = _riemann_zeros(K)
            g = g / g[0]
            denom = 0.25 + g * g
            w_re = (0.5 / denom).astype(np.float32)
            w_im = (-g / denom).astype(np.float32)
            pos = np.arange(N, dtype=np.float32)
            k_idx = np.arange(K, dtype=np.float32)
            inv_freq = ROPE_BASE ** (-k_idx / K)
            phase = pos[:, None] * inv_freq[None, :]
            cos_p = np.cos(phase).astype(np.float32)
            sin_p = np.sin(phase).astype(np.float32)
            log1p = np.log1p(pos)
            log_decay = (0.5 * (log1p[None, :] - log1p[:, None])).astype(np.float32)
            tril = np.tril(np.ones((N, N), dtype=bool))
            return (jnp.asarray(w_re), jnp.asarray(w_im), jnp.asarray(cos_p), jnp.asarray(sin_p), jnp.asarray(log_decay), jnp.asarray(tril))
        key = jax.random.key(seed)
        kx, kq, kk, kv, ko = jax.random.split(key, 5)
        B, N, D = (2, BLOCK, D_MODEL)
        s = 0.02
        return {'x': jax.random.normal(kx, (B, N, D), jnp.float32), 'Wq': jax.random.normal(kq, (D, D), jnp.float32) * s, 'Wk': jax.random.normal(kk, (D, D), jnp.float32) * s, 'Wv': jax.random.normal(kv, (D, D), jnp.float32) * s, 'Wo': jax.random.normal(ko, (D, D), jnp.float32) * s}
    _L1_attn_all = _L1_attn_setup()
    _L1_attn_in = {k: v for k, v in _L1_attn_all.items() if k in ('Wq', 'Wk', 'Wv', 'Wo')}
    del _L1_attn_all

    def _L1_xattn_setup():
        import jax, jax.numpy as jnp
        import numpy as np
        B, L, P = (4, 1024, 256)
        D_MODEL = 256
        D_GLOBAL = 512
        HEADDIM = 32
        EPSILON = 0.001
        RMS_EPS = 1e-05

        def rmsnorm(x, g, eps=RMS_EPS):
            var = jnp.mean(jnp.square(x), axis=-1, keepdims=True)
            return x * jax.lax.rsqrt(var + eps) * g

        def _hnet_depool(h, h_patch_full, patch_lens):
            h_patch = h_patch_full[..., :D_MODEL]
            bsz, plen = (h_patch.shape[0], h_patch.shape[1])
            seqlen = h.shape[1]
            logp = jnp.full((bsz, plen), -EPSILON, dtype=jnp.float32)
            bidx = jnp.cumsum(patch_lens, axis=1) - 1
            boundary_mask = jnp.zeros((bsz, seqlen), dtype=jnp.int32)
            boundary_mask = boundary_mask.at[jnp.arange(bsz)[:, None], bidx].set(1)
            dt = (-jnp.log(-jnp.expm1(logp))).astype(h_patch.dtype)
            x = h_patch / dt[..., None]
            n_heads = D_MODEL // HEADDIM
            A = -jnp.ones((n_heads,), dtype=jnp.float32)
            bcoef = jnp.exp(logp).astype(h_patch.dtype)
            x4 = x.reshape(bsz, plen, n_heads, HEADDIM)
            a = jnp.exp(dt[:, :, None] * A[None, None, :])
            u = (dt * bcoef)[:, :, None, None] * x4
            a_b = jnp.broadcast_to(a[..., None], u.shape)

            def comb(lft, rgt):
                aL, uL = lft
                aR, uR = rgt
                return (aL * aR, uL * aR + uR)
            _, s = jax.lax.associative_scan(comb, (a_b, u), axis=1)
            depool = s.reshape(bsz, plen, D_MODEL)
            plug = jnp.clip(jnp.cumsum(boundary_mask, axis=1) - 1, 0, plen - 1)
            depool_out = depool[jnp.arange(bsz)[:, None], plug]
            return depool_out + h
        key = jax.random.key(seed)
        k1, k2, k3, k4 = jax.random.split(key, 4)
        embeds = jax.random.normal(k1, (B, L, D_MODEL), dtype=jnp.float32)
        patch_embeds = jax.random.normal(k2, (B, P, D_GLOBAL), dtype=jnp.float32)
        patch_lens = jnp.full((B, P), L // P, dtype=jnp.int64)
        W_in = jax.random.normal(k3, (D_MODEL, D_MODEL), dtype=jnp.float32) * 0.02
        b_in = jnp.zeros((D_MODEL,), dtype=jnp.float32)
        g_res = jnp.ones((D_MODEL,), dtype=jnp.float32)
        g_init = jnp.ones((D_GLOBAL,), dtype=jnp.float32)
        return {'embeds': embeds, 'patch_embeds': patch_embeds, 'patch_lens': patch_lens, 'W_in': W_in, 'b_in': b_in, 'g_res': g_res, 'g_init': g_init}
    _L1_xattn_all = _L1_xattn_setup()
    _L1_xattn_in = {k: v for k, v in _L1_xattn_all.items() if k in ('W_in', 'b_in', 'g_res', 'g_init')}
    del _L1_xattn_all

    def _L1_ffn_setup():
        import jax, jax.numpy as jnp
        import numpy as np
        NEG_INF = -1e+30
        K = 2
        key = jax.random.key(seed)
        ks = jax.random.split(key, 5)
        B, S, D, O, E = (8, 512, 256, 256, 8)
        scale = 1.0 / np.sqrt(D)
        return {'x': jax.random.normal(ks[0], (B, S, D), dtype=jnp.float32), 'gate_w': jax.random.normal(ks[1], (E, D), dtype=jnp.float32) * scale, 'gate_b': jnp.zeros((E,), dtype=jnp.float32), 'expert_w': jax.random.normal(ks[2], (E, O, D), dtype=jnp.float32) * scale, 'expert_b': jnp.zeros((E, O), dtype=jnp.float32)}
    _L1_ffn_all = _L1_ffn_setup()
    _L1_ffn_in = {k: v for k, v in _L1_ffn_all.items() if k in ('gate_w', 'gate_b', 'expert_w', 'expert_b')}
    del _L1_ffn_all
    return {'x': x, 'ctx_2048': ctx_2048, 'mask_BxS2_fk1': mask_BxS2_fk1, 'mask_BxS2_if0': mask_BxS2_if0, 'L0_attn_Wq': _L0_attn_in['Wq'], 'L0_attn_Wk': _L0_attn_in['Wk'], 'L0_attn_Wv': _L0_attn_in['Wv'], 'L0_attn_Wo': _L0_attn_in['Wo'], 'L0_attn_bo': _L0_attn_in['bo'], 'L0_xattn_W_src': _L0_xattn_in['W_src'], 'L0_xattn_b_src': _L0_xattn_in['b_src'], 'L0_xattn_W_tgt': _L0_xattn_in['W_tgt'], 'L0_xattn_b_tgt': _L0_xattn_in['b_tgt'], 'L0_xattn_W_out': _L0_xattn_in['W_out'], 'L0_xattn_b_out': _L0_xattn_in['b_out'], 'L0_ffn_w_router': _L0_ffn_in['w_router'], 'L0_ffn_b_router': _L0_ffn_in['b_router'], 'L0_ffn_w1': _L0_ffn_in['w1'], 'L0_ffn_b1': _L0_ffn_in['b1'], 'L0_ffn_w2': _L0_ffn_in['w2'], 'L0_ffn_b2': _L0_ffn_in['b2'], 'L1_attn_Wq': _L1_attn_in['Wq'], 'L1_attn_Wk': _L1_attn_in['Wk'], 'L1_attn_Wv': _L1_attn_in['Wv'], 'L1_attn_Wo': _L1_attn_in['Wo'], 'L1_xattn_W_in': _L1_xattn_in['W_in'], 'L1_xattn_b_in': _L1_xattn_in['b_in'], 'L1_xattn_g_res': _L1_xattn_in['g_res'], 'L1_xattn_g_init': _L1_xattn_in['g_init'], 'L1_ffn_gate_w': _L1_ffn_in['gate_w'], 'L1_ffn_gate_b': _L1_ffn_in['gate_b'], 'L1_ffn_expert_w': _L1_ffn_in['expert_w'], 'L1_ffn_expert_b': _L1_ffn_in['expert_b']}

def reference(x, ctx_2048, mask_BxS2_fk1, mask_BxS2_if0, L0_attn_Wq, L0_attn_Wk, L0_attn_Wv, L0_attn_Wo, L0_attn_bo, L0_xattn_W_src, L0_xattn_b_src, L0_xattn_W_tgt, L0_xattn_b_tgt, L0_xattn_W_out, L0_xattn_b_out, L0_ffn_w_router, L0_ffn_b_router, L0_ffn_w1, L0_ffn_b1, L0_ffn_w2, L0_ffn_b2, L1_attn_Wq, L1_attn_Wk, L1_attn_Wv, L1_attn_Wo, L1_xattn_W_in, L1_xattn_b_in, L1_xattn_g_res, L1_xattn_g_init, L1_ffn_gate_w, L1_ffn_gate_b, L1_ffn_expert_w, L1_ffn_expert_b):
    import jax
    import jax.numpy as jnp

    def _L0_attn_ref(x, Wq, Wk, Wv, Wo, bo):
        import jax, jax.numpy as jnp
        import numpy as np
        B, N, D_IN, D_OUT, HEADS = (4, 1024, 256, 256, 16)
        D_HEAD = D_OUT // HEADS
        q = jax.nn.softmax(jnp.einsum('bni,io->bno', x, Wq), axis=-1)
        k = jax.nn.softmax(jnp.einsum('bni,io->bno', x, Wk), axis=-2)
        v = jnp.einsum('bni,io->bno', x, Wv)
        scale = 1.0 / np.sqrt(D_HEAD).astype(np.float32)
        ctx = jnp.einsum('bnd,bne->bde', k, v) * scale
        y = jnp.einsum('bnd,bde->bne', q, ctx) / jnp.float32(D_OUT)
        return jnp.einsum('bnd,de->bne', y, Wo) + bo

    def _L0_xattn_ref(src, tgt, src_mask, tgt_mask, W_src, b_src, W_tgt, b_tgt, W_out, b_out):
        import jax, jax.numpy as jnp
        import numpy as np
        B, S, T = (32, 128, 128)
        SRC_SIZE, TGT_SIZE, OUT_SIZE, NUM_HEAD = (512, 256, 256, 8)
        HEAD_DIM = OUT_SIZE // NUM_HEAD
        b, s, _ = src.shape
        t = tgt.shape[1]
        src_trans = jnp.einsum('bsf,of->bso', src, W_src) + b_src
        tgt_trans = jnp.einsum('btf,of->bto', tgt, W_tgt) + b_tgt
        src_trans = src_trans * src_mask[:, :, None]
        tgt_trans = tgt_trans * tgt_mask[:, :, None]
        src_key, src_val = jnp.split(src_trans, 2, axis=2)
        k = src_key.reshape(b, s, NUM_HEAD, HEAD_DIM)
        v = src_val.reshape(b, s, NUM_HEAD, HEAD_DIM)
        q = tgt_trans.reshape(b, t, NUM_HEAD, HEAD_DIM)
        scores = jnp.einsum('bthd,bshd->bhts', q, k) / np.sqrt(HEAD_DIM)
        scores = jnp.where(src_mask[:, None, None, :] == 0, -jnp.inf, scores)
        attn = jax.nn.softmax(scores, axis=-1)
        tgt_update = jnp.einsum('bhts,bshd->bthd', attn, v).reshape(b, t, OUT_SIZE)
        cat_tgt = jnp.concatenate([tgt, tgt_update], axis=2)
        return jnp.einsum('btf,of->bto', cat_tgt, W_out) + b_out

    def _L0_ffn_ref(x, w_router, b_router, w1, b1, w2, b2):
        import jax, jax.numpy as jnp
        import numpy as np
        B, T, D, F_FF, E, TOP_K = (8, 512, 256, 1024, 8, 2)
        CAP_FACTOR = 1.25
        b, t, d = x.shape
        n = b * t
        e = w_router.shape[1]
        xf = x.reshape(n, d)
        logits = xf.astype(jnp.float32) @ w_router + b_router
        gates = jax.nn.softmax(logits, axis=-1)
        topv, topi = jax.lax.top_k(gates, TOP_K)
        cap = max(1, int(CAP_FACTOR * n / e))
        e_flat = topi.reshape(-1)
        g_flat = topv.reshape(-1)
        tok = jnp.repeat(jnp.arange(n), TOP_K)
        onehot = jax.nn.one_hot(e_flat, e, dtype=jnp.int32)
        pos = jnp.cumsum(onehot, axis=0)[jnp.arange(n * TOP_K), e_flat] - 1
        keep = pos < cap
        posc = jnp.minimum(pos, cap - 1)
        buf = jnp.zeros((e, cap, d), x.dtype).at[e_flat, posc].add(jnp.where(keep[:, None], xf[tok], 0.0))
        h = jax.nn.gelu(jnp.einsum('ecd,edf->ecf', buf, w1) + b1[:, None, :], approximate=False)
        out = jnp.einsum('ecf,efd->ecd', h, w2) + b2[:, None, :]
        og = out[e_flat, posc]
        w = jnp.where(keep, g_flat, 0.0).astype(x.dtype)
        y = jnp.zeros((n, d), x.dtype).at[tok].add(w[:, None] * og)
        ws = jnp.zeros((n,), x.dtype).at[tok].add(w)
        y = jnp.where((ws > 0.0)[:, None], y / jnp.maximum(ws, 1e-06)[:, None], y)
        return y.reshape(b, t, d)

    def _L1_attn_ref(x, Wq, Wk, Wv, Wo):
        import math
        import jax, jax.numpy as jnp
        import numpy as np
        D_MODEL = 256
        N_HEADS = 16
        BLOCK = 512
        EPS2 = 0.0487
        ROPE_BASE = 10000.0

        def _riemann_zeros(K):
            n = np.arange(1, K + 1, dtype=np.float64)
            t = 10.0 + 6.0 * n
            for _ in range(60):
                f = t / (2 * np.pi) * np.log(t / (2 * np.pi * np.e)) - (n - 0.875)
                fp = np.log(t / (2 * np.pi)) / (2 * np.pi)
                t = t - f / fp
            return t

        def _constants(N, K):
            g = _riemann_zeros(K)
            g = g / g[0]
            denom = 0.25 + g * g
            w_re = (0.5 / denom).astype(np.float32)
            w_im = (-g / denom).astype(np.float32)
            pos = np.arange(N, dtype=np.float32)
            k_idx = np.arange(K, dtype=np.float32)
            inv_freq = ROPE_BASE ** (-k_idx / K)
            phase = pos[:, None] * inv_freq[None, :]
            cos_p = np.cos(phase).astype(np.float32)
            sin_p = np.sin(phase).astype(np.float32)
            log1p = np.log1p(pos)
            log_decay = (0.5 * (log1p[None, :] - log1p[:, None])).astype(np.float32)
            tril = np.tril(np.ones((N, N), dtype=bool))
            return (jnp.asarray(w_re), jnp.asarray(w_im), jnp.asarray(cos_p), jnp.asarray(sin_p), jnp.asarray(log_decay), jnp.asarray(tril))
        B, N, D = x.shape
        H = N_HEADS
        dh = D // H
        K = dh // 2
        w_re, w_im, cos_p, sin_p, log_decay, tril = _constants(N, K)
        q = (x @ Wq).reshape(B, N, H, dh)
        k = (x @ Wk).reshape(B, N, H, dh)
        v = (x @ Wv).reshape(B, N, H, dh)
        q_re, q_im = (q[..., 0::2], q[..., 1::2])
        k_re, k_im = (k[..., 0::2], k[..., 1::2])
        cos_b = cos_p[None, :, None, :]
        sin_b = sin_p[None, :, None, :]
        qt_re = cos_b * q_re + sin_b * q_im
        qt_im = cos_b * q_im - sin_b * q_re
        kt_re = cos_b * k_re + sin_b * k_im
        kt_im = cos_b * k_im - sin_b * k_re
        wr = w_re[None, None, None, :]
        wi = w_im[None, None, None, :]
        qh_re = wr * qt_re - wi * qt_im
        qh_im = wr * qt_im + wi * qt_re
        scores = (jnp.einsum('bihk,bjhk->bhij', qh_re, kt_re) + jnp.einsum('bihk,bjhk->bhij', qh_im, kt_im)) / math.sqrt(dh)
        scores = scores * jnp.exp(log_decay)[None, None, :, :]
        scores = jnp.where(tril[None, None, :, :], scores, -jnp.inf)
        attn = jax.nn.softmax(scores, axis=-1)
        kk = max(1, math.ceil(EPS2 * N))
        if kk < N:
            vals, _ = jax.lax.top_k(attn, kk)
            thresh = vals[..., -1:]
            mask = (attn >= thresh).astype(attn.dtype)
            masked = attn * mask
            attn = masked / jnp.maximum(masked.sum(-1, keepdims=True), 1e-09)
        out = jnp.einsum('bhij,bjhd->bihd', attn, v).reshape(B, N, D)
        return out @ Wo

    def _L1_xattn_ref(embeds, patch_embeds, patch_lens, W_in, b_in, g_res, g_init):
        import jax, jax.numpy as jnp
        import numpy as np
        B, L, P = (4, 1024, 256)
        D_MODEL = 256
        D_GLOBAL = 512
        HEADDIM = 32
        EPSILON = 0.001
        RMS_EPS = 1e-05

        def rmsnorm(x, g, eps=RMS_EPS):
            var = jnp.mean(jnp.square(x), axis=-1, keepdims=True)
            return x * jax.lax.rsqrt(var + eps) * g

        def _hnet_depool(h, h_patch_full, patch_lens):
            h_patch = h_patch_full[..., :D_MODEL]
            bsz, plen = (h_patch.shape[0], h_patch.shape[1])
            seqlen = h.shape[1]
            logp = jnp.full((bsz, plen), -EPSILON, dtype=jnp.float32)
            bidx = jnp.cumsum(patch_lens, axis=1) - 1
            boundary_mask = jnp.zeros((bsz, seqlen), dtype=jnp.int32)
            boundary_mask = boundary_mask.at[jnp.arange(bsz)[:, None], bidx].set(1)
            dt = (-jnp.log(-jnp.expm1(logp))).astype(h_patch.dtype)
            x = h_patch / dt[..., None]
            n_heads = D_MODEL // HEADDIM
            A = -jnp.ones((n_heads,), dtype=jnp.float32)
            bcoef = jnp.exp(logp).astype(h_patch.dtype)
            x4 = x.reshape(bsz, plen, n_heads, HEADDIM)
            a = jnp.exp(dt[:, :, None] * A[None, None, :])
            u = (dt * bcoef)[:, :, None, None] * x4
            a_b = jnp.broadcast_to(a[..., None], u.shape)

            def comb(lft, rgt):
                aL, uL = lft
                aR, uR = rgt
                return (aL * aR, uL * aR + uR)
            _, s = jax.lax.associative_scan(comb, (a_b, u), axis=1)
            depool = s.reshape(bsz, plen, D_MODEL)
            plug = jnp.clip(jnp.cumsum(boundary_mask, axis=1) - 1, 0, plen - 1)
            depool_out = depool[jnp.arange(bsz)[:, None], plug]
            return depool_out + h
        h = rmsnorm(embeds, g_res)
        h = jnp.einsum('bld,ed->ble', h, W_in) + b_in
        h_patch = rmsnorm(patch_embeds, g_init)
        return _hnet_depool(h, h_patch, patch_lens)

    def _L1_ffn_ref(x, gate_w, gate_b, expert_w, expert_b):
        import jax, jax.numpy as jnp
        import numpy as np
        NEG_INF = -1e+30
        K = 2
        pooled = x.mean(axis=1)
        logits = pooled @ gate_w.T + gate_b
        topk_vals, _ = jax.lax.top_k(logits, K)
        min_topk = topk_vals[:, -1:]
        masked = jnp.where(logits < min_topk, -jnp.inf, logits)
        gates = jax.nn.softmax(masked, axis=-1)
        expert_out = jax.nn.gelu(jnp.einsum('bsd,eod->beso', x, expert_w) + expert_b[None, :, None, :], approximate=False)
        return jnp.einsum('be,beso->bso', gates, expert_out)
    x = x + _L0_attn_ref(_layernorm(x, axis=-1), L0_attn_Wq, L0_attn_Wk, L0_attn_Wv, L0_attn_Wo, L0_attn_bo)
    x = x + _L0_xattn_ref(ctx_2048, _layernorm(x, axis=-1), mask_BxS2_fk1, mask_BxS2_fk1, L0_xattn_W_src, L0_xattn_b_src, L0_xattn_W_tgt, L0_xattn_b_tgt, L0_xattn_W_out, L0_xattn_b_out)
    x = x + _L0_ffn_ref(_layernorm(x, axis=-1), L0_ffn_w_router, L0_ffn_b_router, L0_ffn_w1, L0_ffn_b1, L0_ffn_w2, L0_ffn_b2)
    x = x + _L1_attn_ref(_layernorm(x, axis=-1), L1_attn_Wq, L1_attn_Wk, L1_attn_Wv, L1_attn_Wo)
    x = x + _L1_xattn_ref(_layernorm(x, axis=-1), ctx_2048, mask_BxS2_if0, L1_xattn_W_in, L1_xattn_b_in, L1_xattn_g_res, L1_xattn_g_init)
    x = x + _L1_ffn_ref(_layernorm(x, axis=-1), L1_ffn_gate_w, L1_ffn_gate_b, L1_ffn_expert_w, L1_ffn_expert_b)
    return x

_drawn_inputs = setup_inputs


def setup_inputs(seed=0):
    import zlib

    import numpy as np

    out = dict(_drawn_inputs(seed))
    spreads = {'L0_attn_bo': (0.0, 0.1),
     'L0_xattn_b_src': (0.0, 0.1),
     'L0_xattn_b_tgt': (0.0, 0.593),
     'L0_xattn_b_out': (0.0, 0.1),
     'L0_ffn_b_router': (0.0, 0.1),
     'L0_ffn_b1': (0.0, 0.507),
     'L0_ffn_b2': (0.0, 0.1),
     'L1_xattn_b_in': (0.0, 0.1),
     'L1_xattn_g_res': (1.0, 0.2),
     'L1_xattn_g_init': (1.0, 0.2),
     'L1_ffn_gate_b': (0.0, 0.1),
     'L1_ffn_expert_b': (0.0, 0.281)}
    factors = {'L0_attn_Wq': 8.0,
     'L0_attn_Wk': 8.0,
     'L0_attn_Wv': 8.0,
     'L0_attn_Wo': 8.0,
     'L1_attn_Wq': 13.597,
     'L1_attn_Wk': 13.132}
    for name, (base, spread) in spreads.items():
        noise = np.random.default_rng([zlib.crc32(name.encode()), seed]).standard_normal(out[name].shape)
        drawn = base * np.exp(spread * noise) if base else spread * noise
        out[name] = jnp.asarray(drawn.astype(out[name].dtype))
    for name, factor in factors.items():
        out[name] = (out[name] * factor).astype(out[name].dtype)
    return out
```

```python
from contextlib import ExitStack

import concourse.bass as bass
from concourse import mybir

F32 = mybir.dt.float32
BF16 = mybir.dt.bfloat16
I32 = mybir.dt.int32
U32 = mybir.dt.uint32
ALU = mybir.AluOpType
ACT = mybir.ActivationFunctionType
X = mybir.AxisListType.X

P = 128
NB = 8
S = 256
TB = S // P
D = 256
DT = D // P
DC = 512
CT = DC // P
PAIRS = NB // 2
NE = 8
CAP = int(1.25 * NB * S / NE)
F = 1024
FT = F // P
XH, XD = 8, 32
RH, RD = 16, 16
GH = 4
TOPK = 13
NEG = -1.0e30
LN_EPS = 1e-5
SLOTS = [(0, 128), (128, 128), (256, CAP - 256)]


class Signal:

    def __init__(self, sem, per):
        self.sem, self.per = sem, per

    def __call__(self, b, j=None):
        i, h = b
        return self.sem, i * (2 * self.per) + (h * self.per + (self.per if j is None else j))


class HalfSignal:

    def __init__(self, sems, per, first=0):
        self.sems, self.per, self.first = sems, per, first

    def __call__(self, b, j=None):
        i, h = b
        return self.sems[h], i * self.per + (self.first + (self.per if j is None else j))


class OwnSignal:

    def __init__(self, sem, per):
        self.sem, self.per = sem, per

    def __call__(self, b, j=None):
        return self.sem, b[1] * self.per + (self.per if j is None else j)


class OwnHalfSignal:

    def __init__(self, sems, per):
        self.sems, self.per = sems, per

    def __call__(self, b, j=None):
        return self.sems[b[1]], self.per if j is None else j


def finish(eng, own):
    for s in own:
        for sem, count in [(s.sem, 2 * s.per)] if isinstance(s, OwnSignal) else [(x, s.per) for x in s.sems]:
            eng.wait_ge(sem, count)
            eng.sem_clear(sem)


def tile_of(b):
    i, h = b
    return i * (2 * TB) + h * TB


def decoder(nc, a):
    with ExitStack() as ctx:
        def sb(name, shape, dt=F32):
            return ctx.enter_context(nc.sbuf_tensor(name, shape, dt))

        def sem(name):
            return ctx.enter_context(nc.semaphore(name))

        g = {}
        bank = [[ctx.enter_context(nc.psum_tensor(f"bank{h}{k}", [P, 512], F32)) for k in range(4)]
                for h in range(2)]
        g["bank"] = bank
        g["x_all"] = sb("x_all", [P, NB * TB, D])
        g["depool_all"] = sb("depool_all", [P, NB * TB, D])
        g["choice_w"] = sb("choice_w", [P, NB * TB, 2])
        g["choice_row"] = sb("choice_row", [P, NB * TB, 2], U32)
        g["identf"] = sb("identf", [P, P])
        g["identb"] = sb("identb", [P, P], BF16)
        for name, shape in (("qkv_w", [P, DT, 768]), ("attn_out_w", [P, DT, D]), ("win_w", [P, DT, D]),
                            ("gate_w", [P, DT, NE]), ("rope_cos", [P, TB, 512]), ("rope_sin", [P, TB, 512]),
                            ("b_in", [P, D]), ("gate_b", [P, NE]), ("g_res", [P, DT]),
                            ("expert_b", [P, NE, DT]), ("expert_w", [P, DT, NE * D])):
            g[name] = sb("l1_" + name, shape)
        g["s_l1"] = sem("layer1_constants_loaded")
        for name, per, first in (("sent", 64, 32), ("p_in", 32, 0), ("got_in", 64, 0)):
            g[name] = HalfSignal([sem(f"{name}{h}") for h in range(2)], per, first)
        g["slots"] = nc.dram_tensor("slots", (NE * CAP, D), F32, kind="Internal").ap()
        g["expert_rows"] = nc.dram_tensor("expert_rows", (NE * CAP, D), F32, kind="Internal").ap()
        for part in (layer0, experts, layer1):
            used = []
            part(nc, a, g, used)
            if part is not layer1:
                clear(nc, used)


def clear(nc, used):
    nums = sorted(s.num for s in used)
    while nums:
        n = 1
        while n < len(nums) and nums[n] == nums[0] + n:
            n += 1
        nc.sync.sem_clear(range(nums[0], nums[0] + n))
        nums = nums[n:]
    nc.all_engine_barrier()


def norm_stats(dve, x, stats, mv, var, got, b):
    h = b[1]
    for t in range(TB):
        dve.bn_stats(stats[h][:, t, :], x(t)).then_inc(got["stats"].sem, 1)
    for t in range(TB):
        dve.wait_ge(*got["stats"](b, t + 1))
        dve.bn_aggr(mv[h][:, t, :], stats[h][:, t, :]).then_inc(got["mv"].sem, 1)
    dve.wait_ge(*got["mv"](b))
    dve.tensor_scalar(var[h][:, :], mv[h][:, :, 1], LN_EPS, None, ALU.add).then_inc(got["var"].sem, 1)


def norm_apply(dve, x, xn, mv, rstd, got, b):
    h = b[1]
    dve.wait_ge(*got["rstd"](b))
    for t in range(TB):
        dve.tensor_scalar(xn[h][:, t, :], x(t), mv[h][:, t, 0:1], rstd[h][:, t:t + 1],
                          ALU.subtract, ALU.mult).then_inc(got["xn"].sem, 1)


def transpose_rows(pe, out, rows, ident, cols=DT):
    for c in range(cols):
        for t in range(TB):
            last = pe.transpose(out[:, c * S + t * P:c * S + (t + 1) * P], rows[:, t, c * P:(c + 1) * P], ident[:, :])
    return last


def layer0(nc, a, g, used):
    with ExitStack() as ctx:
        def sb(name, shape, dt=F32):
            return ctx.enter_context(nc.sbuf_tensor(name, shape, dt))

        def sb2(name, shape, dt=F32):
            return [sb(f"{name}{h}", shape, dt) for h in range(2)]

        def sem(name):
            used.append(ctx.enter_context(nc.semaphore(name)))
            return used[-1]

        def sig(name, per):
            return Signal(sem(name), per)

        def turns(name, per):
            return HalfSignal([sem(f"{name}{h}") for h in range(2)], per)

        dve_own = []
        idle_r = OwnSignal(sem("pool_idle"), 3)

        def own(name, per):
            dve_own.append(OwnSignal(sem(name), per))
            return dve_own[-1]

        def own_turns(name, per):
            dve_own.append(OwnHalfSignal([sem(f"{name}{h}") for h in range(2)], per))
            return dve_own[-1]

        def norm_signals(name):
            return {"stats": own(name + "_stats", TB), "mv": own(name + "_mv", TB), "var": sig(name + "_var", 1),
                    "rstd": sig(name + "_rstd", 1), "xn": sig(name + "_xn", TB), "xt": sig(name + "_xt_psum", 1),
                    "xts": sig(name + "_xt", 1)}

        bank, x_all = g["bank"], g["x_all"]
        identf, identb = g["identf"], g["identb"]

        qv_w = sb("qv_w", [P, DT, 512])
        k_w = sb("k_w", [P, DT, D])
        lin_out_w = sb("lin_out_w", [P, DT, D])
        src_w = sb("src_w", [P, CT, 512])
        tgt_w = sb("tgt_w", [P, DT, D])
        out_w = sb("out_w", [P, 2 * DT, D])
        router_w = sb("router_w", [P, DT, NE])
        lin_b = sb("lin_b", [P, D])
        val_b = sb("val_b", [P, D])
        out_b = sb("out_b", [P, D])
        key_b = sb("key_b", [P, DT])
        tgt_b = sb("tgt_b", [P, DT])
        router_b = sb("router_b", [P, NE])
        before = sb("before", [P, P])
        beforeb = sb("beforeb", [P, P], BF16)
        onesb = sb("onesb", [P, P], BF16)
        idle = sb("idle_a", [P, 6])
        mhalf = sb("mhalf", [P, TB])
        zeros = sb("zeros", [P, 1280])
        expert_ids = sb("expert_ids", [P, 4, NE])

        stats, mv = sb2("stats", [P, TB, 6]), sb2("mv", [P, TB, 2])
        var, rstd = sb2("var", [P, TB]), sb2("rstd", [P, TB])
        xn, xnT = sb2("xn", [P, TB, D]), sb2("xnT", [P, DT * S])
        kE, qE = sb2("kE", [P, DT, S]), sb2("qE", [P, TB, D])
        kmax, ksum = sb2("kmax", [P, DT]), sb2("ksum", [P, DT])
        qmax, qsum = sb2("qmax", [P, TB]), sb2("qsum", [P, TB])
        krec, qrec = sb2("krec", [P, DT]), sb2("qrec", [P, TB])
        v_lin, kN = sb2("v_lin", [P, TB, D]), sb2("kN", [P, TB, D])
        qT, ctxT, kvo = sb2("qT", [P, DT * S]), sb2("ctxT", [P, DT, D]), sb2("kvo", [P, DT, D])
        src = sb2("src", [P, CT, S])
        mask_row, mask_col = sb2("mask_row", [P, S]), sb2("mask_col", [P, TB])
        mask_bias = sb2("mask_bias", [P, S], BF16)
        xk, xq = sb2("xk", [P, DT, S]), sb2("xq", [P, DT, S])
        vb = sb2("vb", [P, TB, D])
        xv = sb2("xv", [P, TB, D])
        smax = sb2("smax", [P, 4, GH])
        nmax = sb2("nmax", [P, 4, GH])
        probs, probsT = sb2("probs", [P, GH, S]), sb2("probsT", [P, 2, 512])
        den = sb2("den", [P, 4, GH])
        updT = sb2("updT", [P, DT * S])
        logit = sb2("logit", [P, TB, NE])
        top, topi = sb2("top", [P, TB, 8]), sb2("topi", [P, TB, 8], U32)
        topf = sb2("topf", [P, TB, 2])
        tope, tsum = sb2("tope", [P, TB, 8]), sb2("tsum", [P, TB])
        ntop = sb2("ntop", [P, TB])
        oneh = sb2("oneh", [P, TB, 2, NE])
        ohb = sb2("ohb", [P, TB, NE], BF16)
        carry = sb("carry", [P, NE])
        taken = sb2("taken", [P, TB, NE])
        posm, pos = sb2("posm", [P, TB, 2, NE]), sb2("pos", [P, TB, 2])
        keep, over = sb2("keep", [P, TB, 2]), sb2("over", [P, TB, 2])
        rowf, posc = sb2("rowf", [P, TB, 2]), sb2("posc", [P, TB, 2])
        slotf = sb2("slotf", [P, TB, 2])
        slot = sb2("slot", [P, 2 * TB], U32)
        wk, ws = sb2("wk", [P, TB, 2]), sb2("ws", [P, TB])

        s_const, s_x, s_cast = sem("layer0_constants_loaded"), sem("x_loaded"), sem("constants_cast")
        s_zero, s_set = sem("zeros_set"), sem("memsets_done")
        src_in = HalfSignal([sem(f"src_loaded{h}") for h in range(2)], 48)
        N1, N2, N3 = norm_signals("n1"), norm_signals("n2"), norm_signals("n3")
        key_psum, qv_psum = sig("key_psum", 1), sig("qv_psum", TB)
        kmax_r, qmax_r = sig("kmax_r", 2), sig("qmax_r", 2)
        kexp, qexp, vlin_r = sig("kexp", DT), sig("qexp", TB), sig("vlin_r", TB)
        kN_psum, kN_r = sig("kN_psum", 1), sig("kN_r", 1)
        qT_psum, qT_r = sig("qT_psum", 1), sig("qT_r", 1)
        ctx_psum, ctx_r = sig("ctx_psum", 1), sig("ctx_r", 1)
        rec_r, kvo_psum, kvo_r = own("rec_r", 3), sig("kvo_psum", 1), sig("kvo_r", DT)
        lin_psum, xb1 = sig("lin_psum", 1), sig("x_plus_lin_bias", 1)
        x1 = own("x1_ready", TB)
        xk_psum, xk_r, xv_psum = sig("xk_psum", 1), sig("xk_r", DT), sig("xv_psum", 1)
        vb_r, xv_r, mb_r = sig("vb_r", 1), sig("xv_r", TB), sig("mask_bias_r", 1)
        xq_psum, xq_r = sig("xq_psum", 1), sig("xq_r", DT)
        sc_psum, smax_r, nmax_r = turns("scores_psum", 4), own_turns("smax_r", 4), turns("nmax_r", 4)
        pexp, pT_psum, pT_a, pT_v = turns("pexp", 4 * GH), turns("probsT_psum", 4), turns("probsT_act", 4), turns("probsT_dve", 4)
        den_r, pnorm = own_turns("den_r", 4), turns("probs_normed", 4)
        updT_psum, updT_r = sig("updT_psum", 1), sig("updT_r", 1)
        xb2, xo_psum, x2 = sig("x_plus_out_bias", 1), sig("xout_psum", 1), own("x2_ready", TB)
        lg_psum, lg_r, top_r, topi_r = sig("logit_psum", 1), own("logit_r", 1), own("top_r", TB), own("topi_r", TB)
        topf_r, oh_r, ohb_r = own("topf_r", 2), own("oneh_r", 2 * TB), sig("ohb_r", 1)
        cnt_psum, taken_r, carry_r = sig("count_psum", 1), own("taken_r", 1), own("carry_r", 1)
        posm_r, pos_r, route_r = own("posm_r", 2), own("pos_r", 1), own("route_r", 8)
        texp, slot_r, ntop_r = sig("texp", TB), sig("slot_r", 1), sig("ntop_r", 1)
        sent = g["sent"]
        wgt_r = own("weights_r", 5)

        block = ctx.enter_context(nc.Block())

        def load(eng, out, src_ap, s, bc=False):
            eng.dma_start(out, src_ap.partition_broadcast(P) if bc else src_ap).then_inc(s, 16)

        KT = "(c p) n -> p c n"
        const_loads = [
            (qv_w[:, :, 0:D], a["L0_attn_Wq"].rearrange(KT, p=P)), (qv_w[:, :, D:2 * D], a["L0_attn_Wv"].rearrange(KT, p=P)),
            (k_w[:, :, :], a["L0_attn_Wk"].rearrange(KT, p=P)), (lin_out_w[:, :, :], a["L0_attn_Wo"].rearrange(KT, p=P)),
            (src_w[:, :, :], a["L0_xattn_W_srcT"].rearrange(KT, p=P)), (tgt_w[:, :, :], a["L0_xattn_W_tgtT"].rearrange(KT, p=P)),
            (out_w[:, :, :], a["L0_xattn_W_outT"].rearrange(KT, p=P)), (router_w[:, :, :], a["L0_ffn_w_router"].rearrange(KT, p=P)),
            (lin_b[:, :], a["L0_attn_bo"].partition_broadcast(P)), (val_b[:, :], a["L0_xattn_b_src"][D:2 * D].partition_broadcast(P)),
            (out_b[:, :], a["L0_xattn_b_out"].partition_broadcast(P)), (router_b[:, :], a["L0_ffn_b_router"].partition_broadcast(P)),
            (key_b[:, :], a["L0_xattn_b_srcC"][:, 0:DT]), (tgt_b[:, :], a["L0_xattn_b_tgtC"]),
            (before[:, :], a["c_before"]), (identf[:, :], a["c_ident"]),
        ]
        layer1_loads = [
            (g["qkv_w"][:, :, 0:D], a["L1_attn_Wq"].rearrange(KT, p=P)), (g["qkv_w"][:, :, D:2 * D], a["L1_attn_Wk"].rearrange(KT, p=P)),
            (g["qkv_w"][:, :, 2 * D:3 * D], a["L1_attn_Wv"].rearrange(KT, p=P)), (g["attn_out_w"][:, :, :], a["L1_attn_Wo"].rearrange(KT, p=P)),
            (g["win_w"][:, :, :], a["L1_xattn_W_inT"].rearrange(KT, p=P)), (g["gate_w"][:, :, :], a["L1_ffn_gate_wT"].rearrange(KT, p=P)),
            (g["rope_cos"][:, :, :], a["c_cos"].rearrange("(t p) n -> p t n", p=P)),
            (g["rope_sin"][:, :, :], a["c_sin"].rearrange("(t p) n -> p t n", p=P)),
            (g["b_in"][:, :], a["L1_xattn_b_in"].partition_broadcast(P)), (g["gate_b"][:, :], a["L1_ffn_gate_b"].partition_broadcast(P)),
            (g["g_res"][:, :], a["L1_xattn_g_resC"]), (g["expert_b"][:, :, :], a["L1_ffn_expert_bC"]),
            (g["expert_w"][:, :, :], a["L1_ffn_expert_wT"].rearrange(KT, p=P)),
        ]
        g["n_l1"] = 16 * len(layer1_loads)
        n_const = 16 * len(const_loads)
        x_tiles = a["x"].rearrange("(t p) d -> p t d", p=P)
        slots = g["slots"]

        @block.sync
        def _(sp):
            def load_src(n, h):
                sp.dma_start(src[h][:, :, :], a["ctxT"][bass.ds(n * DC, DC), :].rearrange("(c p) s -> p c s", p=P)).then_inc(src_in.sems[h], 16)
                sp.dma_start(mask_row[h][:, :], a["mask"][bass.ds(n * S, S)].partition_broadcast(P)).then_inc(src_in.sems[h], 16)
                sp.dma_start(mask_col[h][:, :], a["maskC"][:, bass.ds(n * TB, TB)]).then_inc(src_in.sems[h], 16)

            sp.dma_start(x_all[:, 0:4, :], x_tiles[:, 0:4, :]).then_inc(s_x, 16)
            for out, src_ap in const_loads[:8]:
                sp.dma_start(out, src_ap).then_inc(s_const, 16)
            for h in range(2):
                load_src(h, h)
            with sp.Fori(0, PAIRS - 1) as i:
                for h in range(2):
                    sp.wait_ge(*xq_r((i, h)))
                    sp.wait_ge(*xv_r((i, h)))
                    sp.wait_ge(*mb_r((i, h)))
                    load_src(i * 2 + (h + 2), h)

        @block.gpsimd
        def _(pool):
            pool.memset(zeros[:, :], 0.0).then_inc(s_zero, 1)
            pool.memset(mhalf[:, :], -0.5).then_inc(s_set, 1)
            pool.memset(onesb[:, :], 1.0).then_inc(s_set, 1)
            pool.memset(carry[:, :], 0.0).then_inc(s_set, 1)
            pool.iota(expert_ids[:, :, :], [[0, 4], [1, NE]], base=0, channel_multiplier=0,
                      allow_small_or_imprecise_dtypes=True).then_inc(s_set, 1)
            pool.wait_ge(s_zero, 1)
            for q in range(4):
                pool.dma_start(slots[q * 5 * P:(q + 1) * 5 * P, :].rearrange("(p r) d -> p (r d)", p=P),
                               zeros[:, :]).then_inc(sent.sems[q % 2], 16)
            pool.wait_ge(s_set, 4)
            pool.wait_ge(s_const, n_const)
            pool.wait_ge(s_x, 64)

            def power(N, b):
                pool.wait_ge(*N["var"](b))
                pool.tensor_tensor(rstd[b[1]][:, :], var[b[1]][:, :], mhalf[:, :], ALU.pow).then_inc(N["rstd"].sem, 1)

            with pool.Fori(0, PAIRS) as i:
                B = [(i, 0), (i, 1)]
                for b in B:
                    power(N1, b)
                for b in B:
                    x = x_all[:, bass.ds(tile_of(b), TB), :]
                    pool.wait_ge(*N1["xn"](b))
                    pool.tensor_tensor(idle[:, 2 * 0 + b[1]:2 * 0 + b[1] + 1], mhalf[:, 0:1], mhalf[:, 0:1], ALU.add).then_inc(idle_r.sem, 1)
                    pool.tensor_tensor(x, x, lin_b[:, :].unsqueeze(1).broadcast_to([P, TB, D]), ALU.add).then_inc(xb1.sem, 1)
                for b in B:
                    power(N2, b)
                for b in B:
                    h = b[1]
                    pool.wait_ge(*vb_r(b))
                    pool.wait_ge(*src_in(b))
                    for t in range(TB):
                        pool.tensor_tensor(xv[h][:, t, :], vb[h][:, t, :], mask_col[h][:, t:t + 1].broadcast_to([P, D]),
                                           ALU.mult).then_inc(xv_r.sem, 1)
                for b in B:
                    x = x_all[:, bass.ds(tile_of(b), TB), :]
                    pool.wait_ge(*N2["xn"](b))
                    pool.tensor_tensor(idle[:, 2 * 1 + b[1]:2 * 1 + b[1] + 1], mhalf[:, 0:1], mhalf[:, 0:1], ALU.add).then_inc(idle_r.sem, 1)
                    pool.tensor_tensor(x, x, out_b[:, :].unsqueeze(1).broadcast_to([P, TB, D]), ALU.add).then_inc(xb2.sem, 1)
                for b in B:
                    power(N3, b)
                for b in B:
                    h = b[1]
                    pool.wait_ge(*slot_r(b))
                    pool.wait_ge(sent.sems[0], sent.first)
                    pool.wait_ge(sent.sems[1], sent.first)
                    pool.tensor_tensor(idle[:, 2 * 2 + b[1]:2 * 2 + b[1] + 1], mhalf[:, 0:1], mhalf[:, 0:1], ALU.add).then_inc(idle_r.sem, 1)
                    for t in range(TB):
                        for k in range(2):
                            pool.indirect_dma_start(
                                out=slots, out_offset=bass.IndirectOffsetOnAxis(ap=slot[h][:, 2 * t + k:2 * t + k + 1], axis=0),
                                in_=xn[h][:, t, :], in_offset=None, bounds_check=NE * CAP - 1, oob_is_err=False,
                            ).then_inc(sent.sems[h], 16)
                finish(pool, [idle_r])
            for h in range(2):
                pool.wait_ge(*sent((PAIRS - 1, h)))

        @block.scalar
        def _(act):
            for q in range(1, 4):
                act.dma_start(x_all[:, 4 * q:4 * q + 4, :], x_tiles[:, 4 * q:4 * q + 4, :]).then_inc(s_x, 16)
            for out, src_ap in const_loads[8:]:
                act.dma_start(out, src_ap).then_inc(s_const, 16)
            act.wait_ge(s_const, n_const)
            act.activation(identb[:, :], identf[:, :], ACT.Copy).then_inc(s_cast, 1)
            act.activation(beforeb[:, :], before[:, :], ACT.Copy).then_inc(s_cast, 1)
            for out, src_ap in layer1_loads:
                act.dma_start(out, src_ap).then_inc(g["s_l1"], 16)

            def evac(out, psum, waits, done):
                for w in waits:
                    act.wait_ge(*w)
                act.activation(out, psum, ACT.Copy).then_inc(done, 1)

            with act.Fori(0, PAIRS) as i:
                B = [(i, 0), (i, 1)]
                for b in B:
                    evac(xnT[b[1]][:, :], bank[b[1]][0][:, :], [N1["xt"](b)], N1["xts"].sem)
                for b in B:
                    h = b[1]
                    act.wait_ge(*kmax_r(b))
                    for c in range(DT):
                        act.activation(kE[h][:, c, :], bank[h][1][:, c * S:(c + 1) * S], ACT.Exp, bias=kmax[h][:, c:c + 1],
                                       accum_out=ksum[h][:, c:c + 1]).then_inc(kexp.sem, 1)
                for b in B:
                    h = b[1]
                    act.wait_ge(*qmax_r(b))
                    for t in range(TB):
                        act.activation(qE[h][:, t, :], bank[h][2 + t][:, 0:D], ACT.Exp, bias=qmax[h][:, t:t + 1],
                                       accum_out=qsum[h][:, t:t + 1]).then_inc(qexp.sem, 1)
                    for t in range(TB):
                        act.activation(v_lin[h][:, t, :], bank[h][2 + t][:, D:2 * D], ACT.Copy).then_inc(vlin_r.sem, 1)
                for b in B:
                    evac(qT[b[1]][:, :], bank[b[1]][0][:, :], [qT_psum(b)], qT_r.sem)
                for b in B:
                    evac(ctxT[b[1]][:, :, :].rearrange("p a c -> p (a c)"), bank[b[1]][2][:, :], [ctx_psum(b)], ctx_r.sem)
                for b in B:
                    evac(xnT[b[1]][:, :], bank[b[1]][2][:, :], [N2["xt"](b)], N2["xts"].sem)

                def exps(b, ch):
                    h = b[1]
                    act.wait_ge(*nmax_r(b, ch + 1))
                    for j in range(GH):
                        act.activation(probs[h][:, j, :], bank[h][j // 2][:, (j % 2) * S:(j % 2 + 1) * S], ACT.Exp,
                                       bias=nmax[h][:, ch, j:j + 1], scale=XD ** -0.5, accum_out=den[h][:, ch, j:j + 1]).then_inc(pexp.sems[h], 1)

                steps = [(b, ch) for ch in range(4) for b in B]
                exps(*steps[0])
                exps(*steps[1])
                for n, (b, ch) in enumerate(steps):
                    evac(probsT[b[1]][:, 0, :], bank[b[1]][0][:, :], [pT_psum(b, ch + 1)], pT_a.sems[b[1]])
                    if ch < 3:
                        exps(*steps[n + 2])
                for b in B:
                    evac(updT[b[1]][:, :], bank[b[1]][2][:, :], [updT_psum(b)], updT_r.sem)
                for b in B:
                    evac(xnT[b[1]][:, :], bank[b[1]][0][:, :], [N3["xt"](b)], N3["xts"].sem)
                for b in B:
                    h = b[1]
                    act.wait_ge(*ntop_r(b))
                    for t in range(TB):
                        act.activation(tope[h][:, t, :], top[h][:, t, :], ACT.Exp, bias=ntop[h][:, t:t + 1],
                                       accum_out=tsum[h][:, t:t + 1]).then_inc(texp.sem, 1)

        @block.tensor
        def _(pe):
            pe.wait_ge(s_const, n_const)
            pe.wait_ge(s_cast, 2)
            pe.wait_ge(s_set, 4)
            with pe.Fori(0, PAIRS) as i:
                B = [(i, 0), (i, 1)]
                for b in B:
                    pe.wait_ge(*N1["xn"](b))
                    transpose_rows(pe, bank[b[1]][0], xn[b[1]], identf).then_inc(N1["xt"].sem, 1)
                for b in B:
                    h = b[1]
                    pe.wait_ge(*N1["xts"](b))
                    for c in range(DT):
                        for k in range(DT):
                            last = pe.matmul(bank[h][1][:, c * S:(c + 1) * S], k_w[:, k, c * P:(c + 1) * P],
                                             xnT[h][:, k * S:(k + 1) * S], start=(k == 0), stop=(k == DT - 1))
                    last.then_inc(key_psum.sem, 1)
                    for t in range(TB):
                        for k in range(DT):
                            last = pe.matmul(bank[h][2 + t][:, :], xnT[h][:, k * S + t * P:k * S + (t + 1) * P],
                                             qv_w[:, k, :], start=(k == 0), stop=(k == DT - 1))
                        last.then_inc(qv_psum.sem, 1)
                for b in B:
                    h = b[1]
                    pe.wait_ge(*kexp(b))
                    for t in range(TB):
                        for c in range(DT):
                            last = pe.transpose(bank[h][1][:, t * D + c * P:t * D + (c + 1) * P],
                                                kE[h][:, c, t * P:(t + 1) * P], identf[:, :])
                    last.then_inc(kN_psum.sem, 1)
                for b in B:
                    pe.wait_ge(*qexp(b))
                    transpose_rows(pe, bank[b[1]][0], qE[b[1]], identf).then_inc(qT_psum.sem, 1)
                for b in B:
                    h = b[1]
                    pe.wait_ge(*kN_r(b))
                    pe.wait_ge(*vlin_r(b))
                    for e in range(DT):
                        for t in range(TB):
                            last = pe.matmul(bank[h][2][:, e * D:(e + 1) * D], v_lin[h][:, t, e * P:(e + 1) * P], kN[h][:, t, :],
                                             start=(t == 0), stop=(t == TB - 1))
                    last.then_inc(ctx_psum.sem, 1)
                for b in B:
                    h = b[1]
                    pe.wait_ge(*ctx_r(b))
                    for d in range(DT):
                        for e in range(DT):
                            last = pe.matmul(bank[h][3][:, d * D:(d + 1) * D], ctxT[h][:, e, d * P:(d + 1) * P], lin_out_w[:, e, :],
                                             start=(e == 0), stop=(e == DT - 1))
                    last.then_inc(kvo_psum.sem, 1)
                for b in B:
                    h = b[1]
                    pe.wait_ge(*kvo_r(b))
                    pe.wait_ge(*qT_r(b))
                    for t in range(TB):
                        for d in range(DT):
                            last = pe.matmul(bank[h][1][:, t * D:(t + 1) * D], qT[h][:, d * S + t * P:d * S + (t + 1) * P],
                                             kvo[h][:, d, :], start=(d == 0), stop=(d == DT - 1))
                    last.then_inc(lin_psum.sem, 1)
                for b in B:
                    h = b[1]
                    pe.wait_ge(*src_in(b))
                    for c in range(DT):
                        for k in range(CT):
                            last = pe.matmul(bank[h][0][:, c * S:(c + 1) * S], src_w[:, k, c * P:(c + 1) * P], src[h][:, k, :],
                                             start=(k == 0), stop=(k == CT - 1))
                    last.then_inc(xk_psum.sem, 1)
                    for t in range(TB):
                        for k in range(CT):
                            last = pe.matmul(bank[h][3][:, t * D:(t + 1) * D], src[h][:, k, t * P:(t + 1) * P], src_w[:, k, D:2 * D],
                                             start=(k == 0), stop=(k == CT - 1))
                    last.then_inc(xv_psum.sem, 1)
                for b in B:
                    pe.wait_ge(*N2["xn"](b))
                    transpose_rows(pe, bank[b[1]][2], xn[b[1]], identf).then_inc(N2["xt"].sem, 1)
                for b in B:
                    h = b[1]
                    pe.wait_ge(*N2["xts"](b))
                    for c in range(DT):
                        for k in range(DT):
                            last = pe.matmul(bank[h][1][:, c * S:(c + 1) * S], tgt_w[:, k, c * P:(c + 1) * P],
                                             xnT[h][:, k * S:(k + 1) * S], start=(k == 0), stop=(k == DT - 1))
                    last.then_inc(xq_psum.sem, 1)

                def head(c, j):
                    return j % 2 * (P // XD) + 2 * c + j // 2

                def scores(b, ch):
                    h, t, c = b[1], ch // 2, ch % 2
                    if ch == 0:
                        pe.wait_ge(*mb_r(b))
                        pe.wait_ge(*xk_r(b))
                        pe.wait_ge(*xq_r(b))
                    else:
                        pe.wait_ge(*pT_a(b, ch))
                        pe.wait_ge(*pT_v(b, ch))
                    for j in range(GH):
                        f, r = divmod(head(c, j), P // XD)
                        r0 = XD * r
                        o = bank[h][j // 2][:, (j % 2) * S:(j % 2 + 1) * S]
                        pe.matmul(o, onesb[r0:r0 + 1, :], mask_bias[h][r0:r0 + 1, :], start=True, stop=False)
                        last = pe.matmul(o, xq[h][r0:r0 + XD, f, t * P:(t + 1) * P], xk[h][r0:r0 + XD, f, :],
                                         start=False, stop=True)
                    last.then_inc(sc_psum.sems[h], 1)

                def turn(b, ch):
                    h = b[1]
                    pe.wait_ge(*pnorm(b, ch + 1))
                    for j in range(GH):
                        for s in range(TB):
                            last = pe.transpose(bank[h][j // 2][:, ((j % 2) * TB + s) * P:((j % 2) * TB + s + 1) * P],
                                                probs[h][:, j, s * P:(s + 1) * P], identf[:, :])
                    last.then_inc(pT_psum.sems[h], 1)

                def values(b, ch):
                    h, t, c = b[1], ch // 2, ch % 2
                    pe.wait_ge(*pT_a(b, ch + 1))
                    pe.wait_ge(*pT_v(b, ch + 1))
                    if ch == 0:
                        pe.wait_ge(*xv_r(b))
                    for j, s in [(j, s) for first in (0, 1) for s in range(TB) for j in (first, first + 2)]:
                        hd = head(c, j)
                        f, r = divmod(hd, P // XD)
                        last = pe.matmul(bank[h][2][XD * r:XD * (r + 1), f * S + t * P:f * S + (t + 1) * P],
                                         xv[h][:, s, hd * XD:(hd + 1) * XD],
                                         probsT[h][:, j // 2, ((j % 2) * TB + s) * P:((j % 2) * TB + s + 1) * P],
                                         start=(s == 0), stop=(s == TB - 1))
                    if ch == 3:
                        last.then_inc(updT_psum.sem, 1)

                steps = [(b, ch) for ch in range(4) for b in B]
                scores(*steps[0])
                scores(*steps[1])
                for n, (b, ch) in enumerate(steps):
                    turn(b, ch)
                    if n:
                        values(*steps[n - 1])
                    if ch < 3:
                        scores(b, ch + 1)
                values(*steps[-1])
                for b in B:
                    h = b[1]
                    pe.wait_ge(*updT_r(b))
                    for t in range(TB):
                        for k in range(2 * DT):
                            left = (xnT if k < DT else updT)[h]
                            last = pe.matmul(bank[h][1][:, t * D:(t + 1) * D], left[:, (k % DT) * S + t * P:(k % DT) * S + (t + 1) * P],
                                             out_w[:, k, :], start=(k == 0), stop=(k == 2 * DT - 1))
                    last.then_inc(xo_psum.sem, 1)
                for b in B:
                    pe.wait_ge(*N3["xn"](b))
                    transpose_rows(pe, bank[b[1]][0], xn[b[1]], identf).then_inc(N3["xt"].sem, 1)
                for b in B:
                    h = b[1]
                    pe.wait_ge(*N3["xts"](b))
                    for t in range(TB):
                        for k in range(DT):
                            last = pe.matmul(bank[h][2][:, t * NE:(t + 1) * NE], xnT[h][:, k * S + t * P:k * S + (t + 1) * P],
                                             router_w[:, k, :], start=(k == 0), stop=(k == DT - 1))
                    last.then_inc(lg_psum.sem, 1)
                for b in B:
                    h = b[1]
                    o = bank[h][3]
                    pe.wait_ge(*ohb_r(b))
                    pe.matmul(o[:, 0:NE], beforeb[:, :], ohb[h][:, 0, :], start=True, stop=True)
                    pe.matmul(o[:, NE:2 * NE], onesb[:, :], ohb[h][:, 0, :], start=True, stop=False)
                    pe.matmul(o[:, NE:2 * NE], beforeb[:, :], ohb[h][:, 1, :], start=False, stop=True)
                    pe.matmul(o[:, 2 * NE:3 * NE], onesb[:, :], ohb[h][:, 0, :], start=True, stop=False)
                    pe.matmul(o[:, 2 * NE:3 * NE], onesb[:, :], ohb[h][:, 1, :], start=False, stop=True).then_inc(cnt_psum.sem, 1)

        @block.vector
        def _(dve):
            dve.wait_ge(s_x, 64)
            dve.wait_ge(s_const, n_const)
            dve.wait_ge(s_set, 4)
            with dve.Fori(0, PAIRS) as i:
                B = [(i, 0), (i, 1)]

                def xt(b):
                    return lambda t: x_all[:, bass.ds(tile_of(b) + t, 1), :].rearrange("p a d -> p (a d)")

                for b in B:
                    norm_stats(dve, xt(b), stats, mv, var, N1, b)
                for b in B:
                    dve.wait_ge(*sent(b, 0))
                    norm_apply(dve, xt(b), xn, mv, rstd, N1, b)
                for b in B:
                    h = b[1]
                    dve.wait_ge(*key_psum(b))
                    dve.tensor_reduce(kmax[h][:, :], bank[h][1][:, :].rearrange("p (c s) -> p c s", c=DT), X, ALU.max, negate=True).then_inc(kmax_r.sem, 2)
                for b in B:
                    h = b[1]
                    for t in range(TB):
                        dve.wait_ge(*qv_psum(b, t + 1))
                        dve.tensor_reduce(qmax[h][:, t:t + 1], bank[h][2 + t][:, 0:D], X, ALU.max, negate=True).then_inc(qmax_r.sem, 1)
                for b in B:
                    h = b[1]
                    dve.wait_ge(*kN_psum(b))
                    dve.tensor_copy(kN[h][:, :, :].rearrange("p t d -> p (t d)"), bank[h][1][:, :]).then_inc(kN_r.sem, 1)
                    dve.wait_ge(*qexp(b))
                    dve.reciprocal(krec[h][:, :], ksum[h][:, :]).then_inc(rec_r.sem, 1)
                    dve.reciprocal(qrec[h][:, :], qsum[h][:, :]).then_inc(rec_r.sem, 1)
                    dve.wait_ge(*rec_r(b, 2))
                    dve.tensor_scalar(qrec[h][:, :], qrec[h][:, :], 0.25 / D, None, ALU.mult).then_inc(rec_r.sem, 1)
                for b in B:
                    h = b[1]
                    dve.wait_ge(*kvo_psum(b))
                    for d in range(DT):
                        dve.tensor_scalar(kvo[h][:, d, :], bank[h][3][:, d * D:(d + 1) * D], krec[h][:, d:d + 1], None,
                                          ALU.mult).then_inc(kvo_r.sem, 1)
                for b in B:
                    h = b[1]
                    dve.wait_ge(*src_in(b))
                    dve.tensor_scalar(mask_bias[h][:, :], mask_row[h][:, :], 0.0, NEG, ALU.is_equal, ALU.mult).then_inc(mb_r.sem, 1)
                for b in B:
                    h = b[1]
                    dve.wait_ge(*lin_psum(b))
                    dve.wait_ge(*xb1(b))
                    dve.wait_ge(*rec_r(b))
                    for t in range(TB):
                        dve.scalar_tensor_tensor(xt(b)(t), bank[h][1][:, t * D:(t + 1) * D], qrec[h][:, t:t + 1], xt(b)(t),
                                                 ALU.mult, ALU.add).then_inc(x1.sem, 1)
                for b in B:
                    dve.wait_ge(*x1(b))
                    norm_stats(dve, xt(b), stats, mv, var, N2, b)
                for b in B:
                    norm_apply(dve, xt(b), xn, mv, rstd, N2, b)
                for b in B:
                    h = b[1]
                    dve.wait_ge(*xk_psum(b))
                    for c in range(DT):
                        dve.scalar_tensor_tensor(xk[h][:, c, :], bank[h][0][:, c * S:(c + 1) * S], key_b[:, c:c + 1], mask_row[h][:, :],
                                                 ALU.add, ALU.mult).then_inc(xk_r.sem, 1)
                    dve.wait_ge(*xv_psum(b))
                    dve.tensor_tensor(vb[h][:, :, :], bank[h][3][:, :].rearrange("p (t d) -> p t d", t=TB),
                                      val_b[:, :].unsqueeze(1).broadcast_to([P, TB, D]), ALU.add).then_inc(vb_r.sem, 1)
                for b in B:
                    h = b[1]
                    dve.wait_ge(*xq_psum(b))
                    for c in range(DT):
                        dve.scalar_tensor_tensor(xq[h][:, c, :], bank[h][1][:, c * S:(c + 1) * S], tgt_b[:, c:c + 1], mask_row[h][:, :],
                                                 ALU.add, ALU.mult).then_inc(xq_r.sem, 1)

                def maxima(b, ch):
                    h = b[1]
                    dve.wait_ge(*sc_psum(b, ch + 1))
                    for q in range(2):
                        last = dve.tensor_reduce(smax[h][:, ch, 2 * q:2 * q + 2], bank[h][q][:, :].rearrange("p (c s) -> p c s", c=2), X, ALU.max)
                    last.then_inc(smax_r.sems[h], 1)
                    dve.wait_ge(*smax_r(b, ch + 1))
                    dve.tensor_scalar(nmax[h][:, ch, :], smax[h][:, ch, :], -XD ** -0.5, None, ALU.mult).then_inc(nmax_r.sems[h], 1)

                def normed(b, ch):
                    h = b[1]
                    dve.wait_ge(*pexp(b, GH * (ch + 1)))
                    dve.reciprocal(den[h][:, ch, :], den[h][:, ch, :]).then_inc(den_r.sems[h], 1)
                    dve.wait_ge(*den_r(b, ch + 1))
                    for j in range(GH):
                        last = dve.tensor_scalar(probs[h][:, j, :], probs[h][:, j, :], den[h][:, ch, j:j + 1], None, ALU.mult)
                    last.then_inc(pnorm.sems[h], 1)

                steps = [(b, ch) for ch in range(4) for b in B]
                maxima(*steps[0])
                maxima(*steps[1])
                normed(*steps[0])
                for n, (b, ch) in enumerate(steps):
                    h = b[1]
                    dve.wait_ge(*pT_psum(b, ch + 1))
                    dve.tensor_copy(probsT[h][:, 1, :], bank[h][1][:, :]).then_inc(pT_v.sems[h], 1)
                    if n + 1 < len(steps):
                        normed(*steps[n + 1])
                    if ch < 3:
                        maxima(*steps[n + 2])
                for b in B:
                    h = b[1]
                    dve.wait_ge(*xo_psum(b))
                    dve.wait_ge(*xb2(b))
                    x = x_all[:, bass.ds(tile_of(b), TB), :]
                    dve.tensor_tensor(x, bank[h][1][:, :].rearrange("p (t d) -> p t d", t=TB), x, ALU.add).then_inc(x2.sem, TB)
                for b in B:
                    dve.wait_ge(*x2(b))
                    norm_stats(dve, xt(b), stats, mv, var, N3, b)
                for b in B:
                    h = b[1]
                    norm_apply(dve, xt(b), xn, mv, rstd, N3, b)
                for b in B:
                    h = b[1]
                    dve.wait_ge(*lg_psum(b))
                    dve.tensor_tensor(logit[h][:, :, :], bank[h][2][:, 0:TB * NE].rearrange("p (t e) -> p t e", t=TB),
                                      router_b[:, :].unsqueeze(1).broadcast_to([P, TB, NE]), ALU.add).then_inc(lg_r.sem, 1)
                    dve.wait_ge(*lg_r(b))
                    for t in range(TB):
                        dve.max(top[h][:, t, :], logit[h][:, t, :]).then_inc(top_r.sem, 1)
                    dve.wait_ge(*top_r(b))
                    for t in range(TB):
                        dve.max_index(topi[h][:, t, :], top[h][:, t, :], logit[h][:, t, :]).then_inc(topi_r.sem, 1)
                    dve.tensor_scalar(ntop[h][:, :], top[h][:, :, 0], -1.0, None, ALU.mult).then_inc(ntop_r.sem, 1)
                    dve.wait_ge(*topi_r(b))
                    dve.tensor_copy(topf[h][:, :, :], topi[h][:, :, 0:2]).then_inc(topf_r.sem, 2)
                    dve.wait_ge(*topf_r(b))
                    for t in range(TB):
                        for k in range(2):
                            dve.tensor_scalar(oneh[h][:, t, k, :], expert_ids[:, 0, :], topf[h][:, t, k:k + 1], None,
                                              ALU.is_equal).then_inc(oh_r.sem, 1)
                    dve.wait_ge(*oh_r(b))
                    dve.tensor_tensor(ohb[h][:, :, :], oneh[h][:, :, 0, :], oneh[h][:, :, 1, :], ALU.add).then_inc(ohb_r.sem, 1)
                for b in B:
                    h = b[1]
                    dve.wait_ge(*cnt_psum(b))
                    dve.tensor_tensor(taken[h][:, :, :], bank[h][3][:, 0:TB * NE].rearrange("p (t e) -> p t e", t=TB),
                                      carry[:, :].unsqueeze(1).broadcast_to([P, TB, NE]), ALU.add).then_inc(taken_r.sem, 1)
                    dve.wait_ge(*taken_r(b))
                    dve.tensor_tensor(carry[:, :], carry[:, :], bank[h][3][:, 2 * NE:3 * NE], ALU.add).then_inc(carry_r.sem, 1)
                    for t in range(TB):
                        dve.tensor_tensor(posm[h][:, t, :, :], oneh[h][:, t, :, :], taken[h][:, t, :].unsqueeze(1).broadcast_to([P, 2, NE]),
                                          ALU.mult).then_inc(posm_r.sem, 1)
                    dve.wait_ge(*posm_r(b))
                    dve.tensor_reduce(pos[h][:, :, :], posm[h][:, :, :, :], X, ALU.add).then_inc(pos_r.sem, 1)
                    dve.wait_ge(*pos_r(b))
                    dve.wait_ge(*carry_r(b))
                    dve.tensor_scalar(keep[h][:, :, :], pos[h][:, :, :], float(CAP), None, ALU.is_lt).then_inc(route_r.sem, 1)
                    dve.tensor_scalar(over[h][:, :, :], pos[h][:, :, :], float(CAP), 4.0 * NE * CAP, ALU.is_ge, ALU.mult).then_inc(route_r.sem, 1)
                    dve.tensor_scalar(posc[h][:, :, :], pos[h][:, :, :], float(CAP - 1), None, ALU.min).then_inc(route_r.sem, 1)
                    dve.wait_ge(*route_r(b, 3))
                    dve.scalar_tensor_tensor(rowf[h][:, :, :], topf[h][:, :, :], float(CAP), posc[h][:, :, :], ALU.mult, ALU.add).then_inc(route_r.sem, 1)
                    dve.wait_ge(*route_r(b, 4))
                    dve.tensor_tensor(slotf[h][:, :, :], rowf[h][:, :, :], over[h][:, :, :], ALU.add).then_inc(route_r.sem, 1)
                    dve.wait_ge(*route_r(b, 5))
                    dve.tensor_copy(slot[h][:, :], slotf[h][:, :, :].rearrange("p t k -> p (t k)")).then_inc(slot_r.sem, 1)
                    dve.tensor_copy(g["choice_row"][:, bass.ds(tile_of(b), TB), :], rowf[h][:, :, :]).then_inc(route_r.sem, 1)
                    dve.wait_ge(*texp(b))
                    dve.reciprocal(ws[h][:, :], tsum[h][:, :]).then_inc(wgt_r.sem, 1)
                    dve.tensor_tensor(wk[h][:, :, :], tope[h][:, :, 0:2], keep[h][:, :, :], ALU.mult).then_inc(wgt_r.sem, 1)
                    dve.wait_ge(*wgt_r(b, 2))
                    dve.tensor_tensor(wk[h][:, :, :], wk[h][:, :, :], ws[h][:, :].unsqueeze(2).broadcast_to([P, TB, 2]), ALU.mult).then_inc(wgt_r.sem, 1)
                    dve.wait_ge(*wgt_r(b, 3))
                    dve.tensor_reduce(ws[h][:, :], wk[h][:, :, :], X, ALU.add).then_inc(wgt_r.sem, 1)
                    dve.wait_ge(*wgt_r(b, 4))
                    dve.tensor_scalar(ws[h][:, :], ws[h][:, :], 1e-6, None, ALU.max).then_inc(wgt_r.sem, 1)
                    dve.wait_ge(*wgt_r(b, 5))
                    dve.reciprocal(ws[h][:, :], ws[h][:, :]).then_inc(route_r.sem, 1)
                    dve.wait_ge(*route_r(b, 7))
                    dve.tensor_tensor(g["choice_w"][:, bass.ds(tile_of(b), TB), :], wk[h][:, :, :],
                                      ws[h][:, :].unsqueeze(2).broadcast_to([P, TB, 2]), ALU.mult).then_inc(route_r.sem, 1)
                finish(dve, dve_own)


def experts(nc, a, g, used):
    with ExitStack() as ctx:
        def sb(name, shape, dt=F32):
            return ctx.enter_context(nc.sbuf_tensor(name, shape, dt))

        def sb2(name, shape, dt=F32):
            return [sb(f"{name}{h}", shape, dt) for h in range(2)]

        def sem(name):
            used.append(ctx.enter_context(nc.semaphore(name)))
            return used[-1]

        def sig(name, per):
            return Signal(sem(name), per)

        def turns(name, per):
            return HalfSignal([sem(f"{name}{h}") for h in range(2)], per)

        bank, identf = g["bank"], g["identf"]
        w1, w2 = sb2("w1", [P, DT, F]), sb2("w2", [P, FT, D])
        b1, b2 = sb2("b1", [P, FT]), sb2("b2", [P, D])
        rows, rowsT = sb2("rows", [P, len(SLOTS), D]), sb2("rowsT", [P, DT, CAP])
        hid, outr = sb2("hid", [P, FT, CAP]), sb2("outr", [P, len(SLOTS), D])
        decayT, upto = sb("decayT", [P, TB, S]), sb("upto", [P, TB, S])
        uptob, ones = sb("uptob", [P, TB, S], BF16), sb("ones", [P, P])
        place, zero = sb("place", [P, TB]), sb("zero", [P, S])
        g_init, mhalf = sb("g_init", [P, D]), sb("mhalf_m", [P, TB])
        lens = sb2("lens", [P, S], I32)
        patch, square = sb2("patch", [P, TB, DC]), sb2("square", [P, TB, DC])
        lensf, ends, wrap = sb2("lensf", [P, S]), sb2("ends", [P, S]), sb2("wrap", [P, S])
        hit, hits = sb2("hit", [P, TB, S]), sb2("hits", [P, TB])
        edge = sb2("edge", [P, TB, P], BF16)
        plug, pick = sb2("plug", [P, S]), sb2("pick", [P, TB, S])
        ssum, msq, rrms = sb2("ssum", [P, TB]), sb2("msq", [P, TB]), sb2("rrms", [P, TB])
        u, state = sb2("u", [P, TB, D]), sb2("state", [P, TB, D])

        s_const, s_set, s_cast = sem("experts_constants_loaded"), sem("m_memsets_done"), sem("m_cast")
        w_in = HalfSignal([sem(f"expert_loaded{h}") for h in range(2)], 96)
        p_in = g["p_in"]
        out_sent = HalfSignal([sem(f"expert_rows_stored{h}") for h in range(2)], 32, 1)
        rt_psum, rt_r = sig("rowsT_psum", 1), sig("rowsT_r", DT)
        h_psum, h_r = turns("hidden_psum", FT), turns("hidden_r", FT)
        o_psum, o_r = sig("expert_out_psum", 3), sig("expert_out_r", 3)
        sq_r, ms_r, rr_r, u_r = sig("square_r", TB), sig("msq_r", 1), sig("rrms_r", 1), sig("u_r", TB)
        ends_r, hit_r, edge_r = sig("ends_r", 4), sig("hit_r", TB), sig("edge_r", TB + 1)
        cs_psum, plug_r, pick_r = sig("edge_count_psum", 1), sig("plug_r", 1), sig("pick_r", TB)
        st_psum, st_r, dp_psum, dp_r = sig("state_psum", 1), sig("state_r", 1), sig("depool_psum", 1), sig("depool_r", 1)
        n_const = 16 * 3
        block = ctx.enter_context(nc.Block())
        slots, expert_rows = g["slots"], g["expert_rows"]

        @block.sync
        def _(sp):
            def load(n, h):
                got = w_in.sems[h]
                sp.dma_start(rows[h][:, 0:2, :], slots[bass.ds(n * CAP, 2 * P), :].rearrange("(t p) d -> p t d", p=P)).then_inc(got, 16)
                sp.dma_start(rows[h][0:CAP - 2 * P, 2, :], slots[bass.ds(n * CAP + 2 * P, CAP - 2 * P), :]).then_inc(got, 16)
                sp.dma_start(w1[h][:, :, :], a["L0_ffn_w1"][bass.ds(n * D, D), :].rearrange("(c p) f -> p c f", p=P)).then_inc(got, 16)
                sp.dma_start(b1[h][:, :], a["L0_ffn_b1C"][bass.ds(n * P, P), :]).then_inc(got, 16)
                sp.dma_start(b2[h][:, :], a["L0_ffn_b2"][bass.ds(n * D, D)].partition_broadcast(P)).then_inc(got, 16)
                sp.dma_start(w2[h][:, :, :], a["L0_ffn_w2"][bass.ds(n * F, F), :].rearrange("(c p) d -> p c d", p=P)).then_inc(got, 16)

            def store(n, h):
                done = out_sent.sems[h]
                sp.dma_start(expert_rows[bass.ds(n * CAP, 2 * P), :].rearrange("(t p) d -> p t d", p=P), outr[h][:, 0:2, :]).then_inc(done, 16)
                sp.dma_start(expert_rows[bass.ds(n * CAP + 2 * P, CAP - 2 * P), :], outr[h][0:CAP - 2 * P, 2, :]).then_inc(done, 16)

            for h in range(2):
                sp.sem_inc(out_sent.sems[h], out_sent.first)
                load(h, h)
            with sp.Fori(0, PAIRS - 1) as i:
                for h in range(2):
                    sp.wait_ge(*o_r((i, h)))
                    store(i * 2 + h, h)
                    load(i * 2 + (h + 2), h)
            for h in range(2):
                sp.wait_ge(*o_r((PAIRS - 1, h)))
                store(NE - 2 + h, h)
            for h in range(2):
                sp.wait_ge(*out_sent((PAIRS - 1, h)))

        @block.gpsimd
        def _(pool):
            pool.memset(mhalf[:, :], -0.5).then_inc(s_set, 1)
            pool.memset(zero[:, :], 0.0).then_inc(s_set, 1)
            pool.memset(ones[:, :], 1.0).then_inc(s_set, 1)
            pool.iota(place[:, :], [[P, TB]], base=0, channel_multiplier=1, allow_small_or_imprecise_dtypes=True).then_inc(s_set, 1)

            def load(n, h):
                pool.dma_start(lens[h][:, :], a["patch_lens"][bass.ds(n * S, S)].partition_broadcast(P)).then_inc(p_in.sems[h], 16)
                pool.dma_start(patch[h][:, :, :], a["ctx"][bass.ds(n * S, S), :].rearrange("(t p) d -> p t d", p=P)).then_inc(p_in.sems[h], 16)

            for h in range(2):
                load(h, h)
            pool.wait_ge(s_set, 4)

            def power(b):
                pool.wait_ge(*ms_r(b))
                pool.tensor_tensor(rrms[b[1]][:, :], msq[b[1]][:, :], mhalf[:, :], ALU.pow).then_inc(rr_r.sem, 1)

            with pool.Fori(0, PAIRS - 1) as i:
                B = [(i, 0), (i, 1)]
                for b in B:
                    power(b)
                for b in B:
                    pool.wait_ge(*ends_r(b))
                    pool.wait_ge(*u_r(b))
                    pool.wait_ge(*sq_r(b))
                    load(i * 2 + (b[1] + 2), b[1])
            for h in range(2):
                power((PAIRS - 1, h))

        @block.scalar
        def _(act):
            KT = "(c p) n -> p c n"
            act.dma_start(decayT[:, :, :], a["c_decayT"].rearrange(KT, p=P)).then_inc(s_const, 16)
            act.dma_start(upto[:, :, :], a["c_upto"].rearrange(KT, p=P)).then_inc(s_const, 16)
            act.dma_start(g_init[:, :], a["L1_xattn_g_init"][0:D].partition_broadcast(P)).then_inc(s_const, 16)
            act.wait_ge(s_const, n_const)
            act.activation(uptob[:, :, :], upto[:, :, :], ACT.Copy).then_inc(s_cast, 1)
            with act.Fori(0, PAIRS) as i:
                B = [(i, 0), (i, 1)]
                for b in B:
                    h = b[1]
                    act.wait_ge(*p_in(b))
                    for t in range(TB):
                        act.activation(square[h][:, t, :], patch[h][:, t, :], ACT.Square, accum_out=ssum[h][:, t:t + 1]).then_inc(sq_r.sem, 1)
                for j in range(FT):
                    for b in B:
                        h = b[1]
                        act.wait_ge(*h_psum(b, j + 1))
                        act.activation(hid[h][:, j, :], bank[h][j % 4][:, 0:CAP], ACT.Gelu, bias=b1[h][:, j:j + 1]).then_inc(h_r.sems[h], 1)
                for b in B:
                    act.wait_ge(*st_psum(b))
                    act.activation(state[b[1]][:, :, :].rearrange("p t d -> p (t d)"), bank[b[1]][3][:, :], ACT.Copy).then_inc(st_r.sem, 1)

        @block.tensor
        def _(pe):
            pe.wait_ge(s_cast, 1)
            with pe.Fori(0, PAIRS) as i:
                B = [(i, 0), (i, 1)]
                for b in B:
                    h = b[1]
                    pe.wait_ge(*w_in(b))
                    for c in range(DT):
                        for t, (s0, n) in enumerate(SLOTS):
                            last = pe.transpose(bank[h][c][:, s0:s0 + n], rows[h][0:n, t, c * P:(c + 1) * P], identf[0:n, 0:n])
                    last.then_inc(rt_psum.sem, 1)
                for b in B:
                    h = b[1]
                    pe.wait_ge(*edge_r(b))
                    for t in range(TB):
                        last = pe.matmul(bank[h][3][:, 0:S], edge[h][:, t, :], uptob[:, t, :], start=(t == 0), stop=(t == TB - 1))
                    last.then_inc(cs_psum.sem, 1)
                for j in range(FT):
                    for b in B:
                        h = b[1]
                        if j == 0:
                            pe.wait_ge(*rt_r(b))
                        if j == 3:
                            pe.wait_ge(*plug_r(b))
                        if j >= 4:
                            pe.wait_ge(*h_r(b, j - 3))
                        for c in range(DT):
                            last = pe.matmul(bank[h][j % 4][:, 0:CAP], w1[h][:, c, j * P:(j + 1) * P], rowsT[h][:, c, :],
                                             start=(c == 0), stop=(c == DT - 1))
                        last.then_inc(h_psum.sems[h], 1)
                for b in B:
                    h = b[1]
                    pe.wait_ge(*u_r(b))
                    pe.wait_ge(*h_r(b))
                    for t in range(TB):
                        for q in range(t + 1):
                            last = pe.matmul(bank[h][3][:, t * D:(t + 1) * D], decayT[:, q, t * P:(t + 1) * P], u[h][:, q, :],
                                             start=(q == 0), stop=(q == t))
                    last.then_inc(st_psum.sem, 1)
                for b in B:
                    h = b[1]
                    for t, (s0, n) in enumerate(SLOTS):
                        for j in range(FT):
                            last = pe.matmul(bank[h][t][0:n, 0:D], hid[h][:, j, s0:s0 + n], w2[h][:, j, :],
                                             start=(j == 0), stop=(j == FT - 1))
                        last.then_inc(o_psum.sem, 1)
                for b in B:
                    h = b[1]
                    pe.wait_ge(*st_r(b))
                    pe.wait_ge(*pick_r(b))
                    for t in range(TB):
                        for q in range(TB):
                            last = pe.matmul(bank[h][3][:, t * D:(t + 1) * D], pick[h][:, q, t * P:(t + 1) * P], state[h][:, q, :],
                                             start=(q == 0), stop=(q == TB - 1))
                    last.then_inc(dp_psum.sem, 1)
                for b in B:
                    pe.wait_ge(*dp_r(b))

        @block.vector
        def _(dve):
            dve.wait_ge(s_const, n_const)
            dve.wait_ge(s_set, 4)
            dve.wait_ge(g["s_l1"], g["n_l1"])
            with dve.Fori(0, PAIRS) as i:
                B = [(i, 0), (i, 1)]
                for b in B:
                    h = b[1]
                    dve.wait_ge(*rt_psum(b))
                    for c in range(DT):
                        dve.tensor_copy(rowsT[h][:, c, :], bank[h][c][:, 0:CAP]).then_inc(rt_r.sem, 1)
                for b in B:
                    h = b[1]
                    dve.wait_ge(*p_in(b))
                    dve.tensor_copy(lensf[h][:, :], lens[h][:, :]).then_inc(ends_r.sem, 1)
                    dve.wait_ge(*ends_r(b, 1))
                    dve.tensor_tensor_scan(ends[h][:, :], lensf[h][:, :], zero[:, :], -1.0, ALU.add, ALU.add).then_inc(ends_r.sem, 1)
                    dve.wait_ge(*ends_r(b, 2))
                    dve.tensor_scalar(wrap[h][:, :], ends[h][:, :], 0.0, float(S), ALU.is_lt, ALU.mult).then_inc(ends_r.sem, 1)
                    dve.wait_ge(*ends_r(b, 3))
                    dve.tensor_tensor(ends[h][:, :], ends[h][:, :], wrap[h][:, :], ALU.add).then_inc(ends_r.sem, 1)
                    dve.wait_ge(*ends_r(b, 4))
                    for t in range(TB):
                        dve.tensor_scalar(hit[h][:, t, :], ends[h][:, :], place[:, t:t + 1], None, ALU.is_equal).then_inc(hit_r.sem, 1)
                    dve.wait_ge(*hit_r(b))
                    dve.tensor_reduce(hits[h][:, :], hit[h][:, :, :], X, ALU.max).then_inc(edge_r.sem, 1)
                    dve.wait_ge(*edge_r(b, 1))
                    for t in range(TB):
                        dve.tensor_scalar(edge[h][:, t, :], ones[:, :], hits[h][:, t:t + 1], None, ALU.mult).then_inc(edge_r.sem, 1)
                for b in B:
                    h = b[1]
                    dve.wait_ge(*sq_r(b))
                    dve.tensor_scalar(msq[h][:, :], ssum[h][:, :], 1.0 / DC, 1e-5, ALU.mult, ALU.add).then_inc(ms_r.sem, 1)
                for b in B:
                    h = b[1]
                    dve.wait_ge(*cs_psum(b))
                    dve.tensor_scalar(plug[h][:, :], bank[h][3][:, 0:S], -1.0, 0.0, ALU.add, ALU.max).then_inc(plug_r.sem, 1)
                    dve.wait_ge(*plug_r(b))
                    for t in range(TB):
                        dve.tensor_scalar(pick[h][:, t, :], plug[h][:, :], place[:, t:t + 1], None, ALU.is_equal).then_inc(pick_r.sem, 1)
                for b in B:
                    h = b[1]
                    dve.wait_ge(*rr_r(b))
                    for t in range(TB):
                        dve.scalar_tensor_tensor(u[h][:, t, :], patch[h][:, t, 0:D], rrms[h][:, t:t + 1], g_init[:, :],
                                                 ALU.mult, ALU.mult).then_inc(u_r.sem, 1)
                for b in B:
                    h = b[1]
                    dve.wait_ge(*out_sent(b, 0))
                    for t, (s0, n) in enumerate(SLOTS):
                        dve.wait_ge(*o_psum(b, t + 1))
                        dve.tensor_tensor(outr[h][0:n, t, :], bank[h][t][0:n, 0:D], b2[h][0:n, :], ALU.add).then_inc(o_r.sem, 1)
                for b in B:
                    h = b[1]
                    dve.wait_ge(*dp_psum(b))
                    dve.tensor_tensor(g["depool_all"][:, bass.ds(tile_of(b), TB), :], bank[h][3][:, :].rearrange("p (t d) -> p t d", t=TB),
                                      g["b_in"][:, :].unsqueeze(1).broadcast_to([P, TB, D]), ALU.add).then_inc(dp_r.sem, 1)


def layer1(nc, a, g, used):
    with ExitStack() as ctx:
        def sb(name, shape, dt=F32):
            return ctx.enter_context(nc.sbuf_tensor(name, shape, dt))

        def sb2(name, shape, dt=F32):
            return [sb(f"{name}{h}", shape, dt) for h in range(2)]

        def sem(name):
            used.append(ctx.enter_context(nc.semaphore(name)))
            return used[-1]

        def sig(name, per):
            return Signal(sem(name), per)

        def turns(name, per):
            return HalfSignal([sem(f"{name}{h}") for h in range(2)], per)

        dve_own = []
        idle_r = OwnSignal(sem("pool_idle_b"), 2)

        def own(name, per):
            dve_own.append(OwnSignal(sem(name), per))
            return dve_own[-1]

        def own_turns(name, per):
            dve_own.append(OwnHalfSignal([sem(f"{name}{h}") for h in range(2)], per))
            return dve_own[-1]

        def norm_signals(name):
            return {"stats": own(name + "_stats", TB), "mv": own(name + "_mv", TB), "var": sig(name + "_var", 1),
                    "rstd": sig(name + "_rstd", 1), "xn": sig(name + "_xn", TB), "xt": sig(name + "_xt_psum", 1),
                    "xts": sig(name + "_xt", DT)}

        bank, x_all, identf, identb = g["bank"], g["x_all"], g["identf"], g["identb"]
        NG = RH // GH
        NT = 2 * GH
        W1, W0 = GH * S, GH * P
        SPAN = [(k * S, S) if k < GH else (W1 + (k - GH) * P, P) for k in range(NT)]

        causal, causalb = sb("causal", [P, P]), sb("causalb", [P, P], BF16)
        mhalf = sb("mhalf_b", [P, TB])
        rows_i, wts = sb2("rows_i", [P, TB * 2], U32), sb2("wts", [P, TB, 2])
        got = sb2("got", [P, TB * 2, D])
        stats, mv = sb2("stats_b", [P, TB, 6]), sb2("mv_b", [P, TB, 2])
        var, rstd = sb2("var_b", [P, TB]), sb2("rstd_b", [P, TB])
        xn, xnT = sb2("xn_b", [P, TB, D]), sb2("xnT_b", [P, DT * S])
        qk, turned = sb2("qk", [P, TB, 512]), sb2("turned", [P, TB, 512])
        shared = sb2("shared", [P, 2 * (W1 + W0)])
        roped = [shared[h][:, 0:TB * 2 * RH * 32].rearrange("p (t a c) -> p t a c", t=TB, a=2 * RH) for h in range(2)]
        vals = sb2("vals", [P, TB, RH, 32])
        qkT = sb2("qkT", [P, NG, 2, S])
        top1, top2 = sb2("top1", [P, NT, 8]), sb2("top2", [P, NT, 8])
        nmax = sb2("nmax_b", [P, NT])
        rest, keptT = [x[:, 0:W1 + W0] for x in shared], [x[:, W1 + W0:2 * (W1 + W0)] for x in shared]
        exps, kept = sb2("exps", [P, W1 + W0]), sb2("kept", [P, W1 + W0])
        att, attr, attn = sb2("att", [P, TB, RH, RD + 1]), sb2("attr", [P, TB, RH]), xn

        attT = sb2("attT", [P, DT * S])
        outT = [attT[h][:, 0:S] for h in range(2)]
        ms = sb2("ms", [P, TB])
        idle, idle_v = sb("idle", [P, 4]), sb("idle_v", [P, 2 * NG])
        pooled, pooledb = sb2("pooled", [P, DT]), sb2("pooledb", [P, DT, P])
        ones = sb("ones_b", [P, P])
        gl, gtop, ngt = sb2("gl", [P, NE]), sb2("gtop", [P, 8]), sb2("ngt", [P, 1])
        ge, gates, gsum = sb2("ge", [P, NE]), sb2("gates", [P, NE]), sb2("gsum", [P, 1])
        NH = 3
        hid = [[sb(f"hid_b{h}{k}", [P, 512])[:, :] for k in range(NH - 1)] + [turned[h][:, 1, :]] for h in range(2)]
        acc, y = [turned[h][:, 0, :] for h in range(2)], sb2("y", [P, TB, D])

        idle_vr = own("dve_idle", NG)
        s_zero, s_set, s_const, s_cast = sem("pads_zeroed"), sem("b_memsets_done"), sem("causal_loaded"), sem("causal_cast")
        idx_r, wts_r = sig("rows_i_r", 1), own("wts_r", 1)
        got_in = g["got_in"]
        comb = own("combined", 2 * TB)
        N4, N5, N6 = norm_signals("n4"), norm_signals("n5"), norm_signals("n6")
        qk_psum, v_psum, qk_r, v_r = sig("qk_psum", TB), sig("v_psum", 1), sig("qk_r", TB), sig("v_r", TB)
        rope_a, rope_r = sig("rope_parts", TB * 3), sig("roped_r", TB)
        qkT_psum, qkT_r = sig("qkT_psum", NG), sig("qkT_r", NG)
        sc_psum = turns("scores_b_psum", NG)
        top1_r, nmax_r = own_turns("top1_r", NG * NT), turns("nmax_b_r", NG)
        rest_r, top2_r = own_turns("rest_r", NG * NT), own_turns("top2_r", NG * NT)
        exp_r = turns("exps_r", NG)
        kept_r = turns("kept_r", NG)
        kT_psum, kT_r = turns("keptT_psum", NG), turns("keptT_r", NG * 3)
        oT_psum, oT_r, av_psum, av_r = turns("outT_psum", NG), turns("outT_r", NG), turns("att_psum", NG), turns("att_r", NG)
        den_r, attn_r = own("att_recip", 1), sig("attn_r", 1)
        aT_psum, aT_r, ao_psum, x4 = sig("attT_psum", 1), sig("attT_r", 1), sig("att_out_psum", 1), own("x4_ready", 1)
        ms_r, ms_p, rr_r = sig("ms_r", 3), sig("ms_rsqrt", 1), own("rr_r", 1)
        xd, win_psum, x5 = sig("x_plus_depool", 1), sig("win_psum", 1), own("x5_ready", 1)
        pb_r, gl_psum, gl_r = sig("pooled_bcast", DT), sig("gate_psum", 1), own("gl_r", 1)
        gtop_r, ngt_r, ge_r, gm_r = own("gtop_r", 1), sig("ngt_r", 1), sig("gate_exp", 1), own("gates_r", 4)
        e_psum, e_r, acc_r = turns("expert_psum", NE), turns("expert_gelu", NE), turns("acc_r", NE)
        f_psum, y_r = sig("final_psum", 1), sig("y_r", 1)
        y_out = HalfSignal([sem(f"y_stored{h}") for h in range(2)], 16, 1)
        block = ctx.enter_context(nc.Block())

        @block.sync
        def _(sp):
            sp.dma_start(causal[:, :], a["c_causal"]).then_inc(s_const, 16)
            for h in range(2):
                sp.sem_inc(y_out.sems[h], y_out.first)
            with sp.Fori(0, PAIRS) as i:
                for b in [(i, 0), (i, 1)]:
                    h = b[1]
                    sp.wait_ge(*y_r(b))
                    sp.dma_start(a["out"][bass.ds((i * 2 + h) * S, S), :].rearrange("(t p) d -> p t d", p=P), y[h][:, :, :]).then_inc(y_out.sems[h], 16)
            for h in range(2):
                sp.wait_ge(*y_out((PAIRS - 1, h)))

        @block.gpsimd
        def _(pool):
            pool.memset(mhalf[:, :], -0.5).then_inc(s_set, 1)
            pool.memset(ones[:, :], 1.0).then_inc(s_set, 1)
            for h in range(2):
                pool.memset(shared[h][:, :], 0.0).then_inc(s_set, 1)
                pool.memset(vals[h][:, :, :, RD:32], 0.0).then_inc(s_zero, 1)
            pool.wait_ge(s_zero, 2)
            for h in range(2):
                pool.memset(vals[h][:, :, :, RD], 1.0).then_inc(s_set, 1)
            pool.wait_ge(s_set, 6)

            def power(v, out, waits, done, b):
                pool.wait_ge(*waits)
                pool.tensor_tensor(out[b[1]][:, :], v[b[1]][:, :], mhalf[:, :], ALU.pow).then_inc(done, 1)

            with pool.Fori(0, PAIRS) as i:
                B = [(i, 0), (i, 1)]
                for b in B:
                    h = b[1]
                    pool.wait_ge(*idx_r(b))
                    pool.tensor_tensor(idle[:, 2 * 0 + b[1]:2 * 0 + b[1] + 1], mhalf[:, 0:1], mhalf[:, 0:1], ALU.add).then_inc(idle_r.sem, 1)
                    for k in range(2 * TB):
                        pool.indirect_dma_start(
                            out=got[h][:, k, :], out_offset=None, in_=g["expert_rows"],
                            in_offset=bass.IndirectOffsetOnAxis(ap=rows_i[h][:, k:k + 1], axis=0),
                            bounds_check=NE * CAP - 1, oob_is_err=False).then_inc(got_in.sems[h], 16)
                for b in B:
                    power(var, rstd, N4["var"](b), N4["rstd"].sem, b)
                for b in B:
                    h = b[1]
                    for t in range(TB):
                        q2 = qk[h][:, t, :].rearrange("p (a two) -> p a two", two=2)
                        o2 = turned[h][:, t, :].rearrange("p (a two) -> p a two", two=2)
                        s2 = g["rope_sin"][:, t, :].rearrange("p (a two) -> p a two", two=2)
                        pool.wait_ge(*qk_r(b, t + 1))
                        for e in range(2):
                            pool.tensor_tensor(o2[:, :, e], q2[:, :, 1 - e], s2[:, :, e], ALU.mult).then_inc(rope_a.sem, 1)
                        pool.wait_ge(*rope_a(b, 3 * t + 2))
                        pool.tensor_tensor(qk[h][:, t, :], qk[h][:, t, :], g["rope_cos"][:, t, :], ALU.mult).then_inc(rope_a.sem, 1)
                        pool.wait_ge(*rope_a(b, 3 * t + 3))
                        pool.tensor_tensor(roped[h][:, t, :, 0:RD], qk[h][:, t, :].rearrange("p (a c) -> p a c", c=RD),
                                           turned[h][:, t, :].rearrange("p (a c) -> p a c", c=RD), ALU.add).then_inc(rope_r.sem, 1)
                for b in B:
                    power(var, rstd, N5["var"](b), N5["rstd"].sem, b)
                for b in B:
                    power(ms, ms, ms_r(b), ms_p.sem, b)
                for b in B:
                    x = x_all[:, bass.ds(tile_of(b), TB), :]
                    pool.wait_ge(*N5["xn"](b))
                    pool.tensor_tensor(idle[:, 2 * 1 + b[1]:2 * 1 + b[1] + 1], mhalf[:, 0:1], mhalf[:, 0:1], ALU.add).then_inc(idle_r.sem, 1)
                    pool.tensor_tensor(x, x, g["depool_all"][:, bass.ds(tile_of(b), TB), :], ALU.add).then_inc(xd.sem, 1)
                for b in B:
                    power(var, rstd, N6["var"](b), N6["rstd"].sem, b)
                finish(pool, [idle_r])

        @block.scalar
        def _(act):
            act.wait_ge(s_const, 16)
            act.activation(causalb[:, :], causal[:, :], ACT.Copy).then_inc(s_cast, 1)
            act.wait_ge(s_set, 6)

            def copy(out, psum, done, *waits, **kw):
                for w in waits:
                    act.wait_ge(*w)
                act.activation(out, psum, ACT.Copy, **kw).then_inc(done, 1)

            with act.Fori(0, PAIRS) as i:
                B = [(i, 0), (i, 1)]
                for b in B:
                    h = b[1]
                    act.wait_ge(*N4["xt"](b))
                    for c in range(DT):
                        copy(xnT[h][:, c * S:(c + 1) * S], bank[h][0][:, c * S:(c + 1) * S], N4["xts"].sem)
                for b in B:
                    h = b[1]
                    for t in range(TB):
                        copy(qk[h][:, t, :], bank[h][2 + t][:, :], qk_r.sem, qk_psum(b, t + 1))
                    act.wait_ge(*v_psum(b))
                    for t in range(TB):
                        copy(vals[h][:, t, :, 0:RD], bank[h][1][:, t * D:(t + 1) * D].rearrange("p (a c) -> p a c", c=RD), v_r.sem)
                for b in B:
                    h = b[1]
                    for q in range(NG):
                        copy(qkT[h][:, q, :, :].rearrange("p a c -> p (a c)"), bank[h][q][:, :], qkT_r.sem, qkT_psum(b, q + 1))
                def heads_out(b, gr):
                    h = b[1]
                    copy(att[h][:, :, gr:RH:NG, :], bank[h][3][:, S:2 * S].rearrange("p (t a c) -> p t a c", t=TB, a=GH)[:, :, :, 0:RD + 1],
                         av_r.sems[h], av_psum(b, gr + 1))

                steps = [(b, gr) for gr in range(NG) for b in B]
                for n_step, (b, gr) in enumerate(steps):
                    h = b[1]
                    act.wait_ge(*nmax_r(b, gr + 1))
                    if gr > 0:
                        act.wait_ge(*kept_r(b, gr))
                    for k, (o, n) in enumerate(SPAN):
                        if o % 512 == 0:
                            act.wait_ge(*rest_r(b, NT * gr + (o + 512) // n - (0 if k < GH else W1 // n - GH)))
                        src = bank[h][o // 512][:, o % 512:o % 512 + n]
                        last = act.activation(exps[h][:, o:o + n], src, ACT.Exp, bias=nmax[h][:, k:k + 1], scale=RD ** -0.5)
                    last.then_inc(exp_r.sems[h], 1)
                    if n_step >= 2:
                        heads_out(*steps[n_step - 2])
                    act.wait_ge(*kT_psum(b, gr + 1))
                    for q in range(3):
                        copy(keptT[h][:, q * 512:(q + 1) * 512], bank[h][q][:, :], kT_r.sems[h])
                    if n_step >= 1:
                        b, gr = steps[n_step - 1]
                        copy(outT[b[1]], bank[b[1]][3][:, 0:S], oT_r.sems[b[1]], oT_psum(b, gr + 1))
                heads_out(*steps[-2])
                b, gr = steps[-1]
                copy(outT[b[1]], bank[b[1]][3][:, 0:S], oT_r.sems[b[1]], oT_psum(b, gr + 1))
                heads_out(b, gr)
                for b in B:
                    copy(attT[b[1]][:, :], bank[b[1]][0][:, :], aT_r.sem, aT_psum(b))
                for b in B:
                    h = b[1]
                    act.wait_ge(*N5["xt"](b))
                    for c in range(DT):
                        copy(xnT[h][:, c * S:(c + 1) * S], bank[h][2][:, c * S:(c + 1) * S], N5["xts"].sem, scale=g["g_res"][:, c:c + 1])
                for b in B:
                    h = b[1]
                    act.wait_ge(*N6["xt"](b))
                    for c in range(DT):
                        copy(xnT[h][:, c * S:(c + 1) * S], bank[h][0][:, c * S:(c + 1) * S], N6["xts"].sem, accum_out=pooled[h][:, c:c + 1])
                for b in B:
                    h = b[1]
                    act.wait_ge(*ngt_r(b))
                    act.activation(ge[h][:, :], gl[h][:, :], ACT.Exp, bias=ngt[h][:, 0:1]).then_inc(ge_r.sem, 1)
                for e in range(NE):
                    for b in B:
                        h = b[1]
                        act.wait_ge(*e_psum(b, e + 1))
                        if e >= NH:
                            act.wait_ge(*acc_r(b, e - NH + 1))
                        for o in range(DT):
                            last = act.activation(hid[h][e % NH][:, o * S:(o + 1) * S], bank[h][e % 3][:, o * S:(o + 1) * S], ACT.Gelu,
                                                  bias=g["expert_b"][:, e, o:o + 1])
                        last.then_inc(e_r.sems[h], 1)

        @block.tensor
        def _(pe):
            pe.wait_ge(s_cast, 1)
            pe.wait_ge(s_set, 6)
            with pe.Fori(0, PAIRS) as i:
                B = [(i, 0), (i, 1)]

                def scores(b, gr):
                    h = b[1]
                    r0 = 32 * gr
                    if gr == 0:
                        pe.wait_ge(*qkT_r(b))
                    else:
                        pe.wait_ge(*kT_r(b, 3 * gr))
                    for k, (o, n) in enumerate(SPAN):
                        q, t = k % GH, 1 if k < GH else 0
                        out = bank[h][o // 512][:, o % 512:o % 512 + n]
                        pe.matmul(out, qkT[h][r0:r0 + RD, q, 0, t * P:(t + 1) * P], qkT[h][r0:r0 + RD, q, 1, 0:n], start=True, stop=False)
                        last = pe.matmul(bank[h][o // 512][:, o % 512 + n - P:o % 512 + n], identb[:, :], causalb[:, :], start=False, stop=True)
                    last.then_inc(sc_psum.sems[h], 1)

                for b in B:
                    pe.wait_ge(*N4["xn"](b))
                    transpose_rows(pe, bank[b[1]][0], xn[b[1]], identf).then_inc(N4["xt"].sem, 1)
                for b in B:
                    h = b[1]
                    pe.wait_ge(*N4["xts"](b))
                    for t in range(TB):
                        for k in range(DT):
                            last = pe.matmul(bank[h][2 + t][:, :], xnT[h][:, k * S + t * P:k * S + (t + 1) * P], g["qkv_w"][:, k, 0:512],
                                             start=(k == 0), stop=(k == DT - 1))
                        last.then_inc(qk_psum.sem, 1)
                    for t in range(TB):
                        for k in range(DT):
                            last = pe.matmul(bank[h][1][:, t * D:(t + 1) * D], xnT[h][:, k * S + t * P:k * S + (t + 1) * P],
                                             g["qkv_w"][:, k, 512:768], start=(k == 0), stop=(k == DT - 1))
                    last.then_inc(v_psum.sem, 1)
                for b in B:
                    h = b[1]
                    pe.wait_ge(*rope_r(b))
                    pe.wait_ge(*v_r(b))
                    for gr in range(NG):
                        for q in range(2):
                            for t in range(TB):
                                last = pe.transpose(bank[h][gr][:, q * S + t * P:q * S + (t + 1) * P],
                                                    roped[h][:, t, q * RH + gr * GH:q * RH + (gr + 1) * GH, :].rearrange("p a c -> p (a c)"),
                                                    identf[:, :])
                        last.then_inc(qkT_psum.sem, 1)
                for b in B:
                    scores(b, 0)

                def weighted(b, gr):
                    h = b[1]
                    pe.wait_ge(*kT_r(b, 3 * gr + 3))
                    if gr > 0:
                        pe.wait_ge(*av_r(b, gr))
                    for s in range(TB):
                        for j in range(GH):
                            last = pe.matmul(bank[h][3][32 * j:32 * j + 32, s * P:S], vals[h][:, s, j * NG + gr, :],
                                             keptT[h][:, (3 * j + 2 * s) * P:(3 * j + 2 + s) * P], start=(s == 0), stop=(s == TB - 1))
                    last.then_inc(oT_psum.sems[h], 1)

                def heads_back(b, gr):
                    h = b[1]
                    pe.wait_ge(*oT_r(b, gr + 1))
                    for t in range(TB):
                        last = pe.transpose(bank[h][3][:, S + t * P:S + (t + 1) * P], outT[h][:, t * P:(t + 1) * P], identf[:, :])
                    last.then_inc(av_psum.sems[h], 1)

                steps = [(b, gr) for gr in range(NG) for b in B]
                for n_step, (b, gr) in enumerate(steps):
                    h = b[1]
                    pe.wait_ge(*kept_r(b, gr + 1))
                    for q in range(3 * GH):
                        j, o = q // 3, (W1 + q // 3 * P, q // 3 * S, q // 3 * S + P)[q % 3]
                        last = pe.transpose(bank[h][q // 4][:, (q % 4) * P:(q % 4 + 1) * P], kept[h][:, o:o + P], identf[:, :])
                    last.then_inc(kT_psum.sems[h], 1)
                    if n_step >= 1:
                        weighted(*steps[n_step - 1])
                    if gr < NG - 1:
                        scores(b, gr + 1)
                    if n_step >= 1:
                        heads_back(*steps[n_step - 1])
                weighted(*steps[-1])
                heads_back(*steps[-1])
                for b in B:
                    pe.wait_ge(*attn_r(b))
                    transpose_rows(pe, bank[b[1]][0], attn[b[1]], identf).then_inc(aT_psum.sem, 1)
                for b in B:
                    h = b[1]
                    pe.wait_ge(*aT_r(b))
                    for t in range(TB):
                        for k in range(DT):
                            last = pe.matmul(bank[h][1][:, t * D:(t + 1) * D], attT[h][:, k * S + t * P:k * S + (t + 1) * P],
                                             g["attn_out_w"][:, k, :], start=(k == 0), stop=(k == DT - 1))
                    last.then_inc(ao_psum.sem, 1)
                for b in B:
                    pe.wait_ge(*N5["xn"](b))
                    transpose_rows(pe, bank[b[1]][2], xn[b[1]], identf).then_inc(N5["xt"].sem, 1)
                for b in B:
                    h = b[1]
                    pe.wait_ge(*N5["xts"](b))
                    for t in range(TB):
                        for k in range(DT):
                            last = pe.matmul(bank[h][1][:, t * D:(t + 1) * D], xnT[h][:, k * S + t * P:k * S + (t + 1) * P],
                                             g["win_w"][:, k, :], start=(k == 0), stop=(k == DT - 1))
                    last.then_inc(win_psum.sem, 1)
                for b in B:
                    pe.wait_ge(*N6["xn"](b))
                    transpose_rows(pe, bank[b[1]][0], xn[b[1]], identf).then_inc(N6["xt"].sem, 1)
                for b in B:
                    h = b[1]
                    pe.wait_ge(*pb_r(b))
                    for k in range(DT):
                        last = pe.matmul(bank[h][3][:, 0:NE], pooledb[h][:, k, :], g["gate_w"][:, k, :], start=(k == 0), stop=(k == DT - 1))
                    last.then_inc(gl_psum.sem, 1)
                for e in range(NE):
                    for b in B:
                        h = b[1]
                        if e >= 3:
                            pe.wait_ge(*e_r(b, e - 2))
                        for o in range(DT):
                            for k in range(DT):
                                last = pe.matmul(bank[h][e % 3][:, o * S:(o + 1) * S], g["expert_w"][:, k, e * D + o * P:e * D + (o + 1) * P],
                                                 xnT[h][:, k * S:(k + 1) * S], start=(k == 0), stop=(k == DT - 1))
                        last.then_inc(e_psum.sems[h], 1)
                for b in B:
                    h = b[1]
                    pe.wait_ge(*acc_r(b))
                    for t in range(TB):
                        for o in range(DT):
                            last = pe.transpose(bank[h][3][:, t * D + o * P:t * D + (o + 1) * P], acc[h][:, o * S + t * P:o * S + (t + 1) * P], identf[:, :])
                    last.then_inc(f_psum.sem, 1)

        @block.vector
        def _(dve):
            dve.wait_ge(s_set, 6)
            with dve.Fori(0, PAIRS) as i:
                B = [(i, 0), (i, 1)]

                def xt(b):
                    return lambda t: x_all[:, bass.ds(tile_of(b) + t, 1), :].rearrange("p a d -> p (a d)")

                for b in B:
                    h = b[1]
                    dve.tensor_copy(rows_i[h][:, :].rearrange("p (t k) -> p t k", k=2), g["choice_row"][:, bass.ds(tile_of(b), TB), :]).then_inc(idx_r.sem, 1)
                    dve.tensor_copy(wts[h][:, :, :], g["choice_w"][:, bass.ds(tile_of(b), TB), :]).then_inc(wts_r.sem, 1)
                for b in B:
                    h = b[1]
                    dve.wait_ge(*wts_r(b))
                    dve.wait_ge(*got_in(b))
                    for k in range(2):
                        for t in range(TB):
                            if k:
                                dve.wait_ge(*comb(b, t + 1))
                            dve.scalar_tensor_tensor(xt(b)(t), got[h][:, 2 * t + k, :], wts[h][:, t, k:k + 1], xt(b)(t),
                                                     ALU.mult, ALU.add).then_inc(comb.sem, 1)
                for b in B:
                    dve.wait_ge(*comb(b))
                    norm_stats(dve, xt(b), stats, mv, var, N4, b)
                for b in B:
                    norm_apply(dve, xt(b), xn, mv, rstd, N4, b)
                for gr in range(NG):
                    for b in B:
                        h = b[1]
                        dve.wait_ge(*sc_psum(b, gr + 1))
                        dve.memset(idle_v[:, 2 * gr + h:2 * gr + h + 1], 0.0).then_inc(idle_vr.sem, 1)
                        for k, (o, n) in enumerate(SPAN):
                            dve.max(top1[h][:, k, :], bank[h][o // 512][:, o % 512:o % 512 + n]).then_inc(top1_r.sems[h], 1)
                        dve.wait_ge(*top1_r(b, NT * (gr + 1)))
                        dve.tensor_scalar(nmax[h][:, :], top1[h][:, :, 0], -RD ** -0.5, None, ALU.mult).then_inc(nmax_r.sems[h], 1)
                        for k, (o, n) in enumerate(SPAN):
                            dve.match_replace(rest[h][:, o:o + n], top1[h][:, k, :], bank[h][o // 512][:, o % 512:o % 512 + n], -3.0e38).then_inc(rest_r.sems[h], 1)
                        dve.wait_ge(*rest_r(b, NT * (gr + 1)))
                        for k, (o, n) in enumerate(SPAN):
                            dve.max(top2[h][:, k, :], rest[h][:, o:o + n]).then_inc(top2_r.sems[h], 1)
                        dve.wait_ge(*top2_r(b, NT * (gr + 1)))
                        dve.wait_ge(*exp_r(b, gr + 1))
                        for k, (o, n) in enumerate(SPAN):
                            last = dve.scalar_tensor_tensor(kept[h][:, o:o + n], bank[h][o // 512][:, o % 512:o % 512 + n],
                                                            top2[h][:, k, TOPK - 9:TOPK - 8], exps[h][:, o:o + n], ALU.is_ge, ALU.mult)
                        last.then_inc(kept_r.sems[h], 1)
                for b in B:
                    h = b[1]
                    dve.wait_ge(*av_r(b))
                    dve.reciprocal(attr[h][:, :, :], att[h][:, :, :, RD]).then_inc(den_r.sem, 1)
                    dve.wait_ge(*den_r(b))
                    dve.tensor_tensor(attn[h][:, :, :].rearrange("p t (a c) -> p t a c", c=RD), att[h][:, :, :, 0:RD],
                                      attr[h][:, :, :].unsqueeze(3).broadcast_to([P, TB, RH, RD]), ALU.mult).then_inc(attn_r.sem, 1)
                for b in B:
                    h = b[1]
                    x = x_all[:, bass.ds(tile_of(b), TB), :]
                    dve.wait_ge(*ao_psum(b))
                    dve.tensor_tensor(x, bank[h][1][:, :].rearrange("p (t d) -> p t d", t=TB), x, ALU.add).then_inc(x4.sem, 1)
                for b in B:
                    dve.wait_ge(*x4(b))
                    norm_stats(dve, xt(b), stats, mv, var, N5, b)
                for b in B:
                    h = b[1]
                    dve.wait_ge(*N5["rstd"](b))
                    dve.tensor_tensor(ms[h][:, :], mv[h][:, :, 1], rstd[h][:, :], ALU.mult).then_inc(ms_r.sem, 1)
                    dve.wait_ge(*ms_r(b, 1))
                    dve.tensor_tensor(ms[h][:, :], ms[h][:, :], rstd[h][:, :], ALU.mult).then_inc(ms_r.sem, 1)
                    dve.wait_ge(*ms_r(b, 2))
                    dve.tensor_scalar(ms[h][:, :], ms[h][:, :], 1e-5, None, ALU.add).then_inc(ms_r.sem, 1)
                for b in B:
                    h = b[1]
                    dve.wait_ge(*ms_p(b))
                    dve.tensor_tensor(rstd[h][:, :], rstd[h][:, :], ms[h][:, :], ALU.mult).then_inc(rr_r.sem, 1)
                    dve.wait_ge(*rr_r(b))
                    norm_apply(dve, xt(b), xn, mv, rstd, N5, b)
                for b in B:
                    h = b[1]
                    x = x_all[:, bass.ds(tile_of(b), TB), :]
                    dve.wait_ge(*win_psum(b))
                    dve.wait_ge(*xd(b))
                    dve.tensor_tensor(x, bank[h][1][:, :].rearrange("p (t d) -> p t d", t=TB), x, ALU.add).then_inc(x5.sem, 1)
                for b in B:
                    dve.wait_ge(*x5(b))
                    norm_stats(dve, xt(b), stats, mv, var, N6, b)
                for b in B:
                    norm_apply(dve, xt(b), xn, mv, rstd, N6, b)
                for b in B:
                    h = b[1]
                    dve.wait_ge(*N6["xts"](b))
                    for c in range(DT):
                        dve.tensor_scalar(pooledb[h][:, c, :], ones[:, :], pooled[h][:, c:c + 1], 1.0 / S, ALU.mult, ALU.mult).then_inc(pb_r.sem, 1)
                for b in B:
                    h = b[1]
                    dve.wait_ge(*gl_psum(b))
                    dve.tensor_tensor(gl[h][:, :], bank[h][3][:, 0:NE], g["gate_b"][:, :], ALU.add).then_inc(gl_r.sem, 1)
                    dve.wait_ge(*gl_r(b))
                    dve.max(gtop[h][:, :], gl[h][:, :]).then_inc(gtop_r.sem, 1)
                    dve.wait_ge(*gtop_r(b))
                    dve.tensor_scalar(ngt[h][:, :], gtop[h][:, 0:1], -1.0, None, ALU.mult).then_inc(ngt_r.sem, 1)
                for b in B:
                    h = b[1]
                    dve.wait_ge(*ge_r(b))
                    dve.scalar_tensor_tensor(gates[h][:, :], gl[h][:, :], gtop[h][:, 1:2], ge[h][:, :], ALU.is_ge, ALU.mult).then_inc(gm_r.sem, 1)
                    dve.wait_ge(*gm_r(b, 1))
                    dve.tensor_reduce(gsum[h][:, :], gates[h][:, :], X, ALU.add).then_inc(gm_r.sem, 1)
                    dve.wait_ge(*gm_r(b, 2))
                    dve.reciprocal(gsum[h][:, :], gsum[h][:, :]).then_inc(gm_r.sem, 1)
                    dve.wait_ge(*gm_r(b, 3))
                    dve.tensor_scalar(gates[h][:, :], gates[h][:, :], gsum[h][:, 0:1], None, ALU.mult).then_inc(gm_r.sem, 1)
                for e in range(NE):
                    for b in B:
                        h = b[1]
                        dve.wait_ge(*e_r(b, e + 1))
                        if e == 0:
                            dve.wait_ge(*gm_r(b))
                            dve.tensor_scalar(acc[h][:, :], hid[h][0][:, :], gates[h][:, 0:1], None, ALU.mult).then_inc(acc_r.sems[h], 1)
                        else:
                            dve.wait_ge(*acc_r(b, e))
                            dve.scalar_tensor_tensor(acc[h][:, :], hid[h][e % NH][:, :], gates[h][:, e:e + 1], acc[h][:, :], ALU.mult, ALU.add).then_inc(acc_r.sems[h], 1)
                for b in B:
                    h = b[1]
                    dve.wait_ge(*f_psum(b))
                    dve.wait_ge(*y_out(b, 0))
                    dve.tensor_tensor(y[h][:, :, :], bank[h][3][:, :].rearrange("p (t d) -> p t d", t=TB), x_all[:, bass.ds(tile_of(b), TB), :],
                                      ALU.add).then_inc(y_r.sem, 1)
                finish(dve, dve_own)


def constants():
    import numpy as np

    n = np.arange(1, RD // 2 + 1, dtype=np.float64)
    t = 10.0 + 6.0 * n
    for _ in range(60):
        f = t / (2 * np.pi) * np.log(t / (2 * np.pi * np.e)) - (n - 0.875)
        t = t - f / (np.log(t / (2 * np.pi)) / (2 * np.pi))
    z = t / t[0]
    denom = 0.25 + z * z
    w_re = (0.5 / denom).astype(np.float32).astype(np.float64)
    w_im = (-z / denom).astype(np.float32).astype(np.float64)
    pos = np.arange(S, dtype=np.float32)
    K = RD // 2
    phase = pos[:, None] * (10000.0 ** (-np.arange(K, dtype=np.float32) / K))[None, :]
    cos, sin = np.cos(phase).astype(np.float32).astype(np.float64), np.sin(phase).astype(np.float32).astype(np.float64)
    grow = np.sqrt(1.0 + pos.astype(np.float64))[:, None]
    kc = np.stack([cos, cos], -1) * grow[:, :, None]
    ks = np.stack([sin, -sin], -1) * grow[:, :, None]
    qc1 = w_re * cos + w_im * sin
    qs1 = w_re * sin - w_im * cos
    qc = np.stack([qc1, qc1], -1) / grow[:, :, None]
    qs = np.stack([qs1, -qs1], -1) / grow[:, :, None]
    c_cos = np.concatenate([np.tile(qc.reshape(S, RD), (1, RH)), np.tile(kc.reshape(S, RD), (1, RH))], 1).astype(np.float32)
    c_sin = np.concatenate([np.tile(qs.reshape(S, RD), (1, RH)), np.tile(ks.reshape(S, RD), (1, RH))], 1).astype(np.float32)
    logp = np.float32(-0.001)
    dt = -np.log(-np.expm1(logp))
    decay, first = float(np.exp(-dt)), float(np.exp(logp))
    i, j = np.arange(S)[:, None], np.arange(S)[None, :]
    gap = np.where(j >= i, j - i, 0)
    c_decayT = np.where(j >= i, first * decay ** gap, 0.0)
    pi, pj = np.arange(P)[:, None], np.arange(P)[None, :]
    return {
        "c_ident": np.eye(P, dtype=np.float32),
        "c_before": (pi < pj).astype(np.float32),
        "c_causal": np.where(pj > pi, NEG, 0.0).astype(np.float32),
        "c_cos": c_cos, "c_sin": c_sin,
        "c_decayT": c_decayT.astype(np.float32),
        "c_upto": (i <= j).astype(np.float32),
    }


def kernel(**inputs):
    import numpy as np
    import concourse.bacc as bacc
    from concourse.bass_utils import run_bass_kernel_spmd

    v = {k: np.asarray(x) for k, x in inputs.items()}
    cols = lambda x: x.reshape(-1, P).T
    arrays = {
        "x": v["x"].reshape(NB * S, D), "ctx": v["ctx_2048"].reshape(NB * S, DC),
        "ctxT": v["ctx_2048"].transpose(0, 2, 1).reshape(NB * DC, S),
        "mask": v["mask_BxS2_fk1"].reshape(-1), "maskC": cols(v["mask_BxS2_fk1"].reshape(-1)),
        "patch_lens": v["mask_BxS2_if0"].reshape(-1),
        "L0_xattn_W_srcT": v["L0_xattn_W_src"].T, "L0_xattn_W_tgtT": v["L0_xattn_W_tgt"].T,
        "L0_xattn_W_outT": v["L0_xattn_W_out"].T, "L0_xattn_b_srcC": cols(v["L0_xattn_b_src"]),
        "L0_xattn_b_tgtC": cols(v["L0_xattn_b_tgt"]),
        "L0_ffn_w1": v["L0_ffn_w1"].reshape(NE * D, F), "L0_ffn_w2": v["L0_ffn_w2"].reshape(NE * F, D),
        "L0_ffn_b1C": v["L0_ffn_b1"].reshape(NE, FT, P).transpose(0, 2, 1).reshape(NE * P, FT),
        "L0_ffn_b2": v["L0_ffn_b2"].reshape(-1),
        "L1_xattn_g_resC": cols(v["L1_xattn_g_res"]),
        "L1_xattn_W_inT": v["L1_xattn_W_in"].T,
        "L1_ffn_gate_wT": v["L1_ffn_gate_w"].T,
        "L1_ffn_expert_wT": v["L1_ffn_expert_w"].transpose(2, 0, 1).reshape(D, NE * D),
        "L1_ffn_expert_bC": v["L1_ffn_expert_b"].reshape(NE, DT, P).transpose(2, 0, 1),
    }
    for k in ("L0_attn_Wq", "L0_attn_Wk", "L0_attn_Wv", "L0_attn_Wo", "L0_attn_bo", "L0_xattn_b_src", "L0_xattn_b_out",
              "L0_ffn_w_router", "L0_ffn_b_router", "L1_attn_Wq", "L1_attn_Wk", "L1_attn_Wv", "L1_attn_Wo",
              "L1_xattn_b_in", "L1_xattn_g_init", "L1_ffn_gate_b"):
        arrays[k] = v[k]
    arrays.update(constants())
    nc = bacc.Bacc("TRN2", target_bir_lowering=False, num_devices=1)
    a, feed = {}, {}
    for k, x in arrays.items():
        feed[f"in_{k}"] = np.ascontiguousarray(x)
        a[k] = nc.dram_tensor(f"in_{k}", x.shape, mybir.dt.from_np(x.dtype), kind="ExternalInput").ap()
    a["out"] = nc.dram_tensor("y_dram", (NB * S, D), F32, kind="ExternalOutput").ap()
    decoder(nc, a)
    r = run_bass_kernel_spmd(nc, [feed], core_ids=[0])
    return r.results[0]["y_dram"].reshape(NB, S, D)
```

```python
from contextlib import ExitStack

import concourse.bass as bass
from concourse import mybir

F32 = mybir.dt.float32
BF16 = mybir.dt.bfloat16
I32 = mybir.dt.int32
U32 = mybir.dt.uint32
ALU = mybir.AluOpType
ACT = mybir.ActivationFunctionType
X = mybir.AxisListType.X

P = 128
NB = 8
S = 256
TB = S // P
D = 256
DT = D // P
DC = 512
CT = DC // P
PAIRS = NB // 2
NE = 8
CAP = int(1.25 * NB * S / NE)
F = 1024
FT = F // P
XH, XD = 8, 32
RH, RD = 16, 16
GH = 4
TOPK = 13
NEG = -1.0e30
LN_EPS = 1e-5
RMS_EPS = 1e-5
SLOTS = [(0, 128), (128, 128), (256, CAP - 256)]


class Signal:

    def __init__(self, sem, per):
        self.sem, self.per = sem, per

    def __call__(self, b, j=None):
        i, h = b
        return self.sem, i * (2 * self.per) + (h * self.per + (self.per if j is None else j))


class HalfSignal:

    def __init__(self, sems, per, first=0):
        self.sems, self.per, self.first = sems, per, first

    def __call__(self, b, j=None):
        i, h = b
        return self.sems[h], i * self.per + (self.first + (self.per if j is None else j))


class OwnSignal:

    def __init__(self, sem, per):
        self.sem, self.per = sem, per

    def __call__(self, b, j=None):
        return self.sem, b[1] * self.per + (self.per if j is None else j)


class OwnHalfSignal:

    def __init__(self, sems, per):
        self.sems, self.per = sems, per

    def __call__(self, b, j=None):
        return self.sems[b[1]], self.per if j is None else j


def finish(eng, own):
    for s in own:
        for sem, count in [(s.sem, 2 * s.per)] if isinstance(s, OwnSignal) else [(x, s.per) for x in s.sems]:
            eng.wait_ge(sem, count)
            eng.sem_clear(sem)


def tile_of(b):
    i, h = b
    return i * (2 * TB) + h * TB


def decoder(nc, a):
    with ExitStack() as ctx:
        def sb(name, shape, dt=F32):
            return ctx.enter_context(nc.sbuf_tensor(name, shape, dt))

        def sem(name):
            return ctx.enter_context(nc.semaphore(name))

        g = {}
        bank = [[ctx.enter_context(nc.psum_tensor(f"bank{h}{k}", [P, 512], F32)) for k in range(4)]
                for h in range(2)]
        g["bank"] = bank
        g["x_all"] = sb("x_all", [P, NB * TB, D])
        g["depool_all"] = sb("depool_all", [P, NB * TB, D])
        g["choice_w"] = sb("choice_w", [P, NB * TB, 2])
        g["choice_row"] = sb("choice_row", [P, NB * TB, 2], U32)
        g["identf"] = sb("identf", [P, P])
        g["identb"] = sb("identb", [P, P], BF16)
        for name, shape in (("qkv_w", [P, DT, 768]), ("attn_out_w", [P, DT, D]), ("win_w", [P, DT, D]),
                            ("gate_w", [P, DT, NE]), ("rope_cos", [P, TB, 512]), ("rope_sin", [P, TB, 512]),
                            ("b_in", [P, D]), ("gate_b", [P, NE]), ("g_res", [P, DT]),
                            ("expert_b", [P, NE, DT]), ("expert_w", [P, DT, NE * D])):
            g[name] = sb("l1_" + name, shape)
        g["s_l1"] = sem("layer1_constants_loaded")
        for name, per, first in (("sent", 64, 32), ("p_in", 32, 0), ("got_in", 64, 0)):
            g[name] = HalfSignal([sem(f"{name}{h}") for h in range(2)], per, first)
        g["slots"] = nc.dram_tensor("slots", (NE * CAP, D), F32, kind="Internal").ap()
        g["expert_rows"] = nc.dram_tensor("expert_rows", (NE * CAP, D), F32, kind="Internal").ap()
        for part in (layer0, experts, layer1):
            used = []
            part(nc, a, g, used)
            if part is not layer1:
                clear(nc, used)


def clear(nc, used):
    nums = sorted(s.num for s in used)
    while nums:
        n = 1
        while n < len(nums) and nums[n] == nums[0] + n:
            n += 1
        nc.sync.sem_clear(range(nums[0], nums[0] + n))
        nums = nums[n:]
    nc.all_engine_barrier()


def norm_stats(dve, x, stats, mv, var, got, b, scale_add=(1.0, LN_EPS)):
    h = b[1]
    for t in range(TB):
        dve.bn_stats(stats[h][:, t, :], x(t)).then_inc(got["stats"].sem, 1)
    for t in range(TB):
        dve.wait_ge(*got["stats"](b, t + 1))
        dve.bn_aggr(mv[h][:, t, :], stats[h][:, t, :]).then_inc(got["mv"].sem, 1)
    dve.wait_ge(*got["mv"](b))
    dve.tensor_scalar(var[h][:, :], mv[h][:, :, 1], *scale_add, ALU.mult, ALU.add).then_inc(got["var"].sem, 1)


def norm_apply(dve, x, xn, mv, rstd, got, b):
    h = b[1]
    dve.wait_ge(*got["rstd"](b))
    for t in range(TB):
        dve.tensor_scalar(xn[h][:, t, :], x(t), mv[h][:, t, 0:1], rstd[h][:, t:t + 1],
                          ALU.subtract, ALU.mult).then_inc(got["xn"].sem, 1)


def transpose_rows(pe, out, rows, ident, cols=DT):
    for c in range(cols):
        for t in range(TB):
            last = pe.transpose(out[:, c * S + t * P:c * S + (t + 1) * P], rows[:, t, c * P:(c + 1) * P], ident[:, :])
    return last


def layer0(nc, a, g, used):
    with ExitStack() as ctx:
        def sb(name, shape, dt=F32):
            return ctx.enter_context(nc.sbuf_tensor(name, shape, dt))

        def sb2(name, shape, dt=F32):
            return [sb(f"{name}{h}", shape, dt) for h in range(2)]

        def sem(name):
            used.append(ctx.enter_context(nc.semaphore(name)))
            return used[-1]

        def sig(name, per):
            return Signal(sem(name), per)

        def turns(name, per):
            return HalfSignal([sem(f"{name}{h}") for h in range(2)], per)

        dve_own = []
        idle_r = OwnSignal(sem("pool_idle"), 3)

        def own(name, per):
            dve_own.append(OwnSignal(sem(name), per))
            return dve_own[-1]

        def own_turns(name, per):
            dve_own.append(OwnHalfSignal([sem(f"{name}{h}") for h in range(2)], per))
            return dve_own[-1]

        def norm_signals(name):
            return {"stats": own(name + "_stats", TB), "mv": own(name + "_mv", TB), "var": sig(name + "_var", 1),
                    "rstd": sig(name + "_rstd", 1), "xn": sig(name + "_xn", TB), "xt": sig(name + "_xt_psum", 1),
                    "xts": sig(name + "_xt", 1)}

        bank, x_all = g["bank"], g["x_all"]
        identf, identb = g["identf"], g["identb"]

        qv_w = sb("qv_w", [P, DT, 512])
        k_w = sb("k_w", [P, DT, D])
        lin_out_w = sb("lin_out_w", [P, DT, D])
        src_w = sb("src_w", [P, CT, 512])
        tgt_w = sb("tgt_w", [P, DT, D])
        out_w = sb("out_w", [P, 2 * DT, D])
        router_w = sb("router_w", [P, DT, NE])
        lin_b = sb("lin_b", [P, D])
        val_b = sb("val_b", [P, D])
        out_b = sb("out_b", [P, D])
        key_b = sb("key_b", [P, DT])
        tgt_b = sb("tgt_b", [P, DT])
        router_b = sb("router_b", [P, NE])
        before = sb("before", [P, P])
        beforeb = sb("beforeb", [P, P], BF16)
        onesb = sb("onesb", [P, P], BF16)
        idle = sb("idle_a", [P, 6])
        mhalf = sb("mhalf", [P, TB])
        zeros = sb("zeros", [P, 1280])
        expert_ids = sb("expert_ids", [P, 4, NE])

        stats, mv = sb2("stats", [P, TB, 6]), sb2("mv", [P, TB, 2])
        var, rstd = sb2("var", [P, TB]), sb2("rstd", [P, TB])
        xn, xnT = sb2("xn", [P, TB, D]), sb2("xnT", [P, DT * S])
        kE, qE = sb2("kE", [P, DT, S]), sb2("qE", [P, TB, D])
        kmax, ksum = sb2("kmax", [P, DT]), sb2("ksum", [P, DT])
        qmax, qsum = sb2("qmax", [P, TB]), sb2("qsum", [P, TB])
        krec, qrec = sb2("krec", [P, DT]), sb2("qrec", [P, TB])
        v_lin, kN = sb2("v_lin", [P, TB, D]), sb2("kN", [P, TB, D])
        qT, ctxT, kvo = sb2("qT", [P, DT * S]), sb2("ctxT", [P, DT, D]), sb2("kvo", [P, DT, D])
        src = sb2("src", [P, CT, S])
        mask_row, mask_col = sb2("mask_row", [P, S]), sb2("mask_col", [P, TB])
        mask_bias = sb2("mask_bias", [P, S], BF16)
        xk, xq = sb2("xk", [P, DT, S]), sb2("xq", [P, DT, S])
        vb = sb2("vb", [P, TB, D])
        xv = sb2("xv", [P, TB, D])
        smax = sb2("smax", [P, 4, GH])
        nmax = sb2("nmax", [P, 4, GH])
        probs, probsT = sb2("probs", [P, GH, S]), sb2("probsT", [P, 2, 512])
        den = sb2("den", [P, 4, GH])
        updT = sb2("updT", [P, DT * S])
        logit = sb2("logit", [P, TB, NE])
        top, topi = sb2("top", [P, TB, 8]), sb2("topi", [P, TB, 8], U32)
        topf = sb2("topf", [P, TB, 2])
        tope, tsum = sb2("tope", [P, TB, 8]), sb2("tsum", [P, TB])
        ntop = sb2("ntop", [P, TB])
        oneh = sb2("oneh", [P, TB, 2, NE])
        ohb = sb2("ohb", [P, TB, NE], BF16)
        carry = sb("carry", [P, NE])
        taken = sb2("taken", [P, TB, NE])
        posm, pos = sb2("posm", [P, TB, 2, NE]), sb2("pos", [P, TB, 2])
        keep, over = sb2("keep", [P, TB, 2]), sb2("over", [P, TB, 2])
        rowf, posc = sb2("rowf", [P, TB, 2]), sb2("posc", [P, TB, 2])
        slotf = sb2("slotf", [P, TB, 2])
        slot = sb2("slot", [P, 2 * TB], U32)
        wk, ws = sb2("wk", [P, TB, 2]), sb2("ws", [P, TB])

        s_const, s_x, s_cast = sem("layer0_constants_loaded"), sem("x_loaded"), sem("constants_cast")
        s_zero, s_set = sem("zeros_set"), sem("memsets_done")
        src_in = HalfSignal([sem(f"src_loaded{h}") for h in range(2)], 48)
        N1, N2, N3 = norm_signals("n1"), norm_signals("n2"), norm_signals("n3")
        key_psum, qv_psum = sig("key_psum", 1), sig("qv_psum", TB)
        kmax_r, qmax_r = sig("kmax_r", 2), sig("qmax_r", 2)
        kexp, qexp, vlin_r = sig("kexp", DT), sig("qexp", TB), sig("vlin_r", TB)
        kN_psum, kN_r = sig("kN_psum", 1), sig("kN_r", 1)
        qT_psum, qT_r = sig("qT_psum", 1), sig("qT_r", 1)
        ctx_psum, ctx_r = sig("ctx_psum", 1), sig("ctx_r", 1)
        rec_r, kvo_psum, kvo_r = own("rec_r", 3), sig("kvo_psum", 1), sig("kvo_r", DT)
        lin_psum, xb1 = sig("lin_psum", 1), sig("x_plus_lin_bias", 1)
        x1 = own("x1_ready", TB)
        xk_psum, xk_r, xv_psum = sig("xk_psum", 1), sig("xk_r", DT), sig("xv_psum", 1)
        vb_r, xv_r, mb_r = sig("vb_r", 1), sig("xv_r", TB), sig("mask_bias_r", 1)
        xq_psum, xq_r = sig("xq_psum", 1), sig("xq_r", DT)
        sc_psum, smax_r, nmax_r = turns("scores_psum", 4), own_turns("smax_r", 4), turns("nmax_r", 4)
        pexp, pT_psum, pT_a, pT_v = turns("pexp", 4 * GH), turns("probsT_psum", 4), turns("probsT_act", 4), turns("probsT_dve", 4)
        den_r, pnorm = own_turns("den_r", 4), turns("probs_normed", 4)
        updT_psum, updT_r = sig("updT_psum", 1), sig("updT_r", 1)
        xb2, xo_psum, x2 = sig("x_plus_out_bias", 1), sig("xout_psum", 1), own("x2_ready", TB)
        lg_psum, lg_r, top_r, topi_r = sig("logit_psum", 1), own("logit_r", 1), own("top_r", TB), own("topi_r", TB)
        topf_r, oh_r, ohb_r = own("topf_r", 2), own("oneh_r", 2 * TB), sig("ohb_r", 1)
        cnt_psum, taken_r, carry_r = sig("count_psum", 1), own("taken_r", 1), own("carry_r", 1)
        posm_r, pos_r, route_r = own("posm_r", 2), own("pos_r", 1), own("route_r", 8)
        texp, slot_r, ntop_r = sig("texp", TB), sig("slot_r", 1), sig("ntop_r", 1)
        sent = g["sent"]
        wgt_r = own("weights_r", 5)

        block = ctx.enter_context(nc.Block())

        def load(eng, out, src_ap, s, bc=False):
            eng.dma_start(out, src_ap.partition_broadcast(P) if bc else src_ap).then_inc(s, 16)

        KT = "(c p) n -> p c n"
        const_loads = [
            (qv_w[:, :, 0:D], a["L0_attn_Wq"].rearrange(KT, p=P)), (qv_w[:, :, D:2 * D], a["L0_attn_Wv"].rearrange(KT, p=P)),
            (k_w[:, :, :], a["L0_attn_Wk"].rearrange(KT, p=P)), (lin_out_w[:, :, :], a["L0_attn_Wo"].rearrange(KT, p=P)),
            (src_w[:, :, :], a["L0_xattn_W_srcT"].rearrange(KT, p=P)), (tgt_w[:, :, :], a["L0_xattn_W_tgtT"].rearrange(KT, p=P)),
            (out_w[:, :, :], a["L0_xattn_W_outT"].rearrange(KT, p=P)), (router_w[:, :, :], a["L0_ffn_w_router"].rearrange(KT, p=P)),
            (lin_b[:, :], a["L0_attn_bo"].partition_broadcast(P)), (val_b[:, :], a["L0_xattn_b_src"][D:2 * D].partition_broadcast(P)),
            (out_b[:, :], a["L0_xattn_b_out"].partition_broadcast(P)), (router_b[:, :], a["L0_ffn_b_router"].partition_broadcast(P)),
            (key_b[:, :], a["L0_xattn_b_srcC"][:, 0:DT]), (tgt_b[:, :], a["L0_xattn_b_tgtC"]),
            (before[:, :], a["c_before"]), (identf[:, :], a["c_ident"]),
        ]
        layer1_loads = [
            (g["qkv_w"][:, :, 0:D], a["L1_attn_Wq"].rearrange(KT, p=P)), (g["qkv_w"][:, :, D:2 * D], a["L1_attn_Wk"].rearrange(KT, p=P)),
            (g["qkv_w"][:, :, 2 * D:3 * D], a["L1_attn_Wv"].rearrange(KT, p=P)), (g["attn_out_w"][:, :, :], a["L1_attn_Wo"].rearrange(KT, p=P)),
            (g["win_w"][:, :, :], a["L1_xattn_W_inT"].rearrange(KT, p=P)), (g["gate_w"][:, :, :], a["L1_ffn_gate_wT"].rearrange(KT, p=P)),
            (g["rope_cos"][:, :, :], a["c_cos"].rearrange("(t p) n -> p t n", p=P)),
            (g["rope_sin"][:, :, :], a["c_sin"].rearrange("(t p) n -> p t n", p=P)),
            (g["b_in"][:, :], a["L1_xattn_b_in"].partition_broadcast(P)), (g["gate_b"][:, :], a["L1_ffn_gate_b"].partition_broadcast(P)),
            (g["g_res"][:, :], a["L1_xattn_g_resC"]), (g["expert_b"][:, :, :], a["L1_ffn_expert_bC"]),
            (g["expert_w"][:, :, :], a["L1_ffn_expert_wT"].rearrange(KT, p=P)),
        ]
        g["n_l1"] = 16 * len(layer1_loads)
        n_const = 16 * len(const_loads)
        x_tiles = a["x"].rearrange("(t p) d -> p t d", p=P)
        slots = g["slots"]

        @block.sync
        def _(sp):
            def load_src(n, h):
                sp.dma_start(src[h][:, :, :], a["ctxT"][bass.ds(n * DC, DC), :].rearrange("(c p) s -> p c s", p=P)).then_inc(src_in.sems[h], 16)
                sp.dma_start(mask_row[h][:, :], a["mask"][bass.ds(n * S, S)].partition_broadcast(P)).then_inc(src_in.sems[h], 16)
                sp.dma_start(mask_col[h][:, :], a["maskC"][:, bass.ds(n * TB, TB)]).then_inc(src_in.sems[h], 16)

            sp.dma_start(x_all[:, 0:4, :], x_tiles[:, 0:4, :]).then_inc(s_x, 16)
            for out, src_ap in const_loads[:8]:
                sp.dma_start(out, src_ap).then_inc(s_const, 16)
            for h in range(2):
                load_src(h, h)
            with sp.Fori(0, PAIRS - 1) as i:
                for h in range(2):
                    sp.wait_ge(*xq_r((i, h)))
                    sp.wait_ge(*xv_r((i, h)))
                    sp.wait_ge(*mb_r((i, h)))
                    load_src(i * 2 + (h + 2), h)

        @block.gpsimd
        def _(pool):
            pool.memset(zeros[:, :], 0.0).then_inc(s_zero, 1)
            pool.memset(mhalf[:, :], -0.5).then_inc(s_set, 1)
            pool.memset(onesb[:, :], 1.0).then_inc(s_set, 1)
            pool.memset(carry[:, :], 0.0).then_inc(s_set, 1)
            pool.iota(expert_ids[:, :, :], [[0, 4], [1, NE]], base=0, channel_multiplier=0,
                      allow_small_or_imprecise_dtypes=True).then_inc(s_set, 1)
            pool.wait_ge(s_zero, 1)
            for q in range(4):
                pool.dma_start(slots[q * 5 * P:(q + 1) * 5 * P, :].rearrange("(p r) d -> p (r d)", p=P),
                               zeros[:, :]).then_inc(sent.sems[q % 2], 16)
            pool.wait_ge(s_set, 4)
            pool.wait_ge(s_const, n_const)
            pool.wait_ge(s_x, 64)

            def power(N, b):
                pool.wait_ge(*N["var"](b))
                pool.tensor_tensor(rstd[b[1]][:, :], var[b[1]][:, :], mhalf[:, :], ALU.pow).then_inc(N["rstd"].sem, 1)

            with pool.Fori(0, PAIRS) as i:
                B = [(i, 0), (i, 1)]
                for b in B:
                    power(N1, b)
                for b in B:
                    x = x_all[:, bass.ds(tile_of(b), TB), :]
                    pool.wait_ge(*N1["xn"](b))
                    pool.tensor_tensor(idle[:, 2 * 0 + b[1]:2 * 0 + b[1] + 1], mhalf[:, 0:1], mhalf[:, 0:1], ALU.add).then_inc(idle_r.sem, 1)
                    pool.tensor_tensor(x, x, lin_b[:, :].unsqueeze(1).broadcast_to([P, TB, D]), ALU.add).then_inc(xb1.sem, 1)
                for b in B:
                    power(N2, b)
                for b in B:
                    h = b[1]
                    pool.wait_ge(*vb_r(b))
                    pool.wait_ge(*src_in(b))
                    for t in range(TB):
                        pool.tensor_tensor(xv[h][:, t, :], vb[h][:, t, :], mask_col[h][:, t:t + 1].broadcast_to([P, D]),
                                           ALU.mult).then_inc(xv_r.sem, 1)
                for b in B:
                    x = x_all[:, bass.ds(tile_of(b), TB), :]
                    pool.wait_ge(*N2["xn"](b))
                    pool.tensor_tensor(idle[:, 2 * 1 + b[1]:2 * 1 + b[1] + 1], mhalf[:, 0:1], mhalf[:, 0:1], ALU.add).then_inc(idle_r.sem, 1)
                    pool.tensor_tensor(x, x, out_b[:, :].unsqueeze(1).broadcast_to([P, TB, D]), ALU.add).then_inc(xb2.sem, 1)
                for b in B:
                    power(N3, b)
                for b in B:
                    h = b[1]
                    pool.wait_ge(*slot_r(b))
                    pool.wait_ge(sent.sems[0], sent.first)
                    pool.wait_ge(sent.sems[1], sent.first)
                    pool.tensor_tensor(idle[:, 2 * 2 + b[1]:2 * 2 + b[1] + 1], mhalf[:, 0:1], mhalf[:, 0:1], ALU.add).then_inc(idle_r.sem, 1)
                    for t in range(TB):
                        for k in range(2):
                            pool.indirect_dma_start(
                                out=slots, out_offset=bass.IndirectOffsetOnAxis(ap=slot[h][:, 2 * t + k:2 * t + k + 1], axis=0),
                                in_=xn[h][:, t, :], in_offset=None, bounds_check=NE * CAP - 1, oob_is_err=False,
                            ).then_inc(sent.sems[h], 16)
                finish(pool, [idle_r])
            for h in range(2):
                pool.wait_ge(*sent((PAIRS - 1, h)))

        @block.scalar
        def _(act):
            for q in range(1, 4):
                act.dma_start(x_all[:, 4 * q:4 * q + 4, :], x_tiles[:, 4 * q:4 * q + 4, :]).then_inc(s_x, 16)
            for out, src_ap in const_loads[8:]:
                act.dma_start(out, src_ap).then_inc(s_const, 16)
            act.wait_ge(s_const, n_const)
            act.activation(identb[:, :], identf[:, :], ACT.Copy).then_inc(s_cast, 1)
            act.activation(beforeb[:, :], before[:, :], ACT.Copy).then_inc(s_cast, 1)
            for out, src_ap in layer1_loads:
                act.dma_start(out, src_ap).then_inc(g["s_l1"], 16)

            def evac(out, psum, waits, done):
                for w in waits:
                    act.wait_ge(*w)
                act.activation(out, psum, ACT.Copy).then_inc(done, 1)

            with act.Fori(0, PAIRS) as i:
                B = [(i, 0), (i, 1)]
                for b in B:
                    evac(xnT[b[1]][:, :], bank[b[1]][0][:, :], [N1["xt"](b)], N1["xts"].sem)
                for b in B:
                    h = b[1]
                    act.wait_ge(*kmax_r(b))
                    for c in range(DT):
                        act.activation(kE[h][:, c, :], bank[h][1][:, c * S:(c + 1) * S], ACT.Exp, bias=kmax[h][:, c:c + 1],
                                       accum_out=ksum[h][:, c:c + 1]).then_inc(kexp.sem, 1)
                for b in B:
                    h = b[1]
                    act.wait_ge(*qmax_r(b))
                    for t in range(TB):
                        act.activation(qE[h][:, t, :], bank[h][2 + t][:, 0:D], ACT.Exp, bias=qmax[h][:, t:t + 1],
                                       accum_out=qsum[h][:, t:t + 1]).then_inc(qexp.sem, 1)
                    for t in range(TB):
                        act.activation(v_lin[h][:, t, :], bank[h][2 + t][:, D:2 * D], ACT.Copy).then_inc(vlin_r.sem, 1)
                for b in B:
                    evac(qT[b[1]][:, :], bank[b[1]][0][:, :], [qT_psum(b)], qT_r.sem)
                for b in B:
                    evac(ctxT[b[1]][:, :, :].rearrange("p a c -> p (a c)"), bank[b[1]][2][:, :], [ctx_psum(b)], ctx_r.sem)
                for b in B:
                    evac(xnT[b[1]][:, :], bank[b[1]][2][:, :], [N2["xt"](b)], N2["xts"].sem)

                def exps(b, ch):
                    h = b[1]
                    act.wait_ge(*nmax_r(b, ch + 1))
                    for j in range(GH):
                        act.activation(probs[h][:, j, :], bank[h][j // 2][:, (j % 2) * S:(j % 2 + 1) * S], ACT.Exp,
                                       bias=nmax[h][:, ch, j:j + 1], scale=XD ** -0.5, accum_out=den[h][:, ch, j:j + 1]).then_inc(pexp.sems[h], 1)

                steps = [(b, ch) for ch in range(4) for b in B]
                exps(*steps[0])
                for n, (b, ch) in enumerate(steps):
                    evac(probsT[b[1]][:, 0, :], bank[b[1]][0][:, :], [pT_psum(b, ch + 1)], pT_a.sems[b[1]])
                    if n + 1 < len(steps):
                        exps(*steps[n + 1])
                for b in B:
                    evac(updT[b[1]][:, :], bank[b[1]][2][:, :], [updT_psum(b)], updT_r.sem)
                for b in B:
                    evac(xnT[b[1]][:, :], bank[b[1]][0][:, :], [N3["xt"](b)], N3["xts"].sem)
                for b in B:
                    h = b[1]
                    act.wait_ge(*ntop_r(b))
                    for t in range(TB):
                        act.activation(tope[h][:, t, :], top[h][:, t, :], ACT.Exp, bias=ntop[h][:, t:t + 1],
                                       accum_out=tsum[h][:, t:t + 1]).then_inc(texp.sem, 1)

        @block.tensor
        def _(pe):
            pe.wait_ge(s_const, n_const)
            pe.wait_ge(s_cast, 2)
            pe.wait_ge(s_set, 4)
            with pe.Fori(0, PAIRS) as i:
                B = [(i, 0), (i, 1)]
                for b in B:
                    pe.wait_ge(*N1["xn"](b))
                    transpose_rows(pe, bank[b[1]][0], xn[b[1]], identf).then_inc(N1["xt"].sem, 1)
                for b in B:
                    h = b[1]
                    pe.wait_ge(*N1["xts"](b))
                    for c in range(DT):
                        for k in range(DT):
                            last = pe.matmul(bank[h][1][:, c * S:(c + 1) * S], k_w[:, k, c * P:(c + 1) * P],
                                             xnT[h][:, k * S:(k + 1) * S], start=(k == 0), stop=(k == DT - 1))
                    last.then_inc(key_psum.sem, 1)
                    for t in range(TB):
                        for k in range(DT):
                            last = pe.matmul(bank[h][2 + t][:, :], xnT[h][:, k * S + t * P:k * S + (t + 1) * P],
                                             qv_w[:, k, :], start=(k == 0), stop=(k == DT - 1))
                        last.then_inc(qv_psum.sem, 1)
                for b in B:
                    h = b[1]
                    pe.wait_ge(*kexp(b))
                    for t in range(TB):
                        for c in range(DT):
                            last = pe.transpose(bank[h][1][:, t * D + c * P:t * D + (c + 1) * P],
                                                kE[h][:, c, t * P:(t + 1) * P], identf[:, :])
                    last.then_inc(kN_psum.sem, 1)
                for b in B:
                    pe.wait_ge(*qexp(b))
                    transpose_rows(pe, bank[b[1]][0], qE[b[1]], identf).then_inc(qT_psum.sem, 1)
                for b in B:
                    h = b[1]
                    pe.wait_ge(*kN_r(b))
                    pe.wait_ge(*vlin_r(b))
                    for e in range(DT):
                        for t in range(TB):
                            last = pe.matmul(bank[h][2][:, e * D:(e + 1) * D], v_lin[h][:, t, e * P:(e + 1) * P], kN[h][:, t, :],
                                             start=(t == 0), stop=(t == TB - 1))
                    last.then_inc(ctx_psum.sem, 1)
                for b in B:
                    h = b[1]
                    pe.wait_ge(*ctx_r(b))
                    for d in range(DT):
                        for e in range(DT):
                            last = pe.matmul(bank[h][3][:, d * D:(d + 1) * D], ctxT[h][:, e, d * P:(d + 1) * P], lin_out_w[:, e, :],
                                             start=(e == 0), stop=(e == DT - 1))
                    last.then_inc(kvo_psum.sem, 1)
                for b in B:
                    h = b[1]
                    pe.wait_ge(*kvo_r(b))
                    pe.wait_ge(*qT_r(b))
                    for t in range(TB):
                        for d in range(DT):
                            last = pe.matmul(bank[h][1][:, t * D:(t + 1) * D], qT[h][:, d * S + t * P:d * S + (t + 1) * P],
                                             kvo[h][:, d, :], start=(d == 0), stop=(d == DT - 1))
                    last.then_inc(lin_psum.sem, 1)
                for b in B:
                    h = b[1]
                    pe.wait_ge(*src_in(b))
                    for c in range(DT):
                        for k in range(CT):
                            last = pe.matmul(bank[h][0][:, c * S:(c + 1) * S], src_w[:, k, c * P:(c + 1) * P], src[h][:, k, :],
                                             start=(k == 0), stop=(k == CT - 1))
                    last.then_inc(xk_psum.sem, 1)
                    for t in range(TB):
                        for k in range(CT):
                            last = pe.matmul(bank[h][3][:, t * D:(t + 1) * D], src[h][:, k, t * P:(t + 1) * P], src_w[:, k, D:2 * D],
                                             start=(k == 0), stop=(k == CT - 1))
                    last.then_inc(xv_psum.sem, 1)
                for b in B:
                    pe.wait_ge(*N2["xn"](b))
                    transpose_rows(pe, bank[b[1]][2], xn[b[1]], identf).then_inc(N2["xt"].sem, 1)
                for b in B:
                    h = b[1]
                    pe.wait_ge(*N2["xts"](b))
                    for c in range(DT):
                        for k in range(DT):
                            last = pe.matmul(bank[h][1][:, c * S:(c + 1) * S], tgt_w[:, k, c * P:(c + 1) * P],
                                             xnT[h][:, k * S:(k + 1) * S], start=(k == 0), stop=(k == DT - 1))
                    last.then_inc(xq_psum.sem, 1)

                def head(c, j):
                    return j % 2 * (P // XD) + 2 * c + j // 2

                def scores(b, ch):
                    h, t, c = b[1], ch // 2, ch % 2
                    if ch == 0:
                        pe.wait_ge(*mb_r(b))
                        pe.wait_ge(*xk_r(b))
                        pe.wait_ge(*xq_r(b))
                    else:
                        pe.wait_ge(*pT_a(b, ch))
                        pe.wait_ge(*pT_v(b, ch))
                    for j in range(GH):
                        f, r = divmod(head(c, j), P // XD)
                        r0 = XD * r
                        o = bank[h][j // 2][:, (j % 2) * S:(j % 2 + 1) * S]
                        pe.matmul(o, onesb[r0:r0 + 1, :], mask_bias[h][r0:r0 + 1, :], start=True, stop=False)
                        last = pe.matmul(o, xq[h][r0:r0 + XD, f, t * P:(t + 1) * P], xk[h][r0:r0 + XD, f, :],
                                         start=False, stop=True)
                    last.then_inc(sc_psum.sems[h], 1)

                def turn(b, ch):
                    h = b[1]
                    pe.wait_ge(*pnorm(b, ch + 1))
                    for j in range(GH):
                        for s in range(TB):
                            last = pe.transpose(bank[h][j // 2][:, ((j % 2) * TB + s) * P:((j % 2) * TB + s + 1) * P],
                                                probs[h][:, j, s * P:(s + 1) * P], identf[:, :])
                    last.then_inc(pT_psum.sems[h], 1)

                def values(b, ch):
                    h, t, c = b[1], ch // 2, ch % 2
                    pe.wait_ge(*pT_a(b, ch + 1))
                    pe.wait_ge(*pT_v(b, ch + 1))
                    if ch == 0:
                        pe.wait_ge(*xv_r(b))
                    for j, s in [(j, s) for first in (0, 1) for s in range(TB) for j in (first, first + 2)]:
                        hd = head(c, j)
                        f, r = divmod(hd, P // XD)
                        last = pe.matmul(bank[h][2][XD * r:XD * (r + 1), f * S + t * P:f * S + (t + 1) * P],
                                         xv[h][:, s, hd * XD:(hd + 1) * XD],
                                         probsT[h][:, j // 2, ((j % 2) * TB + s) * P:((j % 2) * TB + s + 1) * P],
                                         start=(s == 0), stop=(s == TB - 1))
                    if ch == 3:
                        last.then_inc(updT_psum.sem, 1)

                steps = [(b, ch) for ch in range(4) for b in B]
                scores(*steps[0])
                scores(*steps[1])
                for n, (b, ch) in enumerate(steps):
                    turn(b, ch)
                    if n:
                        values(*steps[n - 1])
                    if ch < 3:
                        scores(b, ch + 1)
                values(*steps[-1])
                for b in B:
                    h = b[1]
                    pe.wait_ge(*updT_r(b))
                    for t in range(TB):
                        for k in range(2 * DT):
                            left = (xnT if k < DT else updT)[h]
                            last = pe.matmul(bank[h][1][:, t * D:(t + 1) * D], left[:, (k % DT) * S + t * P:(k % DT) * S + (t + 1) * P],
                                             out_w[:, k, :], start=(k == 0), stop=(k == 2 * DT - 1))
                    last.then_inc(xo_psum.sem, 1)
                for b in B:
                    pe.wait_ge(*N3["xn"](b))
                    transpose_rows(pe, bank[b[1]][0], xn[b[1]], identf).then_inc(N3["xt"].sem, 1)
                for b in B:
                    h = b[1]
                    pe.wait_ge(*N3["xts"](b))
                    for t in range(TB):
                        for k in range(DT):
                            last = pe.matmul(bank[h][2][:, t * NE:(t + 1) * NE], xnT[h][:, k * S + t * P:k * S + (t + 1) * P],
                                             router_w[:, k, :], start=(k == 0), stop=(k == DT - 1))
                    last.then_inc(lg_psum.sem, 1)
                for b in B:
                    h = b[1]
                    o = bank[h][3]
                    pe.wait_ge(*ohb_r(b))
                    pe.matmul(o[:, 0:NE], beforeb[:, :], ohb[h][:, 0, :], start=True, stop=True)
                    pe.matmul(o[:, NE:2 * NE], onesb[:, :], ohb[h][:, 0, :], start=True, stop=False)
                    pe.matmul(o[:, NE:2 * NE], beforeb[:, :], ohb[h][:, 1, :], start=False, stop=True)
                    pe.matmul(o[:, 2 * NE:3 * NE], onesb[:, :], ohb[h][:, 0, :], start=True, stop=False)
                    pe.matmul(o[:, 2 * NE:3 * NE], onesb[:, :], ohb[h][:, 1, :], start=False, stop=True).then_inc(cnt_psum.sem, 1)

        @block.vector
        def _(dve):
            dve.wait_ge(s_x, 64)
            dve.wait_ge(s_const, n_const)
            dve.wait_ge(s_set, 4)
            with dve.Fori(0, PAIRS) as i:
                B = [(i, 0), (i, 1)]

                def xt(b):
                    return lambda t: x_all[:, bass.ds(tile_of(b) + t, 1), :].rearrange("p a d -> p (a d)")

                for b in B:
                    norm_stats(dve, xt(b), stats, mv, var, N1, b)
                for b in B:
                    dve.wait_ge(*sent(b, 0))
                    norm_apply(dve, xt(b), xn, mv, rstd, N1, b)
                for b in B:
                    h = b[1]
                    dve.wait_ge(*key_psum(b))
                    dve.tensor_reduce(kmax[h][:, :], bank[h][1][:, :].rearrange("p (c s) -> p c s", c=DT), X, ALU.max, negate=True).then_inc(kmax_r.sem, 2)
                for b in B:
                    h = b[1]
                    for t in range(TB):
                        dve.wait_ge(*qv_psum(b, t + 1))
                        dve.tensor_reduce(qmax[h][:, t:t + 1], bank[h][2 + t][:, 0:D], X, ALU.max, negate=True).then_inc(qmax_r.sem, 1)
                for b in B:
                    h = b[1]
                    dve.wait_ge(*kN_psum(b))
                    dve.tensor_copy(kN[h][:, :, :].rearrange("p t d -> p (t d)"), bank[h][1][:, :]).then_inc(kN_r.sem, 1)
                    dve.wait_ge(*qexp(b))
                    dve.reciprocal(krec[h][:, :], ksum[h][:, :]).then_inc(rec_r.sem, 1)
                    dve.reciprocal(qrec[h][:, :], qsum[h][:, :]).then_inc(rec_r.sem, 1)
                    dve.wait_ge(*rec_r(b, 2))
                    dve.tensor_scalar(qrec[h][:, :], qrec[h][:, :], 0.25 / D, None, ALU.mult).then_inc(rec_r.sem, 1)
                for b in B:
                    h = b[1]
                    dve.wait_ge(*kvo_psum(b))
                    for d in range(DT):
                        dve.tensor_scalar(kvo[h][:, d, :], bank[h][3][:, d * D:(d + 1) * D], krec[h][:, d:d + 1], None,
                                          ALU.mult).then_inc(kvo_r.sem, 1)
                for b in B:
                    h = b[1]
                    dve.wait_ge(*src_in(b))
                    dve.tensor_scalar(mask_bias[h][:, :], mask_row[h][:, :], 0.0, NEG, ALU.is_equal, ALU.mult).then_inc(mb_r.sem, 1)
                for b in B:
                    h = b[1]
                    dve.wait_ge(*lin_psum(b))
                    dve.wait_ge(*xb1(b))
                    dve.wait_ge(*rec_r(b))
                    for t in range(TB):
                        dve.scalar_tensor_tensor(xt(b)(t), bank[h][1][:, t * D:(t + 1) * D], qrec[h][:, t:t + 1], xt(b)(t),
                                                 ALU.mult, ALU.add).then_inc(x1.sem, 1)
                for b in B:
                    dve.wait_ge(*x1(b))
                    norm_stats(dve, xt(b), stats, mv, var, N2, b)
                for b in B:
                    norm_apply(dve, xt(b), xn, mv, rstd, N2, b)
                for b in B:
                    h = b[1]
                    dve.wait_ge(*xk_psum(b))
                    for c in range(DT):
                        dve.scalar_tensor_tensor(xk[h][:, c, :], bank[h][0][:, c * S:(c + 1) * S], key_b[:, c:c + 1], mask_row[h][:, :],
                                                 ALU.add, ALU.mult).then_inc(xk_r.sem, 1)
                    dve.wait_ge(*xv_psum(b))
                    dve.tensor_tensor(vb[h][:, :, :], bank[h][3][:, :].rearrange("p (t d) -> p t d", t=TB),
                                      val_b[:, :].unsqueeze(1).broadcast_to([P, TB, D]), ALU.add).then_inc(vb_r.sem, 1)
                for b in B:
                    h = b[1]
                    dve.wait_ge(*xq_psum(b))
                    for c in range(DT):
                        dve.scalar_tensor_tensor(xq[h][:, c, :], bank[h][1][:, c * S:(c + 1) * S], tgt_b[:, c:c + 1], mask_row[h][:, :],
                                                 ALU.add, ALU.mult).then_inc(xq_r.sem, 1)

                def maxima(b, ch):
                    h = b[1]
                    dve.wait_ge(*sc_psum(b, ch + 1))
                    for q in range(2):
                        last = dve.tensor_reduce(smax[h][:, ch, 2 * q:2 * q + 2], bank[h][q][:, :].rearrange("p (c s) -> p c s", c=2), X, ALU.max)
                    last.then_inc(smax_r.sems[h], 1)
                    dve.wait_ge(*smax_r(b, ch + 1))
                    dve.tensor_scalar(nmax[h][:, ch, :], smax[h][:, ch, :], -XD ** -0.5, None, ALU.mult).then_inc(nmax_r.sems[h], 1)

                def normed(b, ch):
                    h = b[1]
                    dve.wait_ge(*pexp(b, GH * (ch + 1)))
                    dve.reciprocal(den[h][:, ch, :], den[h][:, ch, :]).then_inc(den_r.sems[h], 1)
                    dve.wait_ge(*den_r(b, ch + 1))
                    for j in range(GH):
                        last = dve.tensor_scalar(probs[h][:, j, :], probs[h][:, j, :], den[h][:, ch, j:j + 1], None, ALU.mult)
                    last.then_inc(pnorm.sems[h], 1)

                steps = [(b, ch) for ch in range(4) for b in B]
                maxima(*steps[0])
                normed(*steps[0])
                for n, (b, ch) in enumerate(steps):
                    h = b[1]
                    if n + 1 < len(steps):
                        maxima(*steps[n + 1])
                    dve.wait_ge(*pT_psum(b, ch + 1))
                    dve.tensor_copy(probsT[h][:, 1, :], bank[h][1][:, :]).then_inc(pT_v.sems[h], 1)
                    if n + 1 < len(steps):
                        normed(*steps[n + 1])
                for b in B:
                    h = b[1]
                    dve.wait_ge(*xo_psum(b))
                    dve.wait_ge(*xb2(b))
                    x = x_all[:, bass.ds(tile_of(b), TB), :]
                    dve.tensor_tensor(x, bank[h][1][:, :].rearrange("p (t d) -> p t d", t=TB), x, ALU.add).then_inc(x2.sem, TB)
                for b in B:
                    dve.wait_ge(*x2(b))
                    norm_stats(dve, xt(b), stats, mv, var, N3, b)
                for b in B:
                    h = b[1]
                    norm_apply(dve, xt(b), xn, mv, rstd, N3, b)
                for b in B:
                    h = b[1]
                    dve.wait_ge(*lg_psum(b))
                    dve.tensor_tensor(logit[h][:, :, :], bank[h][2][:, 0:TB * NE].rearrange("p (t e) -> p t e", t=TB),
                                      router_b[:, :].unsqueeze(1).broadcast_to([P, TB, NE]), ALU.add).then_inc(lg_r.sem, 1)
                    dve.wait_ge(*lg_r(b))
                    for t in range(TB):
                        dve.max(top[h][:, t, :], logit[h][:, t, :]).then_inc(top_r.sem, 1)
                    dve.wait_ge(*top_r(b))
                    for t in range(TB):
                        dve.max_index(topi[h][:, t, :], top[h][:, t, :], logit[h][:, t, :]).then_inc(topi_r.sem, 1)
                    dve.tensor_scalar(ntop[h][:, :], top[h][:, :, 0], -1.0, None, ALU.mult).then_inc(ntop_r.sem, 1)
                    dve.wait_ge(*topi_r(b))
                    dve.tensor_copy(topf[h][:, :, :], topi[h][:, :, 0:2]).then_inc(topf_r.sem, 2)
                    dve.wait_ge(*topf_r(b))
                    for t in range(TB):
                        for k in range(2):
                            dve.tensor_scalar(oneh[h][:, t, k, :], expert_ids[:, 0, :], topf[h][:, t, k:k + 1], None,
                                              ALU.is_equal).then_inc(oh_r.sem, 1)
                    dve.wait_ge(*oh_r(b))
                    dve.tensor_tensor(ohb[h][:, :, :], oneh[h][:, :, 0, :], oneh[h][:, :, 1, :], ALU.add).then_inc(ohb_r.sem, 1)
                for b in B:
                    h = b[1]
                    dve.wait_ge(*cnt_psum(b))
                    dve.tensor_tensor(taken[h][:, :, :], bank[h][3][:, 0:TB * NE].rearrange("p (t e) -> p t e", t=TB),
                                      carry[:, :].unsqueeze(1).broadcast_to([P, TB, NE]), ALU.add).then_inc(taken_r.sem, 1)
                    dve.wait_ge(*taken_r(b))
                    dve.tensor_tensor(carry[:, :], carry[:, :], bank[h][3][:, 2 * NE:3 * NE], ALU.add).then_inc(carry_r.sem, 1)
                    for t in range(TB):
                        dve.tensor_tensor(posm[h][:, t, :, :], oneh[h][:, t, :, :], taken[h][:, t, :].unsqueeze(1).broadcast_to([P, 2, NE]),
                                          ALU.mult).then_inc(posm_r.sem, 1)
                    dve.wait_ge(*posm_r(b))
                    dve.tensor_reduce(pos[h][:, :, :], posm[h][:, :, :, :], X, ALU.add).then_inc(pos_r.sem, 1)
                    dve.wait_ge(*pos_r(b))
                    dve.wait_ge(*carry_r(b))
                    dve.tensor_scalar(keep[h][:, :, :], pos[h][:, :, :], float(CAP), None, ALU.is_lt).then_inc(route_r.sem, 1)
                    dve.tensor_scalar(over[h][:, :, :], pos[h][:, :, :], float(CAP), 4.0 * NE * CAP, ALU.is_ge, ALU.mult).then_inc(route_r.sem, 1)
                    dve.tensor_scalar(posc[h][:, :, :], pos[h][:, :, :], float(CAP - 1), None, ALU.min).then_inc(route_r.sem, 1)
                    dve.wait_ge(*route_r(b, 3))
                    dve.scalar_tensor_tensor(rowf[h][:, :, :], topf[h][:, :, :], float(CAP), posc[h][:, :, :], ALU.mult, ALU.add).then_inc(route_r.sem, 1)
                    dve.wait_ge(*route_r(b, 4))
                    dve.tensor_tensor(slotf[h][:, :, :], rowf[h][:, :, :], over[h][:, :, :], ALU.add).then_inc(route_r.sem, 1)
                    dve.wait_ge(*route_r(b, 5))
                    dve.tensor_copy(slot[h][:, :], slotf[h][:, :, :].rearrange("p t k -> p (t k)")).then_inc(slot_r.sem, 1)
                    dve.tensor_copy(g["choice_row"][:, bass.ds(tile_of(b), TB), :], rowf[h][:, :, :]).then_inc(route_r.sem, 1)
                    dve.wait_ge(*texp(b))
                    dve.reciprocal(ws[h][:, :], tsum[h][:, :]).then_inc(wgt_r.sem, 1)
                    dve.tensor_tensor(wk[h][:, :, :], tope[h][:, :, 0:2], keep[h][:, :, :], ALU.mult).then_inc(wgt_r.sem, 1)
                    dve.wait_ge(*wgt_r(b, 2))
                    dve.tensor_tensor(wk[h][:, :, :], wk[h][:, :, :], ws[h][:, :].unsqueeze(2).broadcast_to([P, TB, 2]), ALU.mult).then_inc(wgt_r.sem, 1)
                    dve.wait_ge(*wgt_r(b, 3))
                    dve.tensor_reduce(ws[h][:, :], wk[h][:, :, :], X, ALU.add).then_inc(wgt_r.sem, 1)
                    dve.wait_ge(*wgt_r(b, 4))
                    dve.tensor_scalar(ws[h][:, :], ws[h][:, :], 1e-6, None, ALU.max).then_inc(wgt_r.sem, 1)
                    dve.wait_ge(*wgt_r(b, 5))
                    dve.reciprocal(ws[h][:, :], ws[h][:, :]).then_inc(route_r.sem, 1)
                    dve.wait_ge(*route_r(b, 7))
                    dve.tensor_tensor(g["choice_w"][:, bass.ds(tile_of(b), TB), :], wk[h][:, :, :],
                                      ws[h][:, :].unsqueeze(2).broadcast_to([P, TB, 2]), ALU.mult).then_inc(route_r.sem, 1)
                finish(dve, dve_own)


def experts(nc, a, g, used):
    with ExitStack() as ctx:
        def sb(name, shape, dt=F32):
            return ctx.enter_context(nc.sbuf_tensor(name, shape, dt))

        def sb2(name, shape, dt=F32):
            return [sb(f"{name}{h}", shape, dt) for h in range(2)]

        def sem(name):
            used.append(ctx.enter_context(nc.semaphore(name)))
            return used[-1]

        def sig(name, per):
            return Signal(sem(name), per)

        def turns(name, per):
            return HalfSignal([sem(f"{name}{h}") for h in range(2)], per)

        bank, identf = g["bank"], g["identf"]
        w1, w2 = sb2("w1", [P, DT, F]), sb2("w2", [P, FT, D])
        b1, b2 = sb2("b1", [P, FT]), sb2("b2", [P, D])
        rows, rowsT = sb2("rows", [P, len(SLOTS), D]), sb2("rowsT", [P, DT, CAP])
        hid, outr = sb2("hid", [P, FT, CAP]), sb2("outr", [P, len(SLOTS), D])
        decayT, upto = sb("decayT", [P, TB, S]), sb("upto", [P, TB, S])
        uptob, ones = sb("uptob", [P, TB, S], BF16), sb("ones", [P, P])
        place, zero = sb("place", [P, TB]), sb("zero", [P, S])
        g_init, mhalf = sb("g_init", [P, D]), sb("mhalf_m", [P, TB])
        lens = sb2("lens", [P, S], I32)
        patch, square = sb2("patch", [P, TB, DC]), sb2("square", [P, TB, DC])
        lensf, ends, wrap = sb2("lensf", [P, S]), sb2("ends", [P, S]), sb2("wrap", [P, S])
        hit, hits = sb2("hit", [P, TB, S]), sb2("hits", [P, TB])
        edge = sb2("edge", [P, TB, P], BF16)
        plug, pick = sb2("plug", [P, S]), sb2("pick", [P, TB, S])
        ssum, msq, rrms = sb2("ssum", [P, TB]), sb2("msq", [P, TB]), sb2("rrms", [P, TB])
        u, state = sb2("u", [P, TB, D]), sb2("state", [P, TB, D])

        s_const, s_set, s_cast = sem("experts_constants_loaded"), sem("m_memsets_done"), sem("m_cast")
        w1_in = HalfSignal([sem(f"rows_and_w1_loaded{h}") for h in range(2)], 64)
        w2_in = HalfSignal([sem(f"w2_loaded{h}") for h in range(2)], 32)
        p_in = g["p_in"]
        out_sent = HalfSignal([sem(f"expert_rows_stored{h}") for h in range(2)], 32, 1)
        rt_psum, rt_r = sig("rowsT_psum", 1), sig("rowsT_r", DT)
        h_psum, h_r = turns("hidden_psum", FT), turns("hidden_r", FT)
        o_psum, o_r = sig("expert_out_psum", 3), sig("expert_out_r", 3)
        sq_r, ms_r, rr_r, u_r = sig("square_r", TB), sig("msq_r", 1), sig("rrms_r", 1), sig("u_r", TB)
        ends_r, hit_r, edge_r = sig("ends_r", 4), sig("hit_r", TB), sig("edge_r", TB + 1)
        cs_psum, plug_r, pick_r = sig("edge_count_psum", 1), sig("plug_r", 1), sig("pick_r", TB)
        st_psum, st_r, dp_psum = sig("state_psum", 1), sig("state_r", 1), sig("depool_psum", 1)
        dp_done = HalfSignal([sem(f"depool_r{h}") for h in range(2)], 1, 1)
        n_const = 16 * 3
        EDGE_J = 5
        block = ctx.enter_context(nc.Block())
        slots, expert_rows = g["slots"], g["expert_rows"]

        @block.sync
        def _(sp):
            def load_first(n, h):
                got = w1_in.sems[h]
                sp.dma_start(rows[h][:, 0:2, :], slots[bass.ds(n * CAP, 2 * P), :].rearrange("(t p) d -> p t d", p=P)).then_inc(got, 16)
                sp.dma_start(rows[h][0:CAP - 2 * P, 2, :], slots[bass.ds(n * CAP + 2 * P, CAP - 2 * P), :]).then_inc(got, 16)
                sp.dma_start(w1[h][:, :, :], a["L0_ffn_w1"][bass.ds(n * D, D), :].rearrange("(c p) f -> p c f", p=P)).then_inc(got, 16)
                sp.dma_start(b1[h][:, :], a["L0_ffn_b1C"][bass.ds(n * P, P), :]).then_inc(got, 16)

            def load_second(n, h):
                got = w2_in.sems[h]
                sp.dma_start(b2[h][:, :], a["L0_ffn_b2"][bass.ds(n * D, D)].partition_broadcast(P)).then_inc(got, 16)
                sp.dma_start(w2[h][:, :, :], a["L0_ffn_w2"][bass.ds(n * F, F), :].rearrange("(c p) d -> p c d", p=P)).then_inc(got, 16)

            def store(n, h):
                done = out_sent.sems[h]
                sp.dma_start(expert_rows[bass.ds(n * CAP, 2 * P), :].rearrange("(t p) d -> p t d", p=P), outr[h][:, 0:2, :]).then_inc(done, 16)
                sp.dma_start(expert_rows[bass.ds(n * CAP + 2 * P, CAP - 2 * P), :], outr[h][0:CAP - 2 * P, 2, :]).then_inc(done, 16)

            for h in range(2):
                sp.sem_inc(out_sent.sems[h], out_sent.first)
                sp.sem_inc(dp_done.sems[h], dp_done.first)
                load_first(h, h)
            for h in range(2):
                load_second(h, h)
            with sp.Fori(0, PAIRS - 1) as i:
                for h in range(2):
                    sp.wait_ge(*h_r((i, h)))
                    load_first(i * 2 + (h + 2), h)
                for h in range(2):
                    sp.wait_ge(*o_r((i, h)))
                    store(i * 2 + h, h)
                    load_second(i * 2 + (h + 2), h)
            for h in range(2):
                sp.wait_ge(*o_r((PAIRS - 1, h)))
                store(NE - 2 + h, h)
            for h in range(2):
                sp.wait_ge(*out_sent((PAIRS - 1, h)))

        @block.gpsimd
        def _(pool):
            pool.memset(mhalf[:, :], -0.5).then_inc(s_set, 1)
            pool.memset(zero[:, :], 0.0).then_inc(s_set, 1)
            pool.memset(ones[:, :], 1.0).then_inc(s_set, 1)
            pool.iota(place[:, :], [[P, TB]], base=0, channel_multiplier=1, allow_small_or_imprecise_dtypes=True).then_inc(s_set, 1)

            def load(n, h):
                pool.dma_start(lens[h][:, :], a["patch_lens"][bass.ds(n * S, S)].partition_broadcast(P)).then_inc(p_in.sems[h], 16)
                pool.dma_start(patch[h][:, :, :], a["ctx"][bass.ds(n * S, S), :].rearrange("(t p) d -> p t d", p=P)).then_inc(p_in.sems[h], 16)

            for h in range(2):
                load(h, h)
            pool.wait_ge(s_set, 4)

            def power(b):
                pool.wait_ge(*ms_r(b))
                pool.tensor_tensor(rrms[b[1]][:, :], msq[b[1]][:, :], mhalf[:, :], ALU.pow).then_inc(rr_r.sem, 1)

            with pool.Fori(0, PAIRS - 1) as i:
                B = [(i, 0), (i, 1)]
                for b in B:
                    power(b)
                for b in B:
                    pool.wait_ge(*ends_r(b))
                    pool.wait_ge(*u_r(b))
                    pool.wait_ge(*sq_r(b))
                    load(i * 2 + (b[1] + 2), b[1])
            for h in range(2):
                power((PAIRS - 1, h))

        @block.scalar
        def _(act):
            KT = "(c p) n -> p c n"
            act.dma_start(decayT[:, :, :], a["c_decayT"].rearrange(KT, p=P)).then_inc(s_const, 16)
            act.dma_start(upto[:, :, :], a["c_upto"].rearrange(KT, p=P)).then_inc(s_const, 16)
            act.dma_start(g_init[:, :], a["L1_xattn_g_init"][0:D].partition_broadcast(P)).then_inc(s_const, 16)
            act.wait_ge(s_const, n_const)
            act.activation(uptob[:, :, :], upto[:, :, :], ACT.Copy).then_inc(s_cast, 1)
            with act.Fori(0, PAIRS) as i:
                B = [(i, 0), (i, 1)]
                for b in B:
                    h = b[1]
                    act.wait_ge(*p_in(b))
                    for t in range(TB):
                        act.activation(square[h][:, t, :], patch[h][:, t, :], ACT.Square, accum_out=ssum[h][:, t:t + 1]).then_inc(sq_r.sem, 1)
                for j in range(FT):
                    for b in B:
                        h = b[1]
                        act.wait_ge(*h_psum(b, j + 1))
                        act.activation(hid[h][:, j, :], bank[h][j % 4][:, 0:CAP], ACT.Gelu, bias=b1[h][:, j:j + 1]).then_inc(h_r.sems[h], 1)
                for b in B:
                    act.wait_ge(*st_psum(b))
                    act.activation(state[b[1]][:, :, :].rearrange("p t d -> p (t d)"), bank[b[1]][3][:, :], ACT.Copy).then_inc(st_r.sem, 1)

        @block.tensor
        def _(pe):
            pe.wait_ge(s_cast, 1)
            with pe.Fori(0, PAIRS) as i:
                B = [(i, 0), (i, 1)]
                for b in B:
                    h = b[1]
                    pe.wait_ge(*w1_in(b))
                    for c in range(DT):
                        for t, (s0, n) in enumerate(SLOTS):
                            last = pe.transpose(bank[h][c][:, s0:s0 + n], rows[h][0:n, t, c * P:(c + 1) * P], identf[0:n, 0:n])
                    last.then_inc(rt_psum.sem, 1)
                for j in range(FT):
                    if j == EDGE_J:
                        for b in B:
                            h = b[1]
                            pe.wait_ge(*edge_r(b))
                            pe.wait_ge(*h_r(b, 4))
                            for t in range(TB):
                                last = pe.matmul(bank[h][3][:, 0:S], edge[h][:, t, :], uptob[:, t, :], start=(t == 0), stop=(t == TB - 1))
                            last.then_inc(cs_psum.sem, 1)
                    for b in B:
                        h = b[1]
                        if j == 0:
                            pe.wait_ge(*rt_r(b))
                        if j == 3:
                            pe.wait_ge(*dp_done(b, 0))
                        if j == FT - 1:
                            pe.wait_ge(*plug_r(b))
                        if j >= 4:
                            pe.wait_ge(*h_r(b, j - 3))
                        for c in range(DT):
                            last = pe.matmul(bank[h][j % 4][:, 0:CAP], w1[h][:, c, j * P:(j + 1) * P], rowsT[h][:, c, :],
                                             start=(c == 0), stop=(c == DT - 1))
                        last.then_inc(h_psum.sems[h], 1)
                for b in B:
                    h = b[1]
                    pe.wait_ge(*u_r(b))
                    pe.wait_ge(*h_r(b))
                    for t in range(TB):
                        for q in range(t + 1):
                            last = pe.matmul(bank[h][3][:, t * D:(t + 1) * D], decayT[:, q, t * P:(t + 1) * P], u[h][:, q, :],
                                             start=(q == 0), stop=(q == t))
                    last.then_inc(st_psum.sem, 1)
                for b in B:
                    h = b[1]
                    for t, (s0, n) in enumerate(SLOTS):
                        if t == 0:
                            pe.wait_ge(*w2_in(b))
                        for j in range(FT):
                            last = pe.matmul(bank[h][t][0:n, 0:D], hid[h][:, j, s0:s0 + n], w2[h][:, j, :],
                                             start=(j == 0), stop=(j == FT - 1))
                        last.then_inc(o_psum.sem, 1)
                for b in B:
                    h = b[1]
                    pe.wait_ge(*st_r(b))
                    pe.wait_ge(*pick_r(b))
                    for t in range(TB):
                        for q in range(TB):
                            last = pe.matmul(bank[h][3][:, t * D:(t + 1) * D], pick[h][:, q, t * P:(t + 1) * P], state[h][:, q, :],
                                             start=(q == 0), stop=(q == TB - 1))
                    last.then_inc(dp_psum.sem, 1)
                for b in B:
                    pe.wait_ge(*o_r(b))

        @block.vector
        def _(dve):
            dve.wait_ge(s_const, n_const)
            dve.wait_ge(s_set, 4)
            dve.wait_ge(g["s_l1"], g["n_l1"])
            with dve.Fori(0, PAIRS) as i:
                B = [(i, 0), (i, 1)]
                for b in B:
                    h = b[1]
                    dve.wait_ge(*rt_psum(b))
                    for c in range(DT):
                        dve.tensor_copy(rowsT[h][:, c, :], bank[h][c][:, 0:CAP]).then_inc(rt_r.sem, 1)
                for b in B:
                    h = b[1]
                    dve.wait_ge(*p_in(b))
                    dve.tensor_copy(lensf[h][:, :], lens[h][:, :]).then_inc(ends_r.sem, 1)
                    dve.wait_ge(*ends_r(b, 1))
                    dve.tensor_tensor_scan(ends[h][:, :], lensf[h][:, :], zero[:, :], -1.0, ALU.add, ALU.add).then_inc(ends_r.sem, 1)
                    dve.wait_ge(*ends_r(b, 2))
                    dve.tensor_scalar(wrap[h][:, :], ends[h][:, :], 0.0, float(S), ALU.is_lt, ALU.mult).then_inc(ends_r.sem, 1)
                    dve.wait_ge(*ends_r(b, 3))
                    dve.tensor_tensor(ends[h][:, :], ends[h][:, :], wrap[h][:, :], ALU.add).then_inc(ends_r.sem, 1)
                    dve.wait_ge(*ends_r(b, 4))
                    for t in range(TB):
                        dve.tensor_scalar(hit[h][:, t, :], ends[h][:, :], place[:, t:t + 1], None, ALU.is_equal).then_inc(hit_r.sem, 1)
                    dve.wait_ge(*hit_r(b))
                    dve.tensor_reduce(hits[h][:, :], hit[h][:, :, :], X, ALU.max).then_inc(edge_r.sem, 1)
                    dve.wait_ge(*edge_r(b, 1))
                    for t in range(TB):
                        dve.tensor_scalar(edge[h][:, t, :], ones[:, :], hits[h][:, t:t + 1], None, ALU.mult).then_inc(edge_r.sem, 1)
                for b in B:
                    h = b[1]
                    dve.wait_ge(*sq_r(b))
                    dve.tensor_scalar(msq[h][:, :], ssum[h][:, :], 1.0 / DC, 1e-5, ALU.mult, ALU.add).then_inc(ms_r.sem, 1)
                for b in B:
                    h = b[1]
                    dve.wait_ge(*cs_psum(b))
                    dve.tensor_scalar(plug[h][:, :], bank[h][3][:, 0:S], -1.0, 0.0, ALU.add, ALU.max).then_inc(plug_r.sem, 1)
                    dve.wait_ge(*plug_r(b))
                    for t in range(TB):
                        dve.tensor_scalar(pick[h][:, t, :], plug[h][:, :], place[:, t:t + 1], None, ALU.is_equal).then_inc(pick_r.sem, 1)
                for b in B:
                    h = b[1]
                    dve.wait_ge(*rr_r(b))
                    for t in range(TB):
                        dve.scalar_tensor_tensor(u[h][:, t, :], patch[h][:, t, 0:D], rrms[h][:, t:t + 1], g_init[:, :],
                                                 ALU.mult, ALU.mult).then_inc(u_r.sem, 1)
                for b in B:
                    h = b[1]
                    dve.wait_ge(*out_sent(b, 0))
                    for t, (s0, n) in enumerate(SLOTS):
                        dve.wait_ge(*o_psum(b, t + 1))
                        dve.tensor_tensor(outr[h][0:n, t, :], bank[h][t][0:n, 0:D], b2[h][0:n, :], ALU.add).then_inc(o_r.sem, 1)
                for b in B:
                    h = b[1]
                    dve.wait_ge(*dp_psum(b))
                    dve.tensor_tensor(g["depool_all"][:, bass.ds(tile_of(b), TB), :], bank[h][3][:, :].rearrange("p (t d) -> p t d", t=TB),
                                      g["b_in"][:, :].unsqueeze(1).broadcast_to([P, TB, D]), ALU.add).then_inc(dp_done.sems[h], 1)


def layer1(nc, a, g, used):
    with ExitStack() as ctx:
        def sb(name, shape, dt=F32):
            return ctx.enter_context(nc.sbuf_tensor(name, shape, dt))

        def sb2(name, shape, dt=F32):
            return [sb(f"{name}{h}", shape, dt) for h in range(2)]

        def sem(name):
            used.append(ctx.enter_context(nc.semaphore(name)))
            return used[-1]

        def sig(name, per):
            return Signal(sem(name), per)

        def turns(name, per):
            return HalfSignal([sem(f"{name}{h}") for h in range(2)], per)

        dve_own, early_own = [], []
        idle_r, idle_gr = OwnSignal(sem("pool_idle_b"), 1), OwnSignal(sem("pool_idle_gather"), 1)

        def own(name, per):
            dve_own.append(OwnSignal(sem(name), per))
            return dve_own[-1]

        def own_turns(name, per):
            dve_own.append(OwnHalfSignal([sem(f"{name}{h}") for h in range(2)], per))
            return dve_own[-1]

        def early(name, per):
            early_own.append(OwnSignal(sem(name), per))
            return early_own[-1]

        def norm_signals(name, own=own):
            return {"stats": own(name + "_stats", TB), "mv": own(name + "_mv", TB), "var": sig(name + "_var", 1),
                    "rstd": sig(name + "_rstd", 1), "xn": sig(name + "_xn", TB), "xt": sig(name + "_xt_psum", 1),
                    "xts": sig(name + "_xt", DT)}

        bank, x_all, identf, identb = g["bank"], g["x_all"], g["identf"], g["identb"]
        NG = RH // GH
        NT = 2 * GH
        W1, W0 = GH * S, GH * P
        SPAN = [(k * S, S) if k < GH else (W1 + (k - GH) * P, P) for k in range(NT)]

        causal, causalb = sb("causal", [P, P]), sb("causalb", [P, P], BF16)
        mhalf = sb("mhalf_b", [P, TB])
        rows_i, wts = sb2("rows_i", [P, TB * 2], U32), sb2("wts", [P, TB, 2])
        got = sb2("got", [P, TB * 2, D])
        stats, mv = sb2("stats_b", [P, TB, 6]), sb2("mv_b", [P, TB, 2])
        var, rstd = sb2("var_b", [P, TB]), sb2("rstd_b", [P, TB])
        xn, xnT = sb2("xn_b", [P, TB, D]), sb2("xnT_b", [P, DT * S])
        qk, turned = sb2("qk", [P, TB, 512]), sb2("turned", [P, TB, 512])
        shared = sb2("shared", [P, 2 * (W1 + W0)])
        roped = [shared[h][:, 0:TB * 2 * RH * 32].rearrange("p (t a c) -> p t a c", t=TB, a=2 * RH) for h in range(2)]
        vals = sb2("vals", [P, TB, RH, 32])
        qkT = sb2("qkT", [P, NG, 2, S])
        top1, top2 = sb2("top1", [P, NT, 8]), sb2("top2", [P, NT, 8])
        nmax = sb2("nmax_b", [P, NT])
        rest, keptT = [x[:, 0:W1 + W0] for x in shared], [x[:, W1 + W0:2 * (W1 + W0)] for x in shared]
        exps, kept = sb2("exps", [P, W1 + W0]), sb2("kept", [P, W1 + W0])
        att, attr, attn = sb2("att", [P, TB, RH, RD + 1]), sb2("attr", [P, TB, RH]), xn

        attT = sb2("attT", [P, DT * S])
        outT = [attT[h][:, 0:S] for h in range(2)]
        idle, idle_v = sb("idle", [P, 4]), sb("idle_v", [P, 2 * NG])
        pooled, pooledb = sb2("pooled", [P, DT]), sb2("pooledb", [P, DT, P])
        ones = sb("ones_b", [P, P])
        gl, gtop, ngt = sb2("gl", [P, NE]), sb2("gtop", [P, 8]), sb2("ngt", [P, 1])
        ge, gates, gsum = sb2("ge", [P, NE]), sb2("gates", [P, NE]), sb2("gsum", [P, 1])
        NH = 3
        hid = [[sb(f"hid_b{h}{k}", [P, 512])[:, :] for k in range(NH - 1)] + [turned[h][:, 1, :]] for h in range(2)]
        acc, y = [turned[h][:, 0, :] for h in range(2)], sb2("y", [P, TB, D])

        idle_vr = own("dve_idle", NG)
        s_half, s_zero, s_set, s_const, s_cast = sem("minus_half_set"), sem("pads_zeroed"), sem("b_memsets_done"), sem("causal_loaded"), sem("causal_cast")
        idx_r, wts_r = sig("rows_i_r", 1), early("wts_r", 1)
        got_in = g["got_in"]
        comb = early("combined", 2 * TB)
        N4, N5, N6 = norm_signals("n4", early), norm_signals("n5"), norm_signals("n6")
        qk_psum, v_psum, qk_r, v_r = sig("qk_psum", TB), sig("v_psum", 1), sig("qk_r", TB), sig("v_r", TB)
        rope_a, rope_r = own("rope_parts", TB * 3), sig("roped_r", TB)
        qkT_psum, qkT_r = sig("qkT_psum", NG), sig("qkT_r", NG)
        sc_psum = turns("scores_b_psum", NG)
        top1_r, nmax_r = own_turns("top1_r", NG * NT), turns("nmax_b_r", NG)
        rest_r, top2_r = own_turns("rest_r", NG * NT), own_turns("top2_r", NG * NT)
        exp_r = turns("exps_r", NG)
        kept_r = turns("kept_r", NG)
        kT_psum, kT_r = turns("keptT_psum", NG * 3), turns("keptT_r", NG * 3)
        oT_psum, oT_r, av_psum, av_r = turns("outT_psum", NG), turns("outT_r", NG), turns("att_psum", NG), turns("att_r", NG)
        den_r, attn_r = own("att_recip", 1), sig("attn_r", 1)
        aT_psum, aT_r, ao_psum, x4 = sig("attT_psum", 1), sig("attT_r", 1), sig("att_out_psum", 1), own("x4_ready", 1)
        xd, win_psum, x5 = sig("x_plus_depool", 1), sig("win_psum", 1), own("x5_ready", 1)
        pb_r, gl_psum, gl_r = sig("pooled_bcast", DT), sig("gate_psum", 1), own("gl_r", 1)
        gtop_r, ngt_r, ge_r, gm_r = own("gtop_r", 1), sig("ngt_r", 1), sig("gate_exp", 1), own("gates_r", 4)
        e_psum, e_r, acc_r = turns("expert_psum", NE), turns("expert_gelu", NE), turns("acc_r", NE)
        f_psum, y_r = sig("final_psum", 1), HalfSignal([sem(f"y_r{h}") for h in range(2)], 1, 1)
        y_out = HalfSignal([sem(f"y_stored{h}") for h in range(2)], 16, 1)
        EXPERTS = [(0, 0), (1, 0), (2, 0)] + [x for e in range(3, NE) for x in ((e - 3, 1), (e, 0))] + [(e, 1) for e in range(NE - 3, NE)]
        block = ctx.enter_context(nc.Block())

        @block.sync
        def _(sp):
            sp.dma_start(causal[:, :], a["c_causal"]).then_inc(s_const, 16)
            for h in range(2):
                sp.sem_inc(y_out.sems[h], y_out.first)
                sp.sem_inc(y_r.sems[h], y_r.first)
            with sp.Fori(0, PAIRS) as i:
                for b in [(i, 0), (i, 1)]:
                    h = b[1]
                    sp.wait_ge(*y_r(b))
                    sp.dma_start(a["out"][bass.ds((i * 2 + h) * S, S), :].rearrange("(t p) d -> p t d", p=P), y[h][:, :, :]).then_inc(y_out.sems[h], 16)
            for h in range(2):
                sp.wait_ge(*y_out((PAIRS - 1, h)))

        @block.gpsimd
        def _(pool):
            pool.memset(mhalf[:, :], -0.5).then_inc(s_half, 1)
            pool.wait_ge(s_half, 1)
            def gather(b):
                h = b[1]
                pool.wait_ge(*idx_r(b))
                pool.tensor_tensor(idle[:, h:h + 1], mhalf[:, 0:1], mhalf[:, 0:1], ALU.add).then_inc(idle_gr.sem, 1)
                for k in range(2 * TB):
                    pool.indirect_dma_start(
                        out=got[h][:, k, :], out_offset=None, in_=g["expert_rows"],
                        in_offset=bass.IndirectOffsetOnAxis(ap=rows_i[h][:, k:k + 1], axis=0),
                        bounds_check=NE * CAP - 1, oob_is_err=False).then_inc(got_in.sems[h], 16)

            for h in range(2):
                gather((0, h))
            pool.memset(ones[:, :], 1.0).then_inc(s_set, 1)
            for h in range(2):
                pool.memset(shared[h][:, :], 0.0).then_inc(s_set, 1)
                pool.memset(vals[h][:, :, :, RD:32], 0.0).then_inc(s_zero, 1)
            pool.wait_ge(s_zero, 2)
            for h in range(2):
                pool.memset(vals[h][:, :, :, RD], 1.0).then_inc(s_set, 1)
            pool.wait_ge(s_set, 5)

            def power(v, out, waits, done, b):
                pool.wait_ge(*waits)
                pool.tensor_tensor(out[b[1]][:, :], v[b[1]][:, :], mhalf[:, :], ALU.pow).then_inc(done, 1)

            def body(i, last_turn):
                B, after = [(i, 0), (i, 1)], [(i + 1, 0), (i + 1, 1)]
                if not last_turn:
                    for b in after:
                        gather(b)
                for b in B:
                    power(var, rstd, N5["var"](b), N5["rstd"].sem, b)
                    x = x_all[:, bass.ds(tile_of(b), TB), :]
                    pool.wait_ge(*N5["xn"](b))
                    pool.tensor_tensor(idle[:, 2 + b[1]:3 + b[1]], mhalf[:, 0:1], mhalf[:, 0:1], ALU.add).then_inc(idle_r.sem, 1)
                    pool.tensor_tensor(x, x, g["depool_all"][:, bass.ds(tile_of(b), TB), :], ALU.add).then_inc(xd.sem, 1)
                for b in B:
                    power(var, rstd, N6["var"](b), N6["rstd"].sem, b)
                finish(pool, [idle_r])
                if not last_turn:
                    for b in after:
                        power(var, rstd, N4["var"](b), N4["rstd"].sem, b)
                    finish(pool, [idle_gr])

            for h in range(2):
                power(var, rstd, N4["var"]((0, h)), N4["rstd"].sem, (0, h))
            finish(pool, [idle_gr])
            with pool.Fori(0, PAIRS - 1) as i:
                body(i, False)
            body(PAIRS - 1, True)

        @block.scalar
        def _(act):
            act.wait_ge(s_const, 16)
            act.activation(causalb[:, :], causal[:, :], ACT.Copy).then_inc(s_cast, 1)
            act.wait_ge(s_set, 5)

            def copy(out, psum, done, *waits, **kw):
                for w in waits:
                    act.wait_ge(*w)
                act.activation(out, psum, ACT.Copy, **kw).then_inc(done, 1)

            def body(i):
                B = [(i, 0), (i, 1)]
                for b in B:
                    h = b[1]
                    act.wait_ge(*N4["xt"](b))
                    for c in range(DT):
                        copy(xnT[h][:, c * S:(c + 1) * S], bank[h][0][:, c * S:(c + 1) * S], N4["xts"].sem)
                for b in B:
                    h = b[1]
                    for t in range(TB):
                        copy(qk[h][:, t, :], bank[h][2 + t][:, :], qk_r.sem, qk_psum(b, t + 1))
                for b in B:
                    h = b[1]
                    act.wait_ge(*v_psum(b))
                    for t in range(TB):
                        copy(vals[h][:, t, :, 0:RD], bank[h][1][:, t * D:(t + 1) * D].rearrange("p (a c) -> p a c", c=RD), v_r.sem)
                for b in B:
                    h = b[1]
                    for q in range(NG):
                        copy(qkT[h][:, q, :, :].rearrange("p a c -> p (a c)"), bank[h][q][:, :], qkT_r.sem, qkT_psum(b, q + 1))
                def turned_out(b, gr):
                    copy(outT[b[1]], bank[b[1]][3][:, 0:S], oT_r.sems[b[1]], oT_psum(b, gr + 1))

                def heads_out(b, gr):
                    h = b[1]
                    copy(att[h][:, :, gr:RH:NG, :], bank[h][3][:, S:2 * S].rearrange("p (t a c) -> p t a c", t=TB, a=GH)[:, :, :, 0:RD + 1],
                         av_r.sems[h], av_psum(b, gr + 1))

                steps = [(b, gr) for gr in range(NG) for b in B]
                for n_step, (b, gr) in enumerate(steps):
                    h = b[1]
                    act.wait_ge(*nmax_r(b, gr + 1))
                    if gr > 0:
                        act.wait_ge(*kept_r(b, gr))
                    for k, (o, n) in enumerate(SPAN):
                        if o % 512 == 0:
                            act.wait_ge(*rest_r(b, NT * gr + (o + 512) // n - (0 if k < GH else W1 // n - GH)))
                        src = bank[h][o // 512][:, o % 512:o % 512 + n]
                        last = act.activation(exps[h][:, o:o + n], src, ACT.Exp, bias=nmax[h][:, k:k + 1], scale=RD ** -0.5)
                    last.then_inc(exp_r.sems[h], 1)
                    if n_step >= 2:
                        turned_out(*steps[n_step - 2])
                        heads_out(*steps[n_step - 2])
                    if n_step == len(steps) - 1:
                        turned_out(*steps[-2])
                        heads_out(*steps[-2])
                    for q in range(3):
                        copy(keptT[h][:, q * 512:(q + 1) * 512], bank[h][q][:, :], kT_r.sems[h], kT_psum(b, 3 * gr + q + 1))
                copy(attT[B[0][1]][:, :], bank[B[0][1]][0][:, :], aT_r.sem, aT_psum(B[0]))
                turned_out(*steps[-1])
                heads_out(*steps[-1])
                copy(attT[B[1][1]][:, :], bank[B[1][1]][0][:, :], aT_r.sem, aT_psum(B[1]))
                for b in B:
                    h = b[1]
                    act.wait_ge(*N5["xt"](b))
                    for c in range(DT):
                        copy(xnT[h][:, c * S:(c + 1) * S], bank[h][2][:, c * S:(c + 1) * S], N5["xts"].sem, scale=g["g_res"][:, c:c + 1])
                for b in B:
                    h = b[1]
                    act.wait_ge(*N6["xt"](b))
                    for c in range(DT):
                        copy(xnT[h][:, c * S:(c + 1) * S], bank[h][0][:, c * S:(c + 1) * S], N6["xts"].sem, accum_out=pooled[h][:, c:c + 1])
                for e, h in EXPERTS:
                    b = B[h]
                    if e == 0:
                        act.wait_ge(*ngt_r(b))
                        act.activation(ge[h][:, :], gl[h][:, :], ACT.Exp, bias=ngt[h][:, 0:1]).then_inc(ge_r.sem, 1)
                    act.wait_ge(*e_psum(b, e + 1))
                    if e >= NH:
                        act.wait_ge(*acc_r(b, e - NH + 1))
                    for o in range(DT):
                        last = act.activation(hid[h][e % NH][:, o * S:(o + 1) * S], bank[h][e % 3][:, o * S:(o + 1) * S], ACT.Gelu,
                                              bias=g["expert_b"][:, e, o:o + 1])
                    last.then_inc(e_r.sems[h], 1)

            with act.Fori(0, PAIRS - 1) as i:
                body(i)
            body(PAIRS - 1)

        @block.tensor
        def _(pe):
            pe.wait_ge(s_cast, 1)
            pe.wait_ge(s_set, 5)

            def turn_rows(b):
                pe.wait_ge(*N4["xn"](b))
                transpose_rows(pe, bank[b[1]][0], xn[b[1]], identf).then_inc(N4["xt"].sem, 1)

            def body(i, last_turn):
                B, after = [(i, 0), (i, 1)], [(i + 1, 0), (i + 1, 1)]

                def scores(b, gr):
                    h = b[1]
                    r0 = 32 * gr
                    if gr == 0:
                        pe.wait_ge(*qkT_r(b))
                    else:
                        pe.wait_ge(*kT_r(b, 3 * gr))
                    for k, (o, n) in enumerate(SPAN):
                        q, t = k % GH, 1 if k < GH else 0
                        out = bank[h][o // 512][:, o % 512:o % 512 + n]
                        pe.matmul(out, qkT[h][r0:r0 + RD, q, 0, t * P:(t + 1) * P], qkT[h][r0:r0 + RD, q, 1, 0:n], start=True, stop=False)
                        last = pe.matmul(bank[h][o // 512][:, o % 512 + n - P:o % 512 + n], identb[:, :], causalb[:, :], start=False, stop=True)
                    last.then_inc(sc_psum.sems[h], 1)

                for b in B:
                    h = b[1]
                    pe.wait_ge(*N4["xts"](b))
                    pe.wait_ge(*y_r(b, 0))
                    for t in range(TB):
                        for k in range(DT):
                            last = pe.matmul(bank[h][2 + t][:, :], xnT[h][:, k * S + t * P:k * S + (t + 1) * P], g["qkv_w"][:, k, 0:512],
                                             start=(k == 0), stop=(k == DT - 1))
                        last.then_inc(qk_psum.sem, 1)
                for b in B:
                    h = b[1]
                    for t in range(TB):
                        for k in range(DT):
                            last = pe.matmul(bank[h][1][:, t * D:(t + 1) * D], xnT[h][:, k * S + t * P:k * S + (t + 1) * P],
                                             g["qkv_w"][:, k, 512:768], start=(k == 0), stop=(k == DT - 1))
                    last.then_inc(v_psum.sem, 1)
                for b in B:
                    h = b[1]
                    pe.wait_ge(*rope_r(b))
                    pe.wait_ge(*v_r(b))
                    for gr in range(NG):
                        for q in range(2):
                            for t in range(TB):
                                last = pe.transpose(bank[h][gr][:, q * S + t * P:q * S + (t + 1) * P],
                                                    roped[h][:, t, q * RH + gr * GH:q * RH + (gr + 1) * GH, :].rearrange("p a c -> p (a c)"),
                                                    identf[:, :])
                        last.then_inc(qkT_psum.sem, 1)
                    scores(b, 0)

                def weighted(b, gr):
                    h = b[1]
                    pe.wait_ge(*kT_r(b, 3 * gr + 3))
                    if gr > 0:
                        pe.wait_ge(*av_r(b, gr))
                    for s in range(TB):
                        for j in range(GH):
                            last = pe.matmul(bank[h][3][32 * j:32 * j + 32, s * P:S], vals[h][:, s, j * NG + gr, :],
                                             keptT[h][:, (3 * j + 2 * s) * P:(3 * j + 2 + s) * P], start=(s == 0), stop=(s == TB - 1))
                    last.then_inc(oT_psum.sems[h], 1)

                def heads_back(b, gr):
                    h = b[1]
                    pe.wait_ge(*oT_r(b, gr + 1))
                    for t in range(TB):
                        last = pe.transpose(bank[h][3][:, S + t * P:S + (t + 1) * P], outT[h][:, t * P:(t + 1) * P], identf[:, :])
                    last.then_inc(av_psum.sems[h], 1)

                steps = [(b, gr) for gr in range(NG) for b in B]
                for n_step, (b, gr) in enumerate(steps):
                    h = b[1]
                    if n_step == len(steps) - 1:
                        weighted(*steps[-2])
                        heads_back(*steps[-2])
                    pe.wait_ge(*kept_r(b, gr + 1))
                    for q in range(3 * GH):
                        j, o = q // 3, (W1 + q // 3 * P, q // 3 * S, q // 3 * S + P)[q % 3]
                        last = pe.transpose(bank[h][q // 4][:, (q % 4) * P:(q % 4 + 1) * P], kept[h][:, o:o + P], identf[:, :])
                        if q % 4 == 3:
                            last.then_inc(kT_psum.sems[h], 1)
                    if 1 <= n_step < len(steps) - 1:
                        weighted(*steps[n_step - 1])
                    if gr < NG - 1:
                        scores(b, gr + 1)
                    if 1 <= n_step < len(steps) - 1:
                        heads_back(*steps[n_step - 1])

                def turn_heads(b):
                    pe.wait_ge(*attn_r(b))
                    transpose_rows(pe, bank[b[1]][0], attn[b[1]], identf).then_inc(aT_psum.sem, 1)

                def out_projection(b):
                    h = b[1]
                    pe.wait_ge(*aT_r(b))
                    for t in range(TB):
                        for k in range(DT):
                            last = pe.matmul(bank[h][1][:, t * D:(t + 1) * D], attT[h][:, k * S + t * P:k * S + (t + 1) * P],
                                             g["attn_out_w"][:, k, :], start=(k == 0), stop=(k == DT - 1))
                    last.then_inc(ao_psum.sem, 1)

                def turn_normed(N, b, k):
                    pe.wait_ge(*N["xn"](b))
                    transpose_rows(pe, bank[b[1]][k], xn[b[1]], identf).then_inc(N["xt"].sem, 1)

                def in_projection(b):
                    h = b[1]
                    pe.wait_ge(*N5["xts"](b))
                    for t in range(TB):
                        for k in range(DT):
                            last = pe.matmul(bank[h][1][:, t * D:(t + 1) * D], xnT[h][:, k * S + t * P:k * S + (t + 1) * P],
                                             g["win_w"][:, k, :], start=(k == 0), stop=(k == DT - 1))
                    last.then_inc(win_psum.sem, 1)

                def expert(b, e):
                    h = b[1]
                    if e == 0:
                        pe.wait_ge(*N6["xts"](b))
                    if e >= 3:
                        pe.wait_ge(*e_r(b, e - 2))
                    for o in range(DT):
                        for k in range(DT):
                            last = pe.matmul(bank[h][e % 3][:, o * S:(o + 1) * S], g["expert_w"][:, k, e * D + o * P:e * D + (o + 1) * P],
                                             xnT[h][:, k * S:(k + 1) * S], start=(k == 0), stop=(k == DT - 1))
                    last.then_inc(e_psum.sems[h], 1)

                def gate_logits(b):
                    h = b[1]
                    pe.wait_ge(*pb_r(b))
                    for k in range(DT):
                        last = pe.matmul(bank[h][3][:, 0:NE], pooledb[h][:, k, :], g["gate_w"][:, k, :], start=(k == 0), stop=(k == DT - 1))
                    last.then_inc(gl_psum.sem, 1)

                def turn_back(b):
                    h = b[1]
                    pe.wait_ge(*acc_r(b))
                    for t in range(TB):
                        for o in range(DT):
                            last = pe.transpose(bank[h][3][:, t * D + o * P:t * D + (o + 1) * P], acc[h][:, o * S + t * P:o * S + (t + 1) * P], identf[:, :])
                    last.then_inc(f_psum.sem, 1)

                turn_heads(B[0])
                weighted(*steps[-1])
                out_projection(B[0])
                heads_back(*steps[-1])
                turn_heads(B[1])
                turn_normed(N5, B[0], 2)
                out_projection(B[1])
                in_projection(B[0])
                turn_normed(N5, B[1], 2)
                turn_normed(N6, B[0], 0)
                in_projection(B[1])
                for e, h in EXPERTS:
                    if (e, h) == EXPERTS[2]:
                        turn_normed(N6, B[1], 0)
                    if (e, h) == EXPERTS[-1] and not last_turn:
                        pe.wait_ge(*e_r(B[0]))
                        turn_rows(after[0])
                    expert(B[h], e)
                    if e == 0:
                        gate_logits(B[h])
                turn_back(B[0])
                if not last_turn:
                    pe.wait_ge(*e_r(B[1]))
                    turn_rows(after[1])
                turn_back(B[1])

            for h in range(2):
                turn_rows((0, h))
            with pe.Fori(0, PAIRS - 1) as i:
                body(i, False)
            body(PAIRS - 1, True)

        @block.vector
        def _(dve):

            def xt(b):
                return lambda t: x_all[:, bass.ds(tile_of(b) + t, 1), :].rearrange("p a d -> p (a d)")

            def choices(b):
                h = b[1]
                dve.tensor_copy(rows_i[h][:, :].rearrange("p (t k) -> p t k", k=2), g["choice_row"][:, bass.ds(tile_of(b), TB), :]).then_inc(idx_r.sem, 1)
                dve.tensor_copy(wts[h][:, :, :], g["choice_w"][:, bass.ds(tile_of(b), TB), :]).then_inc(wts_r.sem, 1)

            def combine(b):
                h = b[1]
                dve.wait_ge(*wts_r(b))
                dve.wait_ge(*got_in(b))
                for k in range(2):
                    for t in range(TB):
                        if k:
                            dve.wait_ge(*comb(b, t + 1))
                        dve.scalar_tensor_tensor(xt(b)(t), got[h][:, 2 * t + k, :], wts[h][:, t, k:k + 1], xt(b)(t),
                                                 ALU.mult, ALU.add).then_inc(comb.sem, 1)

            def first_stats(b):
                dve.wait_ge(*comb(b))
                norm_stats(dve, xt(b), stats, mv, var, N4, b)

            def body(i, last_turn):
                B, after = [(i, 0), (i, 1)], [(i + 1, 0), (i + 1, 1)]
                for b in B:
                    h = b[1]
                    for t in range(TB):
                        q2 = qk[h][:, t, :].rearrange("p (a two) -> p a two", two=2)
                        o2 = turned[h][:, t, :].rearrange("p (a two) -> p a two", two=2)
                        s2 = g["rope_sin"][:, t, :].rearrange("p (a two) -> p a two", two=2)
                        heads = roped[h][:, t, :, 0:RD]
                        dve.wait_ge(*qk_r(b, t + 1))
                        for e in range(2):
                            dve.tensor_tensor(o2[:, :, e], q2[:, :, 1 - e], s2[:, :, e], ALU.mult).then_inc(rope_a.sem, 1)
                        dve.tensor_tensor(heads, qk[h][:, t, :].rearrange("p (a c) -> p a c", c=RD),
                                          g["rope_cos"][:, t, :].rearrange("p (a c) -> p a c", c=RD), ALU.mult).then_inc(rope_a.sem, 1)
                        dve.wait_ge(*rope_a(b, 3 * t + 3))
                        dve.tensor_tensor(heads, heads, turned[h][:, t, :].rearrange("p (a c) -> p a c", c=RD), ALU.add).then_inc(rope_r.sem, 1)
                if not last_turn:
                    for b in after:
                        choices(b)
                for gr in range(NG):
                    for b in B:
                        h = b[1]
                        dve.wait_ge(*sc_psum(b, gr + 1))
                        dve.memset(idle_v[:, 2 * gr + h:2 * gr + h + 1], 0.0).then_inc(idle_vr.sem, 1)
                        for k, (o, n) in enumerate(SPAN):
                            dve.max(top1[h][:, k, :], bank[h][o // 512][:, o % 512:o % 512 + n]).then_inc(top1_r.sems[h], 1)
                        dve.wait_ge(*top1_r(b, NT * (gr + 1)))
                        dve.tensor_scalar(nmax[h][:, :], top1[h][:, :, 0], -RD ** -0.5, None, ALU.mult).then_inc(nmax_r.sems[h], 1)
                        for k, (o, n) in enumerate(SPAN):
                            dve.match_replace(rest[h][:, o:o + n], top1[h][:, k, :], bank[h][o // 512][:, o % 512:o % 512 + n], -3.0e38).then_inc(rest_r.sems[h], 1)
                        dve.wait_ge(*rest_r(b, NT * (gr + 1)))
                        for k, (o, n) in enumerate(SPAN):
                            dve.max(top2[h][:, k, :], rest[h][:, o:o + n]).then_inc(top2_r.sems[h], 1)
                        dve.wait_ge(*top2_r(b, NT * (gr + 1)))
                        dve.wait_ge(*exp_r(b, gr + 1))
                        for k, (o, n) in enumerate(SPAN):
                            last = dve.scalar_tensor_tensor(kept[h][:, o:o + n], bank[h][o // 512][:, o % 512:o % 512 + n],
                                                            top2[h][:, k, TOPK - 9:TOPK - 8], exps[h][:, o:o + n], ALU.is_ge, ALU.mult)
                        last.then_inc(kept_r.sems[h], 1)

                def attention_rows(b):
                    h = b[1]
                    dve.wait_ge(*av_r(b))
                    dve.reciprocal(attr[h][:, :, :], att[h][:, :, :, RD]).then_inc(den_r.sem, 1)
                    dve.wait_ge(*den_r(b))
                    dve.tensor_tensor(attn[h][:, :, :].rearrange("p t (a c) -> p t a c", c=RD), att[h][:, :, :, 0:RD],
                                      attr[h][:, :, :].unsqueeze(3).broadcast_to([P, TB, RH, RD]), ALU.mult).then_inc(attn_r.sem, 1)

                def after_attention(b):
                    h = b[1]
                    x = x_all[:, bass.ds(tile_of(b), TB), :]
                    dve.wait_ge(*ao_psum(b))
                    dve.tensor_tensor(x, bank[h][1][:, :].rearrange("p (t d) -> p t d", t=TB), x, ALU.add).then_inc(x4.sem, 1)
                    dve.wait_ge(*x4(b))
                    norm_stats(dve, xt(b), stats, mv, var, N5, b, (1.0 + RMS_EPS, RMS_EPS * LN_EPS))

                def after_patches(b):
                    h = b[1]
                    x = x_all[:, bass.ds(tile_of(b), TB), :]
                    dve.wait_ge(*win_psum(b))
                    dve.wait_ge(*xd(b))
                    dve.tensor_tensor(x, bank[h][1][:, :].rearrange("p (t d) -> p t d", t=TB), x, ALU.add).then_inc(x5.sem, 1)
                    dve.wait_ge(*x5(b))
                    norm_stats(dve, xt(b), stats, mv, var, N6, b)

                def pooled_rows(b):
                    h = b[1]
                    dve.wait_ge(*N6["xts"](b))
                    for c in range(DT):
                        dve.tensor_scalar(pooledb[h][:, c, :], ones[:, :], pooled[h][:, c:c + 1], 1.0 / S, ALU.mult, ALU.mult).then_inc(pb_r.sem, 1)

                def gate(b):
                    h = b[1]
                    dve.wait_ge(*gl_psum(b))
                    dve.tensor_tensor(gl[h][:, :], bank[h][3][:, 0:NE], g["gate_b"][:, :], ALU.add).then_inc(gl_r.sem, 1)
                    dve.wait_ge(*gl_r(b))
                    dve.max(gtop[h][:, :], gl[h][:, :]).then_inc(gtop_r.sem, 1)
                    dve.wait_ge(*gtop_r(b))
                    dve.tensor_scalar(ngt[h][:, :], gtop[h][:, 0:1], -1.0, None, ALU.mult).then_inc(ngt_r.sem, 1)
                    dve.wait_ge(*ge_r(b))
                    dve.scalar_tensor_tensor(gates[h][:, :], gl[h][:, :], gtop[h][:, 1:2], ge[h][:, :], ALU.is_ge, ALU.mult).then_inc(gm_r.sem, 1)
                    dve.wait_ge(*gm_r(b, 1))
                    dve.tensor_reduce(gsum[h][:, :], gates[h][:, :], X, ALU.add).then_inc(gm_r.sem, 1)
                    dve.wait_ge(*gm_r(b, 2))
                    dve.reciprocal(gsum[h][:, :], gsum[h][:, :]).then_inc(gm_r.sem, 1)
                    dve.wait_ge(*gm_r(b, 3))
                    dve.tensor_scalar(gates[h][:, :], gates[h][:, :], gsum[h][:, 0:1], None, ALU.mult).then_inc(gm_r.sem, 1)

                def output(b):
                    h = b[1]
                    dve.wait_ge(*f_psum(b))
                    dve.wait_ge(*y_out(b, 0))
                    dve.tensor_tensor(y[h][:, :, :], bank[h][3][:, :].rearrange("p (t d) -> p t d", t=TB), x_all[:, bass.ds(tile_of(b), TB), :],
                                      ALU.add).then_inc(y_r.sems[h], 1)

                attention_rows(B[0])
                after_attention(B[0])
                attention_rows(B[1])
                norm_apply(dve, xt(B[0]), xn, mv, rstd, N5, B[0])
                after_attention(B[1])
                norm_apply(dve, xt(B[1]), xn, mv, rstd, N5, B[1])
                after_patches(B[0])
                norm_apply(dve, xt(B[0]), xn, mv, rstd, N6, B[0])
                pooled_rows(B[0])
                after_patches(B[1])
                norm_apply(dve, xt(B[1]), xn, mv, rstd, N6, B[1])
                gate(B[0])
                pooled_rows(B[1])
                for n, (e, h) in enumerate(EXPERTS):
                    b = B[h]
                    if (e, h) == (0, 1):
                        gate(b)
                    dve.wait_ge(*e_r(b, e + 1))
                    if e == 0:
                        dve.wait_ge(*gm_r(b))
                        dve.tensor_scalar(acc[h][:, :], hid[h][0][:, :], gates[h][:, 0:1], None, ALU.mult).then_inc(acc_r.sems[h], 1)
                    else:
                        dve.wait_ge(*acc_r(b, e))
                        dve.scalar_tensor_tensor(acc[h][:, :], hid[h][e % NH][:, :], gates[h][:, e:e + 1], acc[h][:, :], ALU.mult, ALU.add).then_inc(acc_r.sems[h], 1)
                    if not last_turn:
                        if n in (4, 6):
                            combine(after[n // 2 - 2])
                        if n in (8, 9):
                            first_stats(after[n - 8])
                        if n in (10, 11):
                            norm_apply(dve, xt(after[n - 10]), xn, mv, rstd, N4, after[n - 10])
                for b in B:
                    output(b)
                finish(dve, dve_own)
                if not last_turn:
                    finish(dve, early_own)

            for h in range(2):
                choices((0, h))
            for h in range(2):
                combine((0, h))
            dve.wait_ge(s_set, 5)
            for h in range(2):
                first_stats((0, h))
            for h in range(2):
                norm_apply(dve, xt((0, h)), xn, mv, rstd, N4, (0, h))
            finish(dve, early_own)
            with dve.Fori(0, PAIRS - 1) as i:
                body(i, False)
            body(PAIRS - 1, True)


def constants():
    import numpy as np

    n = np.arange(1, RD // 2 + 1, dtype=np.float64)
    t = 10.0 + 6.0 * n
    for _ in range(60):
        f = t / (2 * np.pi) * np.log(t / (2 * np.pi * np.e)) - (n - 0.875)
        t = t - f / (np.log(t / (2 * np.pi)) / (2 * np.pi))
    z = t / t[0]
    denom = 0.25 + z * z
    w_re = (0.5 / denom).astype(np.float32).astype(np.float64)
    w_im = (-z / denom).astype(np.float32).astype(np.float64)
    pos = np.arange(S, dtype=np.float32)
    K = RD // 2
    phase = pos[:, None] * (10000.0 ** (-np.arange(K, dtype=np.float32) / K))[None, :]
    cos, sin = np.cos(phase).astype(np.float32).astype(np.float64), np.sin(phase).astype(np.float32).astype(np.float64)
    grow = np.sqrt(1.0 + pos.astype(np.float64))[:, None]
    kc = np.stack([cos, cos], -1) * grow[:, :, None]
    ks = np.stack([sin, -sin], -1) * grow[:, :, None]
    qc1 = w_re * cos + w_im * sin
    qs1 = w_re * sin - w_im * cos
    qc = np.stack([qc1, qc1], -1) / grow[:, :, None]
    qs = np.stack([qs1, -qs1], -1) / grow[:, :, None]
    c_cos = np.concatenate([np.tile(qc.reshape(S, RD), (1, RH)), np.tile(kc.reshape(S, RD), (1, RH))], 1).astype(np.float32)
    c_sin = np.concatenate([np.tile(qs.reshape(S, RD), (1, RH)), np.tile(ks.reshape(S, RD), (1, RH))], 1).astype(np.float32)
    logp = np.float32(-0.001)
    dt = -np.log(-np.expm1(logp))
    decay, first = float(np.exp(-dt)), float(np.exp(logp))
    i, j = np.arange(S)[:, None], np.arange(S)[None, :]
    gap = np.where(j >= i, j - i, 0)
    c_decayT = np.where(j >= i, first * decay ** gap, 0.0)
    pi, pj = np.arange(P)[:, None], np.arange(P)[None, :]
    return {
        "c_ident": np.eye(P, dtype=np.float32),
        "c_before": (pi < pj).astype(np.float32),
        "c_causal": np.where(pj > pi, NEG, 0.0).astype(np.float32),
        "c_cos": c_cos, "c_sin": c_sin,
        "c_decayT": c_decayT.astype(np.float32),
        "c_upto": (i <= j).astype(np.float32),
    }


def kernel(**inputs):
    import numpy as np
    import concourse.bacc as bacc
    from concourse.bass_utils import run_bass_kernel_spmd

    v = {k: np.asarray(x) for k, x in inputs.items()}
    cols = lambda x: x.reshape(-1, P).T
    arrays = {
        "x": v["x"].reshape(NB * S, D), "ctx": v["ctx_2048"].reshape(NB * S, DC),
        "ctxT": v["ctx_2048"].transpose(0, 2, 1).reshape(NB * DC, S),
        "mask": v["mask_BxS2_fk1"].reshape(-1), "maskC": cols(v["mask_BxS2_fk1"].reshape(-1)),
        "patch_lens": v["mask_BxS2_if0"].reshape(-1),
        "L0_xattn_W_srcT": v["L0_xattn_W_src"].T, "L0_xattn_W_tgtT": v["L0_xattn_W_tgt"].T,
        "L0_xattn_W_outT": v["L0_xattn_W_out"].T, "L0_xattn_b_srcC": cols(v["L0_xattn_b_src"]),
        "L0_xattn_b_tgtC": cols(v["L0_xattn_b_tgt"]),
        "L0_ffn_w1": v["L0_ffn_w1"].reshape(NE * D, F), "L0_ffn_w2": v["L0_ffn_w2"].reshape(NE * F, D),
        "L0_ffn_b1C": v["L0_ffn_b1"].reshape(NE, FT, P).transpose(0, 2, 1).reshape(NE * P, FT),
        "L0_ffn_b2": v["L0_ffn_b2"].reshape(-1),
        "L1_xattn_g_resC": cols(v["L1_xattn_g_res"]),
        "L1_xattn_W_inT": v["L1_xattn_W_in"].T,
        "L1_ffn_gate_wT": v["L1_ffn_gate_w"].T,
        "L1_ffn_expert_wT": v["L1_ffn_expert_w"].transpose(2, 0, 1).reshape(D, NE * D),
        "L1_ffn_expert_bC": v["L1_ffn_expert_b"].reshape(NE, DT, P).transpose(2, 0, 1),
    }
    for k in ("L0_attn_Wq", "L0_attn_Wk", "L0_attn_Wv", "L0_attn_Wo", "L0_attn_bo", "L0_xattn_b_src", "L0_xattn_b_out",
              "L0_ffn_w_router", "L0_ffn_b_router", "L1_attn_Wq", "L1_attn_Wk", "L1_attn_Wv", "L1_attn_Wo",
              "L1_xattn_b_in", "L1_xattn_g_init", "L1_ffn_gate_b"):
        arrays[k] = v[k]
    arrays.update(constants())
    nc = bacc.Bacc("TRN2", target_bir_lowering=False, num_devices=1)
    a, feed = {}, {}
    for k, x in arrays.items():
        feed[f"in_{k}"] = np.ascontiguousarray(x)
        a[k] = nc.dram_tensor(f"in_{k}", x.shape, mybir.dt.from_np(x.dtype), kind="ExternalInput").ap()
    a["out"] = nc.dram_tensor("y_dram", (NB * S, D), F32, kind="ExternalOutput").ap()
    decoder(nc, a)
    r = run_bass_kernel_spmd(nc, [feed], core_ids=[0])
    return r.results[0]["y_dram"].reshape(NB, S, D)
```

```python
from contextlib import ExitStack

import concourse.bass as bass
from concourse import mybir

F32 = mybir.dt.float32
BF16 = mybir.dt.bfloat16
I32 = mybir.dt.int32
U32 = mybir.dt.uint32
ALU = mybir.AluOpType
ACT = mybir.ActivationFunctionType
X = mybir.AxisListType.X

P = 128
NB = 8
S = 256
TB = S // P
D = 256
DT = D // P
DC = 512
CT = DC // P
PAIRS = NB // 2
NE = 8
CAP = int(1.25 * NB * S / NE)
F = 1024
FT = F // P
XH, XD = 8, 32
RH, RD = 16, 16
GH = 4
TOPK = 13
NEG = -1.0e30
LN_EPS = 1e-5
RMS_EPS = 1e-5
SLOTS = [(0, 128), (128, 128), (256, CAP - 256)]


class Signal:

    def __init__(self, sem, per):
        self.sem, self.per = sem, per

    def __call__(self, b, j=None):
        i, h = b
        return self.sem, i * (2 * self.per) + (h * self.per + (self.per if j is None else j))


class HalfSignal:

    def __init__(self, sems, per, first=0):
        self.sems, self.per, self.first = sems, per, first

    def __call__(self, b, j=None):
        i, h = b
        return self.sems[h], i * self.per + (self.first + (self.per if j is None else j))


class OwnSignal:

    def __init__(self, sem, per):
        self.sem, self.per = sem, per

    def __call__(self, b, j=None):
        return self.sem, b[1] * self.per + (self.per if j is None else j)


class OwnHalfSignal:

    def __init__(self, sems, per):
        self.sems, self.per = sems, per

    def __call__(self, b, j=None):
        return self.sems[b[1]], self.per if j is None else j


def finish(eng, own):
    for s in own:
        for sem, count in [(s.sem, 2 * s.per)] if isinstance(s, OwnSignal) else [(x, s.per) for x in s.sems]:
            eng.wait_ge(sem, count)
            eng.sem_clear(sem)


def tile_of(b):
    i, h = b
    return i * (2 * TB) + h * TB


def decoder(nc, a):
    with ExitStack() as ctx:
        def sb(name, shape, dt=F32):
            return ctx.enter_context(nc.sbuf_tensor(name, shape, dt))

        def sem(name):
            return ctx.enter_context(nc.semaphore(name))

        g = {}
        bank = [[ctx.enter_context(nc.psum_tensor(f"bank{h}{k}", [P, 512], F32)) for k in range(4)]
                for h in range(2)]
        g["bank"] = bank
        g["x_all"] = sb("x_all", [P, NB * TB, D])
        g["depool_all"] = sb("depool_all", [P, NB * TB, D])
        g["choice_w"] = sb("choice_w", [P, NB * TB, 2])
        g["choice_row"] = sb("choice_row", [P, NB * TB, 2], U32)
        g["identf"] = sb("identf", [P, P])
        g["identb"] = sb("identb", [P, P], BF16)
        for name, shape in (("qkv_w", [P, DT, 768]), ("attn_out_w", [P, DT, D]), ("win_w", [P, DT, D]),
                            ("gate_w", [P, DT, NE]), ("rope_cos", [P, TB, 512]), ("rope_sin", [P, TB, 512]),
                            ("b_in", [P, D]), ("gate_b", [P, NE]), ("g_res", [P, DT]),
                            ("expert_b", [P, NE, DT]), ("expert_w", [P, DT, NE * D])):
            g[name] = sb("l1_" + name, shape)
        g["s_l1"] = sem("layer1_constants_loaded")
        for name, per, first in (("sent", 64, 64), ("p_in", 32, 0), ("got_in", 64, 0)):
            g[name] = HalfSignal([sem(f"{name}{h}") for h in range(2)], per, first)
        g["slots"] = nc.dram_tensor("slots", (NE * CAP, D), F32, kind="Internal").ap()
        g["expert_rows"] = nc.dram_tensor("expert_rows", (NE * CAP, D), F32, kind="Internal").ap()
        g["w1_in"] = HalfSignal([sem(f"w1_loaded{h}") for h in range(2)], 16)
        with ExitStack() as early:
            g["w1"] = [early.enter_context(nc.sbuf_tensor(f"w1{h}", [P, DT, F], F32)) for h in range(2)]
            for part in (layer0, experts):
                used = []
                part(nc, a, g, used)
                clear(nc, used)
        layer1(nc, a, g, [])


def clear(nc, used):
    nums = sorted(s.num for s in used)
    while nums:
        n = 1
        while n < len(nums) and nums[n] == nums[0] + n:
            n += 1
        nc.sync.sem_clear(range(nums[0], nums[0] + n))
        nums = nums[n:]
    nc.all_engine_barrier()


def norm_stats(dve, x, stats, mv, var, got, b, scale_add=(1.0, LN_EPS)):
    h = b[1]
    for t in range(TB):
        dve.bn_stats(stats[h][:, t, :], x(t)).then_inc(got["stats"].sem, 1)
    for t in range(TB):
        dve.wait_ge(*got["stats"](b, t + 1))
        dve.bn_aggr(mv[h][:, t, :], stats[h][:, t, :]).then_inc(got["mv"].sem, 1)
    dve.wait_ge(*got["mv"](b))
    dve.tensor_scalar(var[h][:, :], mv[h][:, :, 1], *scale_add, ALU.mult, ALU.add).then_inc(got["var"].sem, 1)


def norm_apply(dve, x, xn, mv, rstd, got, b):
    h = b[1]
    dve.wait_ge(*got["rstd"](b))
    for t in range(TB):
        dve.tensor_scalar(xn[h][:, t, :], x(t), mv[h][:, t, 0:1], rstd[h][:, t:t + 1],
                          ALU.subtract, ALU.mult).then_inc(got["xn"].sem, 1)


def transpose_rows(pe, out, rows, ident, cols=DT):
    for c in range(cols):
        for t in range(TB):
            last = pe.transpose(out[:, c * S + t * P:c * S + (t + 1) * P], rows[:, t, c * P:(c + 1) * P], ident[:, :])
    return last


def load_w1(sp, a, g, n, h):
    sp.dma_start(g["w1"][h][:, :, :], a["L0_ffn_w1"][bass.ds(n * D, D), :].rearrange("(c p) f -> p c f", p=P)).then_inc(g["w1_in"].sems[h], 16)


def layer0(nc, a, g, used):
    with ExitStack() as ctx:
        def sb(name, shape, dt=F32):
            return ctx.enter_context(nc.sbuf_tensor(name, shape, dt))

        def sb2(name, shape, dt=F32):
            return [sb(f"{name}{h}", shape, dt) for h in range(2)]

        def sem(name):
            used.append(ctx.enter_context(nc.semaphore(name)))
            return used[-1]

        def sig(name, per):
            return Signal(sem(name), per)

        def turns(name, per):
            return HalfSignal([sem(f"{name}{h}") for h in range(2)], per)

        dve_own, late_own, early_own = [], [], []
        idle_r, idle_nr, idle_sr = OwnSignal(sem("pool_idle"), 1), OwnSignal(sem("pool_idle_early"), 1), OwnSignal(sem("pool_idle_slots"), 1)

        def own(name, per):
            dve_own.append(OwnSignal(sem(name), per))
            return dve_own[-1]

        def late(name, per):
            late_own.append(OwnSignal(sem(name), per))
            return late_own[-1]

        def own_turns(name, per):
            dve_own.append(OwnHalfSignal([sem(f"{name}{h}") for h in range(2)], per))
            return dve_own[-1]

        def early(name, per):
            early_own.append(OwnSignal(sem(name), per))
            return early_own[-1]

        def norm_signals(name, own=own):
            return {"stats": own(name + "_stats", TB), "mv": own(name + "_mv", TB), "var": sig(name + "_var", 1),
                    "rstd": sig(name + "_rstd", 1), "xn": sig(name + "_xn", TB), "xt": sig(name + "_xt_psum", 1),
                    "xts": sig(name + "_xt", 1)}

        bank, x_all = g["bank"], g["x_all"]
        identf, identb = g["identf"], g["identb"]

        qv_w = sb("qv_w", [P, DT, 512])
        k_w = sb("k_w", [P, DT, D])
        lin_out_w = sb("lin_out_w", [P, DT, D])
        src_w = sb("src_w", [P, CT, 512])
        tgt_w = sb("tgt_w", [P, DT, D])
        out_w = sb("out_w", [P, 2 * DT, D])
        router_w = sb("router_w", [P, DT, NE])
        lin_b = sb("lin_b", [P, D])
        val_b = sb("val_b", [P, D])
        out_b = sb("out_b", [P, D])
        key_b = sb("key_b", [P, DT])
        tgt_b = sb("tgt_b", [P, DT])
        router_b = sb("router_b", [P, NE])
        before = sb("before", [P, P])
        beforeb = sb("beforeb", [P, P], BF16)
        onesb = sb("onesb", [P, P], BF16)
        idle = sb("idle_a", [P, 6])
        mhalf = sb("mhalf", [P, TB])
        zeros = sb("zeros", [P, 640])
        expert_ids = sb("expert_ids", [P, 4, NE])

        stats, mv = sb2("stats", [P, TB, 6]), sb2("mv", [P, TB, 2])
        var, rstd = sb2("var", [P, TB]), sb2("rstd", [P, TB])
        xn, xnT = sb2("xn", [P, TB, D]), sb2("xnT", [P, DT * S])
        routed = sb2("routed", [P, TB, D])
        probs, probsT = sb2("probs", [P, GH, S]), sb2("probsT", [P, 2, 512])
        kE, qE = [x[:, 0:DT, :] for x in probs], [x[:, DT:2 * DT, :] for x in probs]
        kmax, ksum = sb2("kmax", [P, DT]), sb2("ksum", [P, DT])
        qmax, qsum = sb2("qmax", [P, TB]), sb2("qsum", [P, TB])
        krec, qrec = sb2("krec", [P, DT]), sb2("qrec", [P, TB])
        v_lin, kN = [[x[:, k, :].rearrange("p (t d) -> p t d", t=TB) for x in probsT] for k in range(2)]
        qT, ctxT, kvo = sb2("qT", [P, DT * S]), sb2("ctxT", [P, DT, D]), sb2("kvo", [P, DT, D])
        src = sb2("src", [P, CT, S])
        mask_row, mask_col = sb2("mask_row", [P, S]), sb2("mask_col", [P, TB])
        mask_bias = sb2("mask_bias", [P, S], BF16)
        xk, xq = sb2("xk", [P, DT, S]), sb2("xq", [P, DT, S])
        vb = sb2("vb", [P, TB, D])
        xv = sb2("xv", [P, TB, D])
        smax = sb2("smax", [P, 4, GH])
        nmax = sb2("nmax", [P, 4, GH])
        kraw = sb2("kraw", [P, DT, S])
        den = sb2("den", [P, 4, GH])
        updT = sb2("updT", [P, DT * S])
        routedT = updT
        logit = sb2("logit", [P, TB, NE])
        top, topi = sb2("top", [P, TB, 8]), sb2("topi", [P, TB, 8], U32)
        topf = sb2("topf", [P, TB, 2])
        tope, tsum = sb2("tope", [P, TB, 8]), sb2("tsum", [P, TB])
        ntop = sb2("ntop", [P, TB])
        oneh = sb2("oneh", [P, TB, 2, NE])
        ohb = sb2("ohb", [P, TB, NE], BF16)
        carry = sb("carry", [P, NE])
        taken = sb2("taken", [P, TB, NE])
        posm, pos = sb2("posm", [P, TB, 2, NE]), sb2("pos", [P, TB, 2])
        keep, over = sb2("keep", [P, TB, 2]), sb2("over", [P, TB, 2])
        rowf, posc = sb2("rowf", [P, TB, 2]), sb2("posc", [P, TB, 2])
        slotf = sb2("slotf", [P, TB, 2])
        slot = sb2("slot", [P, 2 * TB], U32)
        wk, ws = sb2("wk", [P, TB, 2]), sb2("ws", [P, TB])

        s_first, s_const, s_cast = sem("first_constants_loaded"), sem("layer0_constants_loaded"), sem("constants_cast")
        s_x, s_rest = sem("first_x_loaded"), sem("other_x_loaded")
        s_zero, s_set = sem("zeros_set"), sem("memsets_done")
        src_in = HalfSignal([sem(f"src_loaded{h}") for h in range(2)], 16)
        mask_in = HalfSignal([sem(f"masks_loaded{h}") for h in range(2)], 32)
        N1, N2, N3 = norm_signals("n1", early), norm_signals("n2"), norm_signals("n3")
        key_psum, qv_psum = sig("key_psum", 1), sig("qv_psum", TB)
        kmax_r, qmax_r = sig("kmax_r", 2), sig("qmax_r", 2)
        kexp, qexp, vlin_r = sig("kexp", DT), sig("qexp", TB), sig("vlin_r", TB)
        kN_psum, kN_r = sig("kN_psum", 1), sig("kN_r", 1)
        qT_psum, qT_r = sig("qT_psum", 1), sig("qT_r", 1)
        ctx_psum, ctx_r = sig("ctx_psum", 1), sig("ctx_r", 1)
        rec_r, kvo_psum, kvo_r = own("rec_r", 3), sig("kvo_psum", 1), sig("kvo_r", DT)
        lin_psum, xb1 = sig("lin_psum", 1), sig("x_plus_lin_bias", 1)
        x1 = own("x1_ready", TB)
        xk_psum, xk_r, xv_psum = sig("xk_psum", 1), sig("xk_r", DT), sig("xv_psum", 1)
        kraw_r, vb_r, xv_r, mb_r = sig("kraw_r", DT), sig("vb_r", 1), sig("xv_r", TB), sig("mask_bias_r", 1)
        xq_psum, xq_r = sig("xq_psum", 1), sig("xq_r", DT)
        sc_psum, smax_r, nmax_r = turns("scores_psum", 4), own_turns("smax_r", 4), turns("nmax_r", 4)
        pexp, pT_psum, pT_a, pT_v = turns("pexp", 4 * GH), turns("probsT_psum", 4), turns("probsT_act", 4), turns("probsT_dve", 4)
        den_r, pnorm = own_turns("den_r", 4), turns("probs_normed", 4)
        updT_psum, updT_r = sig("updT_psum", 1), sig("updT_r", 1)
        xb2, xo_psum, x2 = sig("x_plus_out_bias", 1), sig("xout_psum", 1), own("x2_ready", TB)
        lg_psum, lg_r, top_r, topi_r = sig("logit_psum", 1), late("logit_r", 1), late("top_r", TB), late("topi_r", TB)
        topf_r, oh_r, ohb_r = late("topf_r", 2), late("oneh_r", 2 * TB), sig("ohb_r", 1)
        cnt_psum, taken_r, carry_r = sig("count_psum", 1), late("taken_r", 1), sig("carry_r", 1)
        posm_r, pos_r, route_r = late("posm_r", 2), late("pos_r", 1), late("route_r", 8)
        texp, slot_r, ntop_r = sig("texp", TB), sig("slot_r", 1), sig("ntop_r", 1)
        sent = g["sent"]
        wgt_r = late("weights_r", 5)

        block = ctx.enter_context(nc.Block())

        def load(eng, out, src_ap, s, bc=False):
            eng.dma_start(out, src_ap.partition_broadcast(P) if bc else src_ap).then_inc(s, 16)

        KT = "(c p) n -> p c n"
        sync_loads = [
            (k_w[:, :, :], a["L0_attn_Wk"].rearrange(KT, p=P)), (qv_w[:, :, 0:D], a["L0_attn_Wq"].rearrange(KT, p=P)),
            (qv_w[:, :, D:2 * D], a["L0_attn_Wv"].rearrange(KT, p=P)),
        ]
        first_loads = [
            (identf[:, :], a["c_ident"]),
            (lin_b[:, :], a["L0_attn_bo"].partition_broadcast(P)), (val_b[:, :], a["L0_xattn_b_src"][D:2 * D].partition_broadcast(P)),
            (out_b[:, :], a["L0_xattn_b_out"].partition_broadcast(P)), (router_b[:, :], a["L0_ffn_b_router"].partition_broadcast(P)),
            (key_b[:, :], a["L0_xattn_b_srcC"][:, 0:DT]), (tgt_b[:, :], a["L0_xattn_b_tgtC"]),
        ]
        const_loads = [
            (lin_out_w[:, :, :], a["L0_attn_Wo"].rearrange(KT, p=P)),
            (src_w[:, :, :], a["L0_xattn_W_srcT"].rearrange(KT, p=P)), (tgt_w[:, :, :], a["L0_xattn_W_tgtT"].rearrange(KT, p=P)),
            (out_w[:, :, :], a["L0_xattn_W_outT"].rearrange(KT, p=P)), (router_w[:, :, :], a["L0_ffn_w_router"].rearrange(KT, p=P)),
            (before[:, :], a["c_before"]),
        ]
        layer1_loads = [
            (g["qkv_w"][:, :, 0:D], a["L1_attn_Wq"].rearrange(KT, p=P)), (g["qkv_w"][:, :, D:2 * D], a["L1_attn_Wk"].rearrange(KT, p=P)),
            (g["qkv_w"][:, :, 2 * D:3 * D], a["L1_attn_Wv"].rearrange(KT, p=P)), (g["attn_out_w"][:, :, :], a["L1_attn_Wo"].rearrange(KT, p=P)),
            (g["win_w"][:, :, :], a["L1_xattn_W_inT"].rearrange(KT, p=P)), (g["gate_w"][:, :, :], a["L1_ffn_gate_wT"].rearrange(KT, p=P)),
            (g["rope_cos"][:, :, :], a["c_cos"].rearrange("(t p) n -> p t n", p=P)),
            (g["rope_sin"][:, :, :], a["c_sin"].rearrange("(t p) n -> p t n", p=P)),
            (g["b_in"][:, :], a["L1_xattn_b_in"].partition_broadcast(P)), (g["gate_b"][:, :], a["L1_ffn_gate_b"].partition_broadcast(P)),
            (g["g_res"][:, :], a["L1_xattn_g_resC"]), (g["expert_b"][:, :, :], a["L1_ffn_expert_bC"]),
            (g["expert_w"][:, :, :], a["L1_ffn_expert_wT"].rearrange(KT, p=P)),
        ]
        g["n_l1"] = 16 * len(layer1_loads)
        n_first, n_const = 16 * len(sync_loads + first_loads), 16 * len(const_loads)
        x_tiles = a["x"].rearrange("(t p) d -> p t d", p=P)
        slots = g["slots"]

        @block.sync
        def _(sp):
            def load_src(n, h):
                sp.dma_start(src[h][:, :, :], a["ctxT"][bass.ds(n * DC, DC), :].rearrange("(c p) s -> p c s", p=P)).then_inc(src_in.sems[h], 16)

            def load_masks(n, h):
                sp.dma_start(mask_row[h][:, :], a["mask"][bass.ds(n * S, S)].partition_broadcast(P)).then_inc(mask_in.sems[h], 16)
                sp.dma_start(mask_col[h][:, :], a["maskC"][:, bass.ds(n * TB, TB)]).then_inc(mask_in.sems[h], 16)

            sp.dma_start(x_all[:, 0:4, :], x_tiles[:, 0:4, :]).then_inc(s_x, 16)
            for out, src_ap in sync_loads:
                sp.dma_start(out, src_ap).then_inc(s_first, 16)
            for h in range(2):
                load_src(h, h)
                load_masks(h, h)
            with sp.Fori(0, PAIRS - 1) as i:
                for h in range(2):
                    sp.wait_ge(*xv_psum((i, h)))
                    load_src(i * 2 + (h + 2), h)
                for h in range(2):
                    sp.wait_ge(*xk_r((i, h)))
                    sp.wait_ge(*xq_r((i, h)))
                    sp.wait_ge(*xv_r((i, h)))
                    sp.wait_ge(*mb_r((i, h)))
                    load_masks(i * 2 + (h + 2), h)
            for h in range(2):
                load_w1(sp, a, g, h, h)

        @block.gpsimd
        def _(pool):
            pool.memset(zeros[:, :], 0.0).then_inc(s_zero, 1)
            pool.memset(mhalf[:, :], -0.5).then_inc(s_set, 1)
            pool.memset(onesb[:, :], 1.0).then_inc(s_set, 1)
            pool.memset(carry[:, :], 0.0).then_inc(s_set, 1)
            pool.iota(expert_ids[:, :, :], [[0, 4], [1, NE]], base=0, channel_multiplier=0,
                      allow_small_or_imprecise_dtypes=True).then_inc(s_set, 1)
            pool.wait_ge(s_zero, 1)
            for q in range(8):
                pool.dma_start(slots[q * CAP:(q + 1) * CAP, :].rearrange("r d -> (r d)").rearrange("(p x) -> p x", p=P),
                               zeros[:, :]).then_inc(sent.sems[q % 2], 16)
            pool.wait_ge(s_set, 4)
            pool.wait_ge(s_first, n_first)
            pool.wait_ge(s_x, 16)

            def power(N, b):
                pool.wait_ge(*N["var"](b))
                pool.tensor_tensor(rstd[b[1]][:, :], var[b[1]][:, :], mhalf[:, :], ALU.pow).then_inc(N["rstd"].sem, 1)

            def plus_lin_bias(b):
                x = x_all[:, bass.ds(tile_of(b), TB), :]
                pool.wait_ge(*N1["xn"](b))
                pool.tensor_tensor(idle[:, b[1]:b[1] + 1], mhalf[:, 0:1], mhalf[:, 0:1], ALU.add).then_inc(idle_nr.sem, 1)
                pool.tensor_tensor(x, x, lin_b[:, :].unsqueeze(1).broadcast_to([P, TB, D]), ALU.add).then_inc(xb1.sem, 1)

            def to_slots(b):
                h = b[1]
                pool.wait_ge(*slot_r(b))
                pool.wait_ge(sent.sems[0], sent.first)
                pool.wait_ge(sent.sems[1], sent.first)
                pool.tensor_tensor(idle[:, 4 + h:5 + h], mhalf[:, 0:1], mhalf[:, 0:1], ALU.add).then_inc(idle_sr.sem, 1)
                for t in range(TB):
                    for k in range(2):
                        pool.indirect_dma_start(
                            out=slots, out_offset=bass.IndirectOffsetOnAxis(ap=slot[h][:, 2 * t + k:2 * t + k + 1], axis=0),
                            in_=routed[h][:, t, :], in_offset=None, bounds_check=NE * CAP - 1, oob_is_err=False,
                        ).then_inc(sent.sems[h], 16)

            def body(i, first_turn, last_turn):
                B, last, after = [(i, 0), (i, 1)], [(i - 1, 0), (i - 1, 1)], [(i + 1, 0), (i + 1, 1)]
                for b in B:
                    power(N2, b)
                if not first_turn:
                    for b in last:
                        to_slots(b)
                    finish(pool, [idle_sr])
                for b in B:
                    h = b[1]
                    pool.wait_ge(*vb_r(b))
                    pool.wait_ge(*mask_in(b))
                    for t in range(TB):
                        pool.tensor_tensor(xv[h][:, t, :], vb[h][:, t, :], mask_col[h][:, t:t + 1].broadcast_to([P, D]),
                                           ALU.mult).then_inc(xv_r.sem, 1)
                for b in B:
                    x = x_all[:, bass.ds(tile_of(b), TB), :]
                    pool.wait_ge(*N2["xn"](b))
                    pool.tensor_tensor(idle[:, 2 * 1 + b[1]:2 * 1 + b[1] + 1], mhalf[:, 0:1], mhalf[:, 0:1], ALU.add).then_inc(idle_r.sem, 1)
                    pool.tensor_tensor(x, x, out_b[:, :].unsqueeze(1).broadcast_to([P, TB, D]), ALU.add).then_inc(xb2.sem, 1)
                if not last_turn:
                    for b in after:
                        power(N1, b)
                for b in B:
                    power(N3, b)
                if not last_turn:
                    for b in after:
                        plus_lin_bias(b)
                    finish(pool, [idle_nr])
                finish(pool, [idle_r])

            for h in range(2):
                power(N1, (0, h))
            for h in range(2):
                plus_lin_bias((0, h))
            finish(pool, [idle_nr])
            pool.wait_ge(s_rest, 48)
            body(0, True, False)
            with pool.Fori(1, PAIRS - 1) as i:
                body(i, False, False)
            body(PAIRS - 1, False, True)
            for h in range(2):
                to_slots((PAIRS - 1, h))
            for h in range(2):
                pool.wait_ge(*sent((PAIRS - 1, h)))

        @block.scalar
        def _(act):
            for out, src_ap in first_loads:
                act.dma_start(out, src_ap).then_inc(s_first, 16)
            for out, src_ap in const_loads:
                act.dma_start(out, src_ap).then_inc(s_const, 16)
            for q in range(1, 4):
                act.dma_start(x_all[:, 4 * q:4 * q + 4, :], x_tiles[:, 4 * q:4 * q + 4, :]).then_inc(s_rest, 16)

            def evac(out, psum, waits, done):
                for w in waits:
                    act.wait_ge(*w)
                act.activation(out, psum, ACT.Copy).then_inc(done, 1)

            def routed_turned(b):
                evac(routedT[b[1]][:, :], bank[b[1]][0][:, :], [N3["xt"](b)], N3["xts"].sem)

            def top_exps(b):
                h = b[1]
                act.wait_ge(*ntop_r(b))
                for t in range(TB):
                    act.activation(tope[h][:, t, :], top[h][:, t, :], ACT.Exp, bias=ntop[h][:, t:t + 1],
                                   accum_out=tsum[h][:, t:t + 1]).then_inc(texp.sem, 1)

            def body(i, first_turn):
                B, last = [(i, 0), (i, 1)], [(i - 1, 0), (i - 1, 1)]
                for b in B:
                    evac(xnT[b[1]][:, :], bank[b[1]][0][:, :], [N1["xt"](b)], N1["xts"].sem)
                for b in B:
                    h = b[1]
                    if not first_turn:
                        routed_turned(last[h])
                    act.wait_ge(*kmax_r(b))
                    for c in range(DT):
                        act.activation(kE[h][:, c, :], bank[h][1][:, c * S:(c + 1) * S], ACT.Exp, bias=kmax[h][:, c:c + 1],
                                       accum_out=ksum[h][:, c:c + 1]).then_inc(kexp.sem, 1)
                for b in B:
                    h = b[1]
                    act.wait_ge(*qmax_r(b))
                    for t in range(TB):
                        act.activation(qE[h][:, t, :], bank[h][2 + t][:, 0:D], ACT.Exp, bias=qmax[h][:, t:t + 1],
                                       accum_out=qsum[h][:, t:t + 1]).then_inc(qexp.sem, 1)
                    for t in range(TB):
                        act.activation(v_lin[h][:, t, :], bank[h][2 + t][:, D:2 * D], ACT.Copy).then_inc(vlin_r.sem, 1)
                if not first_turn:
                    for b in last:
                        top_exps(b)
                for b in B:
                    evac(qT[b[1]][:, :], bank[b[1]][0][:, :], [qT_psum(b)], qT_r.sem)
                for b in B:
                    evac(ctxT[b[1]][:, :, :].rearrange("p a c -> p (a c)"), bank[b[1]][2][:, :], [ctx_psum(b)], ctx_r.sem)
                for b in B:
                    evac(xnT[b[1]][:, :], bank[b[1]][2][:, :], [N2["xt"](b)], N2["xts"].sem)

                def exps(b, ch):
                    h = b[1]
                    act.wait_ge(*nmax_r(b, ch + 1))
                    for j in range(GH):
                        act.activation(probs[h][:, j, :], bank[h][j // 2][:, (j % 2) * S:(j % 2 + 1) * S], ACT.Exp,
                                       bias=nmax[h][:, ch, j:j + 1], scale=XD ** -0.5, accum_out=den[h][:, ch, j:j + 1]).then_inc(pexp.sems[h], 1)

                steps = [(b, ch) for ch in range(4) for b in B]
                exps(*steps[0])
                for n, (b, ch) in enumerate(steps):
                    evac(probsT[b[1]][:, 0, :], bank[b[1]][0][:, :], [pT_psum(b, ch + 1)], pT_a.sems[b[1]])
                    if n + 1 < len(steps):
                        exps(*steps[n + 1])
                for b in B:
                    evac(updT[b[1]][:, :], bank[b[1]][2][:, :], [updT_psum(b)], updT_r.sem)

            body(0, True)
            act.wait_ge(s_first, n_first)
            act.wait_ge(s_const, n_const)
            act.activation(identb[:, :], identf[:, :], ACT.Copy).then_inc(s_cast, 1)
            act.activation(beforeb[:, :], before[:, :], ACT.Copy).then_inc(s_cast, 1)
            for out, src_ap in layer1_loads:
                act.dma_start(out, src_ap).then_inc(g["s_l1"], 16)
            with act.Fori(1, PAIRS - 1) as i:
                body(i, False)
            body(PAIRS - 1, False)
            for step in (routed_turned, top_exps):
                for h in range(2):
                    step((PAIRS - 1, h))

        @block.tensor
        def _(pe):
            pe.wait_ge(s_first, n_first)
            pe.wait_ge(s_set, 4)

            def counts(b):
                h = b[1]
                o = bank[h][0]
                pe.wait_ge(*ohb_r(b))
                pe.matmul(o[:, 0:NE], beforeb[:, :], ohb[h][:, 0, :], start=True, stop=True)
                pe.matmul(o[:, NE:2 * NE], onesb[:, :], ohb[h][:, 0, :], start=True, stop=False)
                pe.matmul(o[:, NE:2 * NE], beforeb[:, :], ohb[h][:, 1, :], start=False, stop=True)
                pe.matmul(o[:, 2 * NE:3 * NE], onesb[:, :], ohb[h][:, 0, :], start=True, stop=False)
                pe.matmul(o[:, 2 * NE:3 * NE], onesb[:, :], ohb[h][:, 1, :], start=False, stop=True).then_inc(cnt_psum.sem, 1)

            def turn_routed(b):
                h = b[1]
                pe.wait_ge(*N3["xn"](b))
                transpose_rows(pe, bank[h][0], routed[h], identf).then_inc(N3["xt"].sem, 1)

            def router_logits(b):
                h = b[1]
                pe.wait_ge(*N3["xts"](b))
                for t in range(TB):
                    for k in range(DT):
                        last = pe.matmul(bank[h][0][:, t * NE:(t + 1) * NE], routedT[h][:, k * S + t * P:k * S + (t + 1) * P],
                                         router_w[:, k, :], start=(k == 0), stop=(k == DT - 1))
                last.then_inc(lg_psum.sem, 1)

            def source_keys(b, k, c):
                h = b[1]
                for q in range(CT):
                    last = pe.matmul(bank[h][k][:, c * S:(c + 1) * S], src_w[:, q, c * P:(c + 1) * P], src[h][:, q, :],
                                     start=(q == 0), stop=(q == CT - 1))
                if c == DT - 1:
                    last.then_inc(xk_psum.sem, 1)

            def source_values(b, t):
                h = b[1]
                for q in range(CT):
                    last = pe.matmul(bank[h][3][:, t * D:(t + 1) * D], src[h][:, q, t * P:(t + 1) * P], src_w[:, q, D:2 * D],
                                     start=(q == 0), stop=(q == CT - 1))
                if t == TB - 1:
                    last.then_inc(xv_psum.sem, 1)

            def body(i, first_turn, last_turn):
                B, last_pair, after = [(i, 0), (i, 1)], [(i - 1, 0), (i - 1, 1)], [(i + 1, 0), (i + 1, 1)]
                for b in B:
                    pe.wait_ge(*N1["xn"](b))
                    transpose_rows(pe, bank[b[1]][0], xn[b[1]], identf).then_inc(N1["xt"].sem, 1)
                for b in B:
                    h = b[1]
                    pe.wait_ge(*N1["xts"](b))
                    if not first_turn:
                        pe.wait_ge(*N3["var"](last_pair[h]))
                    for c in range(DT):
                        for k in range(DT):
                            last = pe.matmul(bank[h][1][:, c * S:(c + 1) * S], k_w[:, k, c * P:(c + 1) * P],
                                             xnT[h][:, k * S:(k + 1) * S], start=(k == 0), stop=(k == DT - 1))
                    last.then_inc(key_psum.sem, 1)
                    if not first_turn:
                        turn_routed(last_pair[h])
                        pe.wait_ge(*(kraw_r if h else vb_r)(b))
                    for t in range(TB):
                        for k in range(DT):
                            last = pe.matmul(bank[h][2 + t][:, :], xnT[h][:, k * S + t * P:k * S + (t + 1) * P],
                                             qv_w[:, k, :], start=(k == 0), stop=(k == DT - 1))
                        last.then_inc(qv_psum.sem, 1)
                    if not first_turn:
                        router_logits(last_pair[h])
                for b in B:
                    h = b[1]
                    pe.wait_ge(*kexp(b))
                    for t in range(TB):
                        for c in range(DT):
                            last = pe.transpose(bank[h][1][:, t * D + c * P:t * D + (c + 1) * P],
                                                kE[h][:, c, t * P:(t + 1) * P], identf[:, :])
                    last.then_inc(kN_psum.sem, 1)
                if not first_turn:
                    for b in last_pair:
                        pe.wait_ge(*ntop_r(b))
                for b in B:
                    pe.wait_ge(*qexp(b))
                    transpose_rows(pe, bank[b[1]][0], qE[b[1]], identf).then_inc(qT_psum.sem, 1)
                for b in B:
                    h = b[1]
                    pe.wait_ge(*kN_r(b))
                    pe.wait_ge(*vlin_r(b))
                    for e in range(DT):
                        for t in range(TB):
                            last = pe.matmul(bank[h][2][:, e * D:(e + 1) * D], v_lin[h][:, t, e * P:(e + 1) * P], kN[h][:, t, :],
                                             start=(t == 0), stop=(t == TB - 1))
                    last.then_inc(ctx_psum.sem, 1)
                if not first_turn:
                    for b in B:
                        pe.wait_ge(*qT_r(b))
                        counts(last_pair[b[1]])
                if first_turn:
                    pe.wait_ge(s_const, n_const)
                for b in B:
                    h = b[1]
                    pe.wait_ge(*ctx_r(b))
                    for d in range(DT):
                        for e in range(DT):
                            last = pe.matmul(bank[h][3][:, d * D:(d + 1) * D], ctxT[h][:, e, d * P:(d + 1) * P], lin_out_w[:, e, :],
                                             start=(e == 0), stop=(e == DT - 1))
                    last.then_inc(kvo_psum.sem, 1)
                for b in B:
                    h = b[1]
                    pe.wait_ge(*kvo_r(b))
                    pe.wait_ge(*qT_r(b))
                    for t in range(TB):
                        for d in range(DT):
                            last = pe.matmul(bank[h][1][:, t * D:(t + 1) * D], qT[h][:, d * S + t * P:d * S + (t + 1) * P],
                                             kvo[h][:, d, :], start=(d == 0), stop=(d == DT - 1))
                    last.then_inc(lin_psum.sem, 1)
                if first_turn:
                    for b in B:
                        pe.wait_ge(*src_in(b))
                        for c in range(DT):
                            source_keys(b, 0, c)
                        for t in range(TB):
                            source_values(b, t)
                if not first_turn:
                    pe.wait_ge(*kraw_r(B[1]))
                    for t in range(TB):
                        source_values(B[1], t)
                for b in B:
                    pe.wait_ge(*N2["xn"](b))
                    transpose_rows(pe, bank[b[1]][2], xn[b[1]], identf).then_inc(N2["xt"].sem, 1)
                for b in B:
                    h = b[1]
                    pe.wait_ge(*N2["xts"](b))
                    for c in range(DT):
                        for k in range(DT):
                            last = pe.matmul(bank[h][1][:, c * S:(c + 1) * S], tgt_w[:, k, c * P:(c + 1) * P],
                                             xnT[h][:, k * S:(k + 1) * S], start=(k == 0), stop=(k == DT - 1))
                    last.then_inc(xq_psum.sem, 1)

                def head(c, j):
                    return j % 2 * (P // XD) + 2 * c + j // 2

                def scores(b, ch):
                    h, t, c = b[1], ch // 2, ch % 2
                    if ch == 0:
                        pe.wait_ge(*mb_r(b))
                        pe.wait_ge(*xk_r(b))
                        pe.wait_ge(*xq_r(b))
                    else:
                        pe.wait_ge(*pT_a(b, ch))
                        pe.wait_ge(*pT_v(b, ch))
                    for j in range(GH):
                        f, r = divmod(head(c, j), P // XD)
                        r0 = XD * r
                        o = bank[h][j // 2][:, (j % 2) * S:(j % 2 + 1) * S]
                        pe.matmul(o, onesb[r0:r0 + 1, :], mask_bias[h][r0:r0 + 1, :], start=True, stop=False)
                        last = pe.matmul(o, xq[h][r0:r0 + XD, f, t * P:(t + 1) * P], xk[h][r0:r0 + XD, f, :],
                                         start=False, stop=True)
                    last.then_inc(sc_psum.sems[h], 1)

                def turn(b, ch):
                    h = b[1]
                    pe.wait_ge(*pnorm(b, ch + 1))
                    for j in range(GH):
                        for s in range(TB):
                            last = pe.transpose(bank[h][j // 2][:, ((j % 2) * TB + s) * P:((j % 2) * TB + s + 1) * P],
                                                probs[h][:, j, s * P:(s + 1) * P], identf[:, :])
                    last.then_inc(pT_psum.sems[h], 1)

                def values(b, ch):
                    h, t, c = b[1], ch // 2, ch % 2
                    pe.wait_ge(*pT_a(b, ch + 1))
                    pe.wait_ge(*pT_v(b, ch + 1))
                    if ch == 0:
                        pe.wait_ge(*xv_r(b))
                    for j, s in [(j, s) for first in (0, 1) for s in range(TB) for j in (first, first + 2)]:
                        hd = head(c, j)
                        f, r = divmod(hd, P // XD)
                        last = pe.matmul(bank[h][2][XD * r:XD * (r + 1), f * S + t * P:f * S + (t + 1) * P],
                                         xv[h][:, s, hd * XD:(hd + 1) * XD],
                                         probsT[h][:, j // 2, ((j % 2) * TB + s) * P:((j % 2) * TB + s + 1) * P],
                                         start=(s == 0), stop=(s == TB - 1))
                    if ch == 3:
                        last.then_inc(updT_psum.sem, 1)

                steps = [(b, ch) for ch in range(4) for b in B]
                scores(*steps[0])
                scores(*steps[1])
                for n, (b, ch) in enumerate(steps):
                    turn(b, ch)
                    if n:
                        values(*steps[n - 1])
                    if ch < 3:
                        scores(b, ch + 1)
                    if not last_turn:
                        ahead = after[b[1]]
                        if ch == 0:
                            pe.wait_ge(*src_in(ahead))
                            if b[1]:
                                pe.wait_ge(*vb_r(b))
                        if ch < 2:
                            source_keys(ahead, 3, ch)
                        elif b[1] == 0:
                            pe.wait_ge(*kraw_r(ahead))
                            source_values(ahead, ch - 2)
                values(*steps[-1])
                for b in B:
                    h = b[1]
                    pe.wait_ge(*updT_r(b))
                    for t in range(TB):
                        for k in range(2 * DT):
                            left = (xnT if k < DT else updT)[h]
                            last = pe.matmul(bank[h][1][:, t * D:(t + 1) * D], left[:, (k % DT) * S + t * P:(k % DT) * S + (t + 1) * P],
                                             out_w[:, k, :], start=(k == 0), stop=(k == 2 * DT - 1))
                    last.then_inc(xo_psum.sem, 1)

            body(0, True, False)
            pe.wait_ge(s_cast, 2)
            with pe.Fori(1, PAIRS - 1) as i:
                body(i, False, False)
            body(PAIRS - 1, False, True)
            for step in (turn_routed, router_logits, counts):
                for h in range(2):
                    step((PAIRS - 1, h))

        @block.vector
        def _(dve):
            dve.wait_ge(s_x, 16)
            dve.wait_ge(s_first, n_first)
            dve.wait_ge(s_set, 4)

            def xt(b):
                return lambda t: x_all[:, bass.ds(tile_of(b) + t, 1), :].rearrange("p a d -> p (a d)")

            def logits(b):
                h = b[1]
                dve.wait_ge(*lg_psum(b))
                dve.tensor_tensor(logit[h][:, :, :], bank[h][0][:, 0:TB * NE].rearrange("p (t e) -> p t e", t=TB),
                                  router_b[:, :].unsqueeze(1).broadcast_to([P, TB, NE]), ALU.add).then_inc(lg_r.sem, 1)

            def choose(b):
                h = b[1]
                dve.wait_ge(*lg_r(b))
                for t in range(TB):
                    dve.max(top[h][:, t, :], logit[h][:, t, :]).then_inc(top_r.sem, 1)
                dve.wait_ge(*top_r(b))
                for t in range(TB):
                    dve.max_index(topi[h][:, t, :], top[h][:, t, :], logit[h][:, t, :]).then_inc(topi_r.sem, 1)
                dve.tensor_scalar(ntop[h][:, :], top[h][:, :, 0], -1.0, None, ALU.mult).then_inc(ntop_r.sem, 1)
                dve.wait_ge(*topi_r(b))
                dve.tensor_copy(topf[h][:, :, :], topi[h][:, :, 0:2]).then_inc(topf_r.sem, 2)
                dve.wait_ge(*topf_r(b))
                for t in range(TB):
                    for k in range(2):
                        dve.tensor_scalar(oneh[h][:, t, k, :], expert_ids[:, 0, :], topf[h][:, t, k:k + 1], None,
                                          ALU.is_equal).then_inc(oh_r.sem, 1)
                dve.wait_ge(*oh_r(b))
                dve.tensor_tensor(ohb[h][:, :, :], oneh[h][:, :, 0, :], oneh[h][:, :, 1, :], ALU.add).then_inc(ohb_r.sem, 1)

            def slots_taken(b):
                h = b[1]
                dve.wait_ge(*cnt_psum(b))
                dve.tensor_tensor(taken[h][:, :, :], bank[h][0][:, 0:TB * NE].rearrange("p (t e) -> p t e", t=TB),
                                  carry[:, :].unsqueeze(1).broadcast_to([P, TB, NE]), ALU.add).then_inc(taken_r.sem, 1)
                dve.wait_ge(*taken_r(b))
                dve.tensor_tensor(carry[:, :], carry[:, :], bank[h][0][:, 2 * NE:3 * NE], ALU.add).then_inc(carry_r.sem, 1)
                dve.wait_ge(*carry_r(b))

            def places(b):
                h = b[1]
                for t in range(TB):
                    dve.tensor_tensor(posm[h][:, t, :, :], oneh[h][:, t, :, :], taken[h][:, t, :].unsqueeze(1).broadcast_to([P, 2, NE]),
                                      ALU.mult).then_inc(posm_r.sem, 1)
                dve.wait_ge(*posm_r(b))
                dve.tensor_reduce(pos[h][:, :, :], posm[h][:, :, :, :], X, ALU.add).then_inc(pos_r.sem, 1)
                dve.wait_ge(*pos_r(b))
                dve.tensor_scalar(keep[h][:, :, :], pos[h][:, :, :], float(CAP), None, ALU.is_lt).then_inc(route_r.sem, 1)
                dve.tensor_scalar(over[h][:, :, :], pos[h][:, :, :], float(CAP), 4.0 * NE * CAP, ALU.is_ge, ALU.mult).then_inc(route_r.sem, 1)
                dve.tensor_scalar(posc[h][:, :, :], pos[h][:, :, :], float(CAP - 1), None, ALU.min).then_inc(route_r.sem, 1)
                dve.wait_ge(*route_r(b, 3))
                dve.scalar_tensor_tensor(rowf[h][:, :, :], topf[h][:, :, :], float(CAP), posc[h][:, :, :], ALU.mult, ALU.add).then_inc(route_r.sem, 1)
                dve.wait_ge(*route_r(b, 4))
                dve.tensor_tensor(slotf[h][:, :, :], rowf[h][:, :, :], over[h][:, :, :], ALU.add).then_inc(route_r.sem, 1)
                dve.wait_ge(*route_r(b, 5))
                dve.tensor_copy(slot[h][:, :], slotf[h][:, :, :].rearrange("p t k -> p (t k)")).then_inc(slot_r.sem, 1)
                dve.tensor_copy(g["choice_row"][:, bass.ds(tile_of(b), TB), :], rowf[h][:, :, :]).then_inc(route_r.sem, 1)
                dve.wait_ge(*texp(b))
                dve.reciprocal(ws[h][:, :], tsum[h][:, :]).then_inc(wgt_r.sem, 1)
                dve.tensor_tensor(wk[h][:, :, :], tope[h][:, :, 0:2], keep[h][:, :, :], ALU.mult).then_inc(wgt_r.sem, 1)
                dve.wait_ge(*wgt_r(b, 2))
                dve.tensor_tensor(wk[h][:, :, :], wk[h][:, :, :], ws[h][:, :].unsqueeze(2).broadcast_to([P, TB, 2]), ALU.mult).then_inc(wgt_r.sem, 1)
                dve.wait_ge(*wgt_r(b, 3))
                dve.tensor_reduce(ws[h][:, :], wk[h][:, :, :], X, ALU.add).then_inc(wgt_r.sem, 1)
                dve.wait_ge(*wgt_r(b, 4))
                dve.tensor_scalar(ws[h][:, :], ws[h][:, :], 1e-6, None, ALU.max).then_inc(wgt_r.sem, 1)
                dve.wait_ge(*wgt_r(b, 5))
                dve.reciprocal(ws[h][:, :], ws[h][:, :]).then_inc(route_r.sem, 1)
                dve.wait_ge(*route_r(b, 7))
                dve.tensor_tensor(g["choice_w"][:, bass.ds(tile_of(b), TB), :], wk[h][:, :, :],
                                  ws[h][:, :].unsqueeze(2).broadcast_to([P, TB, 2]), ALU.mult).then_inc(route_r.sem, 1)

            def keys_out(b, k):
                h = b[1]
                dve.wait_ge(*xk_psum(b))
                for c in range(DT):
                    dve.tensor_scalar(kraw[h][:, c, :], bank[h][k][:, c * S:(c + 1) * S], key_b[:, c:c + 1], None, ALU.add).then_inc(kraw_r.sem, 1)

            def masked_keys(b):
                h = b[1]
                dve.wait_ge(*kraw_r(b))
                dve.wait_ge(*mask_in(b))
                dve.tensor_tensor(xk[h][:, :, :], kraw[h][:, :, :], mask_row[h][:, :].unsqueeze(1).broadcast_to([P, DT, S]),
                                  ALU.mult).then_inc(xk_r.sem, DT)

            def values_out(b):
                h = b[1]
                dve.wait_ge(*xv_psum(b))
                dve.tensor_tensor(vb[h][:, :, :], bank[h][3][:, :].rearrange("p (t d) -> p t d", t=TB),
                                  val_b[:, :].unsqueeze(1).broadcast_to([P, TB, D]), ALU.add).then_inc(vb_r.sem, 1)

            def body(i, first_turn, last_turn):
                B, last_pair, after = [(i, 0), (i, 1)], [(i - 1, 0), (i - 1, 1)], [(i + 1, 0), (i + 1, 1)]
                for b in B:
                    h = b[1]
                    dve.wait_ge(*key_psum(b))
                    dve.tensor_reduce(kmax[h][:, :], bank[h][1][:, :].rearrange("p (c s) -> p c s", c=DT), X, ALU.max, negate=True).then_inc(kmax_r.sem, 2)
                    for t in range(TB):
                        dve.wait_ge(*qv_psum(b, t + 1))
                        dve.tensor_reduce(qmax[h][:, t:t + 1], bank[h][2 + t][:, 0:D], X, ALU.max, negate=True).then_inc(qmax_r.sem, 1)
                    if not first_turn:
                        logits(last_pair[h])
                        choose(last_pair[h])
                for b in B:
                    h = b[1]
                    dve.wait_ge(*kN_psum(b))
                    dve.tensor_copy(kN[h][:, :, :].rearrange("p t d -> p (t d)"), bank[h][1][:, :]).then_inc(kN_r.sem, 1)
                    dve.wait_ge(*qexp(b))
                    dve.reciprocal(krec[h][:, :], ksum[h][:, :]).then_inc(rec_r.sem, 1)
                    dve.reciprocal(qrec[h][:, :], qsum[h][:, :]).then_inc(rec_r.sem, 1)
                    dve.wait_ge(*rec_r(b, 2))
                    dve.tensor_scalar(qrec[h][:, :], qrec[h][:, :], 0.25 / D, None, ALU.mult).then_inc(rec_r.sem, 1)
                if not first_turn:
                    for b in B:
                        masked_keys(b)
                for b in B:
                    h = b[1]
                    dve.wait_ge(*kvo_psum(b))
                    for d in range(DT):
                        dve.tensor_scalar(kvo[h][:, d, :], bank[h][3][:, d * D:(d + 1) * D], krec[h][:, d:d + 1], None,
                                          ALU.mult).then_inc(kvo_r.sem, 1)
                if not first_turn:
                    for b in last_pair:
                        slots_taken(b)
                for b in B:
                    h = b[1]
                    dve.wait_ge(*mask_in(b))
                    dve.tensor_scalar(mask_bias[h][:, :], mask_row[h][:, :], 0.0, NEG, ALU.is_equal, ALU.mult).then_inc(mb_r.sem, 1)
                for b in B:
                    h = b[1]
                    dve.wait_ge(*lin_psum(b))
                    dve.wait_ge(*xb1(b))
                    dve.wait_ge(*rec_r(b))
                    for t in range(TB):
                        dve.scalar_tensor_tensor(xt(b)(t), bank[h][1][:, t * D:(t + 1) * D], qrec[h][:, t:t + 1], xt(b)(t),
                                                 ALU.mult, ALU.add).then_inc(x1.sem, 1)
                for b in B:
                    dve.wait_ge(*x1(b))
                    norm_stats(dve, xt(b), stats, mv, var, N2, b)
                for b in B:
                    norm_apply(dve, xt(b), xn, mv, rstd, N2, b)
                if not first_turn:
                    places(last_pair[0])
                for b in B:
                    h = b[1]
                    if first_turn:
                        keys_out(b, 0)
                        values_out(b)
                        masked_keys(b)
                for b in B:
                    h = b[1]
                    dve.wait_ge(*xq_psum(b))
                    for c in range(DT):
                        dve.scalar_tensor_tensor(xq[h][:, c, :], bank[h][1][:, c * S:(c + 1) * S], tgt_b[:, c:c + 1], mask_row[h][:, :],
                                                 ALU.add, ALU.mult).then_inc(xq_r.sem, 1)
                if not first_turn:
                    values_out(B[1])

                def maxima(b, ch):
                    h = b[1]
                    dve.wait_ge(*sc_psum(b, ch + 1))
                    for q in range(2):
                        last = dve.tensor_reduce(smax[h][:, ch, 2 * q:2 * q + 2], bank[h][q][:, :].rearrange("p (c s) -> p c s", c=2), X, ALU.max)
                    last.then_inc(smax_r.sems[h], 1)
                    dve.wait_ge(*smax_r(b, ch + 1))
                    dve.tensor_scalar(nmax[h][:, ch, :], smax[h][:, ch, :], -XD ** -0.5, None, ALU.mult).then_inc(nmax_r.sems[h], 1)

                def normed(b, ch):
                    h = b[1]
                    dve.wait_ge(*pexp(b, GH * (ch + 1)))
                    dve.reciprocal(den[h][:, ch, :], den[h][:, ch, :]).then_inc(den_r.sems[h], 1)
                    dve.wait_ge(*den_r(b, ch + 1))
                    for j in range(GH):
                        last = dve.tensor_scalar(probs[h][:, j, :], probs[h][:, j, :], den[h][:, ch, j:j + 1], None, ALU.mult)
                    last.then_inc(pnorm.sems[h], 1)

                steps = [(b, ch) for ch in range(4) for b in B]
                maxima(*steps[0])
                normed(*steps[0])
                for n, (b, ch) in enumerate(steps):
                    h = b[1]
                    if n + 1 < len(steps):
                        maxima(*steps[n + 1])
                    if n == 1 and not first_turn:
                        places(last_pair[1])
                    dve.wait_ge(*pT_psum(b, ch + 1))
                    dve.tensor_copy(probsT[h][:, 1, :], bank[h][1][:, :]).then_inc(pT_v.sems[h], 1)
                    if not last_turn:
                        if n in (3, 4):
                            keys_out(after[n - 3], 3)
                        if n == 7:
                            values_out(after[0])
                    if n + 1 < len(steps):
                        normed(*steps[n + 1])
                if not last_turn:
                    for b in after:
                        norm_stats(dve, xt(b), stats, mv, var, N1, b)
                    for b in after:
                        norm_apply(dve, xt(b), xn, mv, rstd, N1, b)
                    finish(dve, early_own)

                def after_sources(b):
                    h = b[1]
                    dve.wait_ge(*xo_psum(b))
                    dve.wait_ge(*xb2(b))
                    x = x_all[:, bass.ds(tile_of(b), TB), :]
                    dve.tensor_tensor(x, bank[h][1][:, :].rearrange("p (t d) -> p t d", t=TB), x, ALU.add).then_inc(x2.sem, TB)
                    dve.wait_ge(*x2(b))
                    norm_stats(dve, xt(b), stats, mv, var, N3, b)

                def routed_rows(b):
                    dve.wait_ge(*sent(b, 0))
                    norm_apply(dve, xt(b), routed, mv, rstd, N3, b)

                after_sources(B[0])
                routed_rows(B[0])
                after_sources(B[1])
                routed_rows(B[1])
                finish(dve, dve_own)
                if not first_turn:
                    finish(dve, late_own)

            for h in range(2):
                norm_stats(dve, xt((0, h)), stats, mv, var, N1, (0, h))
            for h in range(2):
                norm_apply(dve, xt((0, h)), xn, mv, rstd, N1, (0, h))
            finish(dve, early_own)
            dve.wait_ge(s_rest, 48)
            body(0, True, False)
            with dve.Fori(1, PAIRS - 1) as i:
                body(i, False, False)
            body(PAIRS - 1, False, True)
            last_pair = [(PAIRS - 1, 0), (PAIRS - 1, 1)]
            for step in (logits, choose, slots_taken, places):
                for b in last_pair:
                    step(b)


def experts(nc, a, g, used):
    with ExitStack() as ctx:
        def sb(name, shape, dt=F32):
            return ctx.enter_context(nc.sbuf_tensor(name, shape, dt))

        def sb2(name, shape, dt=F32):
            return [sb(f"{name}{h}", shape, dt) for h in range(2)]

        def sem(name):
            used.append(ctx.enter_context(nc.semaphore(name)))
            return used[-1]

        def sig(name, per):
            return Signal(sem(name), per)

        def turns(name, per):
            return HalfSignal([sem(f"{name}{h}") for h in range(2)], per)

        bank, identf = g["bank"], g["identf"]
        w1, w2 = g["w1"], sb2("w2", [P, FT, D])
        b1, b2 = sb2("b1", [P, FT]), sb2("b2", [P, D])
        rows, rowsT = sb2("rows", [P, len(SLOTS), D]), sb2("rowsT", [P, DT, CAP])
        hid, outr = sb2("hid", [P, FT, CAP]), sb2("outr", [P, len(SLOTS), D])
        decayT, upto = sb("decayT", [P, TB, S]), sb("upto", [P, TB, S])
        uptob, ones = sb("uptob", [P, TB, S], BF16), sb("ones", [P, P])
        place, zero = sb("place", [P, TB]), sb("zero", [P, S])
        g_init, mhalf = sb("g_init", [P, D]), sb("mhalf_m", [P, TB])
        lens = sb2("lens", [P, S], I32)
        patch, square = sb2("patch", [P, TB, DC]), sb2("square", [P, TB, DC])
        lensf, ends, wrap = sb2("lensf", [P, S]), sb2("ends", [P, S]), sb2("wrap", [P, S])
        hit, hits = sb2("hit", [P, TB, S]), sb2("hits", [P, TB])
        edge = sb2("edge", [P, TB, P], BF16)
        plug, pick = sb2("plug", [P, S]), sb2("pick", [P, TB, S])
        ssum, msq, rrms = sb2("ssum", [P, TB]), sb2("msq", [P, TB]), sb2("rrms", [P, TB])
        u, state = sb2("u", [P, TB, D]), sb2("state", [P, TB, D])

        s_const, s_set, s_cast = sem("experts_constants_loaded"), sem("m_memsets_done"), sem("m_cast")
        rows_in = HalfSignal([sem(f"rows_loaded{h}") for h in range(2)], 48)
        w1_in = g["w1_in"]
        w2_in = HalfSignal([sem(f"w2_loaded{h}") for h in range(2)], 32)
        p_in = g["p_in"]
        out_sent = HalfSignal([sem(f"expert_rows_stored{h}") for h in range(2)], 32, 1)
        rt_psum, rt_r = sig("rowsT_psum", 1), sig("rowsT_r", DT)
        h_psum, h_r = turns("hidden_psum", FT), turns("hidden_r", FT)
        o_psum, o_r = sig("expert_out_psum", 3), sig("expert_out_r", 3)
        sq_r, ms_r, rr_r, u_r = sig("square_r", TB), sig("msq_r", 1), sig("rrms_r", 1), sig("u_r", TB)
        ends_r, hit_r, edge_r = sig("ends_r", 4), sig("hit_r", TB), sig("edge_r", TB + 1)
        cs_psum, plug_r, pick_r = sig("edge_count_psum", 1), sig("plug_r", 1), sig("pick_r", TB)
        st_psum, st_r, dp_psum = sig("state_psum", 1), sig("state_r", 1), sig("depool_psum", 1)
        dp_done = HalfSignal([sem(f"depool_r{h}") for h in range(2)], 1, 1)
        n_const = 16 * 3
        EDGE_J = 5
        block = ctx.enter_context(nc.Block())
        slots, expert_rows = g["slots"], g["expert_rows"]

        @block.sync
        def _(sp):
            def load_rows(n, h):
                got = rows_in.sems[h]
                sp.dma_start(b1[h][:, :], a["L0_ffn_b1C"][bass.ds(n * P, P), :]).then_inc(got, 16)
                sp.dma_start(rows[h][:, 0:2, :], slots[bass.ds(n * CAP, 2 * P), :].rearrange("(t p) d -> p t d", p=P)).then_inc(got, 16)
                sp.dma_start(rows[h][0:CAP - 2 * P, 2, :], slots[bass.ds(n * CAP + 2 * P, CAP - 2 * P), :]).then_inc(got, 16)

            def load_second(n, h):
                got = w2_in.sems[h]
                sp.dma_start(b2[h][:, :], a["L0_ffn_b2"][bass.ds(n * D, D)].partition_broadcast(P)).then_inc(got, 16)
                sp.dma_start(w2[h][:, :, :], a["L0_ffn_w2"][bass.ds(n * F, F), :].rearrange("(c p) d -> p c d", p=P)).then_inc(got, 16)

            def store(n, h):
                done = out_sent.sems[h]
                sp.dma_start(expert_rows[bass.ds(n * CAP, 2 * P), :].rearrange("(t p) d -> p t d", p=P), outr[h][:, 0:2, :]).then_inc(done, 16)
                sp.dma_start(expert_rows[bass.ds(n * CAP + 2 * P, CAP - 2 * P), :], outr[h][0:CAP - 2 * P, 2, :]).then_inc(done, 16)

            for h in range(2):
                sp.sem_inc(out_sent.sems[h], out_sent.first)
                sp.sem_inc(dp_done.sems[h], dp_done.first)
                load_rows(h, h)
            for h in range(2):
                load_second(h, h)
            with sp.Fori(0, PAIRS - 1) as i:
                for h in range(2):
                    sp.wait_ge(*h_r((i, h)))
                    load_rows(i * 2 + (h + 2), h)
                    load_w1(sp, a, g, i * 2 + (h + 2), h)
                for h in range(2):
                    sp.wait_ge(*o_r((i, h)))
                    store(i * 2 + h, h)
                    load_second(i * 2 + (h + 2), h)
            for h in range(2):
                sp.wait_ge(*o_r((PAIRS - 1, h)))
                store(NE - 2 + h, h)
            for h in range(2):
                sp.wait_ge(*out_sent((PAIRS - 1, h)))

        @block.gpsimd
        def _(pool):
            pool.memset(mhalf[:, :], -0.5).then_inc(s_set, 1)
            pool.memset(zero[:, :], 0.0).then_inc(s_set, 1)
            pool.memset(ones[:, :], 1.0).then_inc(s_set, 1)
            pool.iota(place[:, :], [[P, TB]], base=0, channel_multiplier=1, allow_small_or_imprecise_dtypes=True).then_inc(s_set, 1)

            def load(n, h):
                pool.dma_start(lens[h][:, :], a["patch_lens"][bass.ds(n * S, S)].partition_broadcast(P)).then_inc(p_in.sems[h], 16)
                pool.dma_start(patch[h][:, :, :], a["ctx"][bass.ds(n * S, S), :].rearrange("(t p) d -> p t d", p=P)).then_inc(p_in.sems[h], 16)

            for h in range(2):
                load(h, h)
            pool.wait_ge(s_set, 4)

            def power(b):
                pool.wait_ge(*ms_r(b))
                pool.tensor_tensor(rrms[b[1]][:, :], msq[b[1]][:, :], mhalf[:, :], ALU.pow).then_inc(rr_r.sem, 1)

            with pool.Fori(0, PAIRS - 1) as i:
                B = [(i, 0), (i, 1)]
                for b in B:
                    power(b)
                for b in B:
                    pool.wait_ge(*ends_r(b))
                    pool.wait_ge(*u_r(b))
                    pool.wait_ge(*sq_r(b))
                    load(i * 2 + (b[1] + 2), b[1])
            for h in range(2):
                power((PAIRS - 1, h))

        @block.scalar
        def _(act):
            KT = "(c p) n -> p c n"
            act.dma_start(upto[:, :, :], a["c_upto"].rearrange(KT, p=P)).then_inc(s_const, 16)
            act.dma_start(g_init[:, :], a["L1_xattn_g_init"][0:D].partition_broadcast(P)).then_inc(s_const, 16)
            act.dma_start(decayT[:, :, :], a["c_decayT"].rearrange(KT, p=P)).then_inc(s_const, 16)
            act.wait_ge(s_const, n_const)
            act.activation(uptob[:, :, :], upto[:, :, :], ACT.Copy).then_inc(s_cast, 1)
            with act.Fori(0, PAIRS) as i:
                B = [(i, 0), (i, 1)]
                for b in B:
                    h = b[1]
                    act.wait_ge(*p_in(b))
                    for t in range(TB):
                        act.activation(square[h][:, t, :], patch[h][:, t, :], ACT.Square, accum_out=ssum[h][:, t:t + 1]).then_inc(sq_r.sem, 1)
                for j in range(FT):
                    for b in B:
                        h = b[1]
                        act.wait_ge(*h_psum(b, j + 1))
                        act.activation(hid[h][:, j, :], bank[h][j % 4][:, 0:CAP], ACT.Gelu, bias=b1[h][:, j:j + 1]).then_inc(h_r.sems[h], 1)
                for b in B:
                    act.wait_ge(*st_psum(b))
                    act.activation(state[b[1]][:, :, :].rearrange("p t d -> p (t d)"), bank[b[1]][3][:, :], ACT.Copy).then_inc(st_r.sem, 1)

        @block.tensor
        def _(pe):
            with pe.Fori(0, PAIRS) as i:
                B = [(i, 0), (i, 1)]
                for b in B:
                    h = b[1]
                    pe.wait_ge(*rows_in(b))
                    for c in range(DT):
                        for t, (s0, n) in enumerate(SLOTS):
                            last = pe.transpose(bank[h][c][:, s0:s0 + n], rows[h][0:n, t, c * P:(c + 1) * P], identf[0:n, 0:n])
                    last.then_inc(rt_psum.sem, 1)
                for j in range(FT):
                    if j == EDGE_J:
                        pe.wait_ge(s_cast, 1)
                        for b in B:
                            h = b[1]
                            pe.wait_ge(*edge_r(b))
                            pe.wait_ge(*h_r(b, 4))
                            for t in range(TB):
                                last = pe.matmul(bank[h][3][:, 0:S], edge[h][:, t, :], uptob[:, t, :], start=(t == 0), stop=(t == TB - 1))
                            last.then_inc(cs_psum.sem, 1)
                    for b in B:
                        h = b[1]
                        if j == 0:
                            pe.wait_ge(*rt_r(b))
                            pe.wait_ge(*w1_in(b))
                        if j == 3:
                            pe.wait_ge(*dp_done(b, 0))
                        if j == FT - 1:
                            pe.wait_ge(*plug_r(b))
                        if j >= 4:
                            pe.wait_ge(*h_r(b, j - 3))
                        for c in range(DT):
                            last = pe.matmul(bank[h][j % 4][:, 0:CAP], w1[h][:, c, j * P:(j + 1) * P], rowsT[h][:, c, :],
                                             start=(c == 0), stop=(c == DT - 1))
                        last.then_inc(h_psum.sems[h], 1)
                for b in B:
                    h = b[1]
                    pe.wait_ge(*u_r(b))
                    pe.wait_ge(*h_r(b))
                    for t in range(TB):
                        for q in range(t + 1):
                            last = pe.matmul(bank[h][3][:, t * D:(t + 1) * D], decayT[:, q, t * P:(t + 1) * P], u[h][:, q, :],
                                             start=(q == 0), stop=(q == t))
                    last.then_inc(st_psum.sem, 1)
                for b in B:
                    h = b[1]
                    for t, (s0, n) in enumerate(SLOTS):
                        if t == 0:
                            pe.wait_ge(*w2_in(b))
                        for j in range(FT):
                            last = pe.matmul(bank[h][t][0:n, 0:D], hid[h][:, j, s0:s0 + n], w2[h][:, j, :],
                                             start=(j == 0), stop=(j == FT - 1))
                        last.then_inc(o_psum.sem, 1)
                for b in B:
                    h = b[1]
                    pe.wait_ge(*st_r(b))
                    pe.wait_ge(*pick_r(b))
                    for t in range(TB):
                        for q in range(TB):
                            last = pe.matmul(bank[h][3][:, t * D:(t + 1) * D], pick[h][:, q, t * P:(t + 1) * P], state[h][:, q, :],
                                             start=(q == 0), stop=(q == TB - 1))
                    last.then_inc(dp_psum.sem, 1)
                for b in B:
                    pe.wait_ge(*o_r(b))

        @block.vector
        def _(dve):
            dve.wait_ge(g["s_l1"], g["n_l1"])
            with dve.Fori(0, PAIRS) as i:
                B = [(i, 0), (i, 1)]
                for b in B:
                    h = b[1]
                    dve.wait_ge(*rt_psum(b))
                    for c in range(DT):
                        dve.tensor_copy(rowsT[h][:, c, :], bank[h][c][:, 0:CAP]).then_inc(rt_r.sem, 1)
                dve.wait_ge(s_const, n_const)
                dve.wait_ge(s_set, 4)
                for b in B:
                    h = b[1]
                    dve.wait_ge(*p_in(b))
                    dve.tensor_copy(lensf[h][:, :], lens[h][:, :]).then_inc(ends_r.sem, 1)
                    dve.wait_ge(*ends_r(b, 1))
                    dve.tensor_tensor_scan(ends[h][:, :], lensf[h][:, :], zero[:, :], -1.0, ALU.add, ALU.add).then_inc(ends_r.sem, 1)
                    dve.wait_ge(*ends_r(b, 2))
                    dve.tensor_scalar(wrap[h][:, :], ends[h][:, :], 0.0, float(S), ALU.is_lt, ALU.mult).then_inc(ends_r.sem, 1)
                    dve.wait_ge(*ends_r(b, 3))
                    dve.tensor_tensor(ends[h][:, :], ends[h][:, :], wrap[h][:, :], ALU.add).then_inc(ends_r.sem, 1)
                    dve.wait_ge(*ends_r(b, 4))
                    for t in range(TB):
                        dve.tensor_scalar(hit[h][:, t, :], ends[h][:, :], place[:, t:t + 1], None, ALU.is_equal).then_inc(hit_r.sem, 1)
                    dve.wait_ge(*hit_r(b))
                    dve.tensor_reduce(hits[h][:, :], hit[h][:, :, :], X, ALU.max).then_inc(edge_r.sem, 1)
                    dve.wait_ge(*edge_r(b, 1))
                    for t in range(TB):
                        dve.tensor_scalar(edge[h][:, t, :], ones[:, :], hits[h][:, t:t + 1], None, ALU.mult).then_inc(edge_r.sem, 1)
                for b in B:
                    h = b[1]
                    dve.wait_ge(*sq_r(b))
                    dve.tensor_scalar(msq[h][:, :], ssum[h][:, :], 1.0 / DC, 1e-5, ALU.mult, ALU.add).then_inc(ms_r.sem, 1)
                for b in B:
                    h = b[1]
                    dve.wait_ge(*cs_psum(b))
                    dve.tensor_scalar(plug[h][:, :], bank[h][3][:, 0:S], -1.0, 0.0, ALU.add, ALU.max).then_inc(plug_r.sem, 1)
                    dve.wait_ge(*plug_r(b))
                    for t in range(TB):
                        dve.tensor_scalar(pick[h][:, t, :], plug[h][:, :], place[:, t:t + 1], None, ALU.is_equal).then_inc(pick_r.sem, 1)
                for b in B:
                    h = b[1]
                    dve.wait_ge(*rr_r(b))
                    for t in range(TB):
                        dve.scalar_tensor_tensor(u[h][:, t, :], patch[h][:, t, 0:D], rrms[h][:, t:t + 1], g_init[:, :],
                                                 ALU.mult, ALU.mult).then_inc(u_r.sem, 1)
                for b in B:
                    h = b[1]
                    dve.wait_ge(*out_sent(b, 0))
                    for t, (s0, n) in enumerate(SLOTS):
                        dve.wait_ge(*o_psum(b, t + 1))
                        dve.tensor_tensor(outr[h][0:n, t, :], bank[h][t][0:n, 0:D], b2[h][0:n, :], ALU.add).then_inc(o_r.sem, 1)
                for b in B:
                    h = b[1]
                    dve.wait_ge(*dp_psum(b))
                    dve.tensor_tensor(g["depool_all"][:, bass.ds(tile_of(b), TB), :], bank[h][3][:, :].rearrange("p (t d) -> p t d", t=TB),
                                      g["b_in"][:, :].unsqueeze(1).broadcast_to([P, TB, D]), ALU.add).then_inc(dp_done.sems[h], 1)


def layer1(nc, a, g, used):
    with ExitStack() as ctx:
        def sb(name, shape, dt=F32):
            return ctx.enter_context(nc.sbuf_tensor(name, shape, dt))

        def sb2(name, shape, dt=F32):
            return [sb(f"{name}{h}", shape, dt) for h in range(2)]

        def sem(name):
            used.append(ctx.enter_context(nc.semaphore(name)))
            return used[-1]

        def sig(name, per):
            return Signal(sem(name), per)

        def turns(name, per):
            return HalfSignal([sem(f"{name}{h}") for h in range(2)], per)

        dve_own, early_own = [], []
        idle_r, idle_gr = OwnSignal(sem("pool_idle_b"), 1), OwnSignal(sem("pool_idle_gather"), 1)

        def own(name, per):
            dve_own.append(OwnSignal(sem(name), per))
            return dve_own[-1]

        def own_turns(name, per):
            dve_own.append(OwnHalfSignal([sem(f"{name}{h}") for h in range(2)], per))
            return dve_own[-1]

        def early(name, per):
            early_own.append(OwnSignal(sem(name), per))
            return early_own[-1]

        def norm_signals(name, own=own):
            return {"stats": own(name + "_stats", TB), "mv": own(name + "_mv", TB), "var": sig(name + "_var", 1),
                    "rstd": sig(name + "_rstd", 1), "xn": sig(name + "_xn", TB), "xt": sig(name + "_xt_psum", 1),
                    "xts": sig(name + "_xt", DT)}

        bank, x_all, identf, identb = g["bank"], g["x_all"], g["identf"], g["identb"]
        NG = RH // GH
        NT = 2 * GH
        W1, W0 = GH * S, GH * P
        SPAN = [(k * S, S) if k < GH else (W1 + (k - GH) * P, P) for k in range(NT)]

        causal, causalb = sb("causal", [P, P]), sb("causalb", [P, P], BF16)
        mhalf = sb("mhalf_b", [P, TB])
        rows_i, wts = sb2("rows_i", [P, TB * 2], U32), sb2("wts", [P, TB, 2])
        got = sb2("got", [P, TB * 2, D])
        stats, mv = sb2("stats_b", [P, TB, 6]), sb2("mv_b", [P, TB, 2])
        var, rstd = sb2("var_b", [P, TB]), sb2("rstd_b", [P, TB])
        xn, xnT = sb2("xn_b", [P, TB, D]), sb2("xnT_b", [P, DT * S])
        qk, turned = sb2("qk", [P, TB, 512]), sb2("turned", [P, TB, 512])
        shared = sb2("shared", [P, 2 * (W1 + W0)])
        roped = [shared[h][:, 0:TB * 2 * RH * 32].rearrange("p (t a c) -> p t a c", t=TB, a=2 * RH) for h in range(2)]
        vals = sb2("vals", [P, TB, RH, 32])
        qkT = sb2("qkT", [P, NG, 2, S])
        top1, top2 = sb2("top1", [P, NT, 8]), sb2("top2", [P, NT, 8])
        nmax = sb2("nmax_b", [P, NT])
        rest, keptT = [x[:, 0:W1 + W0] for x in shared], [x[:, W1 + W0:2 * (W1 + W0)] for x in shared]
        exps, kept = sb2("exps", [P, W1 + W0]), sb2("kept", [P, W1 + W0])
        att, attr, attn = sb2("att", [P, TB, RH, RD + 1]), sb2("attr", [P, TB, RH]), xn
        attT = sb2("attT", [P, DT * S])
        outT = [attT[h][:, 0:S] for h in range(2)]
        idle, idle_v = sb("idle", [P, 4]), sb("idle_v", [P, 2 * NG])
        pooled, pooledb = sb2("pooled", [P, DT]), sb2("pooledb", [P, DT, P])
        ones = sb("ones_b", [P, P])
        gl, gtop, ngt = sb2("gl", [P, NE]), sb2("gtop", [P, 8]), sb2("ngt", [P, 1])
        ge, gates, gsum = sb2("ge", [P, NE]), sb2("gates", [P, NE]), sb2("gsum", [P, 1])
        NH = 3
        hid = [[sb(f"hid_b{h}{k}", [P, 512])[:, :] for k in range(NH - 1)] + [turned[h][:, 1, :]] for h in range(2)]
        acc, y = [turned[h][:, 0, :] for h in range(2)], sb2("y", [P, TB, D])

        idle_vr = own("dve_idle", NG)
        s_half, s_zero, s_set, s_const, s_cast = sem("minus_half_set"), sem("pads_zeroed"), sem("b_memsets_done"), sem("causal_loaded"), sem("causal_cast")
        idx_r, wts_r = sig("rows_i_r", 1), early("wts_r", 1)
        got_in = g["got_in"]
        comb = early("combined", 2 * TB)
        N4, N5, N6 = norm_signals("n4", early), norm_signals("n5"), norm_signals("n6")
        qk_psum, v_psum, qk_r, v_r = sig("qk_psum", TB), sig("v_psum", 1), sig("qk_r", TB), sig("v_r", TB)
        rope_a, rope_r = own("rope_parts", TB * 3), sig("roped_r", TB)
        qkT_psum, qkT_r = sig("qkT_psum", NG), sig("qkT_r", NG)
        sc_psum = turns("scores_b_psum", NG)
        top1_r, nmax_r = own_turns("top1_r", NG * NT), turns("nmax_b_r", NG)
        rest_r, top2_r = own_turns("rest_r", NG * NT), own_turns("top2_r", NG * NT)
        exp_r = turns("exps_r", NG)
        kept_r = turns("kept_r", NG * NT)
        KEEP, KEPT_FOR = (0, 4, 1, 5, 2, 3, 6, 7), (4, 7, 8)
        kT_psum, kT_r = turns("keptT_psum", NG * 3), turns("keptT_r", NG * 3)
        oT_psum, oT_r, av_psum, av_r = turns("outT_psum", NG), turns("outT_r", NG), turns("att_psum", NG), turns("att_r", NG)
        den_r, attn_r = own("att_recip", 1), sig("attn_r", 1)
        aT_psum, aT_r, ao_psum, x4 = sig("attT_psum", 1), sig("attT_r", 1), sig("att_out_psum", 1), own("x4_ready", 1)
        xd, win_psum, x5 = sig("x_plus_depool", 1), sig("win_psum", 1), own("x5_ready", 1)
        pb_r, gl_psum, gl_r = sig("pooled_bcast", DT), sig("gate_psum", 1), own("gl_r", 1)
        gtop_r, ngt_r, ge_r, gm_r = own("gtop_r", 1), sig("ngt_r", 1), sig("gate_exp", 1), own("gates_r", 4)
        e_psum, e_r, acc_r = turns("expert_psum", NE), turns("expert_gelu", NE), turns("acc_r", NE)
        f_psum, y_r = sig("final_psum", 1), HalfSignal([sem(f"y_r{h}") for h in range(2)], 1, 1)
        y_out = HalfSignal([sem(f"y_stored{h}") for h in range(2)], 16, 1)
        EXPERTS = [(0, 0), (1, 0), (2, 0)] + [x for e in range(3, NE) for x in ((e - 3, 1), (e, 0))] + [(e, 1) for e in range(NE - 3, NE)]
        block = ctx.enter_context(nc.Block())

        @block.sync
        def _(sp):
            sp.dma_start(causal[:, :], a["c_causal"]).then_inc(s_const, 16)
            for h in range(2):
                sp.sem_inc(y_out.sems[h], y_out.first)
                sp.sem_inc(y_r.sems[h], y_r.first)
            with sp.Fori(0, PAIRS) as i:
                for b in [(i, 0), (i, 1)]:
                    h = b[1]
                    sp.wait_ge(*y_r(b))
                    sp.dma_start(a["out"][bass.ds((i * 2 + h) * S, S), :].rearrange("(t p) d -> p t d", p=P), y[h][:, :, :]).then_inc(y_out.sems[h], 16)
            for h in range(2):
                sp.wait_ge(*y_out((PAIRS - 1, h)))

        @block.gpsimd
        def _(pool):
            pool.memset(mhalf[:, :], -0.5).then_inc(s_half, 1)
            pool.wait_ge(s_half, 1)
            def gather(b):
                h = b[1]
                pool.wait_ge(*idx_r(b))
                pool.tensor_tensor(idle[:, h:h + 1], mhalf[:, 0:1], mhalf[:, 0:1], ALU.add).then_inc(idle_gr.sem, 1)
                for k in range(2 * TB):
                    pool.indirect_dma_start(
                        out=got[h][:, k, :], out_offset=None, in_=g["expert_rows"],
                        in_offset=bass.IndirectOffsetOnAxis(ap=rows_i[h][:, k:k + 1], axis=0),
                        bounds_check=NE * CAP - 1, oob_is_err=False).then_inc(got_in.sems[h], 16)

            for h in range(2):
                gather((0, h))

            def power(v, out, waits, done, b):
                pool.wait_ge(*waits)
                pool.tensor_tensor(out[b[1]][:, :], v[b[1]][:, :], mhalf[:, :], ALU.pow).then_inc(done, 1)

            def body(i, last_turn):
                B, after = [(i, 0), (i, 1)], [(i + 1, 0), (i + 1, 1)]
                if not last_turn:
                    for b in after:
                        gather(b)
                for b in B:
                    power(var, rstd, N5["var"](b), N5["rstd"].sem, b)
                    x = x_all[:, bass.ds(tile_of(b), TB), :]
                    pool.wait_ge(*N5["xn"](b))
                    pool.tensor_tensor(idle[:, 2 + b[1]:3 + b[1]], mhalf[:, 0:1], mhalf[:, 0:1], ALU.add).then_inc(idle_r.sem, 1)
                    pool.tensor_tensor(x, x, g["depool_all"][:, bass.ds(tile_of(b), TB), :], ALU.add).then_inc(xd.sem, 1)
                for b in B:
                    power(var, rstd, N6["var"](b), N6["rstd"].sem, b)
                finish(pool, [idle_r])
                if not last_turn:
                    for b in after:
                        power(var, rstd, N4["var"](b), N4["rstd"].sem, b)
                    finish(pool, [idle_gr])

            for h in range(2):
                power(var, rstd, N4["var"]((0, h)), N4["rstd"].sem, (0, h))
            finish(pool, [idle_gr])
            with pool.Fori(0, PAIRS - 1) as i:
                body(i, False)
            body(PAIRS - 1, True)

        @block.scalar
        def _(act):
            act.wait_ge(s_const, 16)
            act.activation(causalb[:, :], causal[:, :], ACT.Copy).then_inc(s_cast, 1)
            act.wait_ge(s_set, 5)

            def copy(out, psum, done, *waits, **kw):
                for w in waits:
                    act.wait_ge(*w)
                act.activation(out, psum, ACT.Copy, **kw).then_inc(done, 1)

            def body(i):
                B = [(i, 0), (i, 1)]
                for b in B:
                    h = b[1]
                    act.wait_ge(*N4["xt"](b))
                    for c in range(DT):
                        copy(xnT[h][:, c * S:(c + 1) * S], bank[h][0][:, c * S:(c + 1) * S], N4["xts"].sem)
                for b in B:
                    h = b[1]
                    for t in range(TB):
                        copy(qk[h][:, t, :], bank[h][2 + t][:, :], qk_r.sem, qk_psum(b, t + 1))
                for b in B:
                    h = b[1]
                    for q in range(NG):
                        copy(qkT[h][:, q, :, :].rearrange("p a c -> p (a c)"), bank[h][q][:, :], qkT_r.sem, qkT_psum(b, q + 1))
                def turned_out(b, gr):
                    copy(outT[b[1]], bank[b[1]][3][:, 0:S], oT_r.sems[b[1]], oT_psum(b, gr + 1))

                def heads_out(b, gr):
                    h = b[1]
                    copy(att[h][:, :, gr:RH:NG, :], bank[h][3][:, S:2 * S].rearrange("p (t a c) -> p t a c", t=TB, a=GH)[:, :, :, 0:RD + 1],
                         av_r.sems[h], av_psum(b, gr + 1))

                steps = [(b, gr) for gr in range(NG) for b in B]
                for n_step, (b, gr) in enumerate(steps):
                    h = b[1]
                    act.wait_ge(*nmax_r(b, gr + 1))
                    if gr > 0:
                        act.wait_ge(*kept_r(b, NT * gr))
                    for k, (o, n) in enumerate(SPAN):
                        if o % 512 == 0:
                            act.wait_ge(*rest_r(b, NT * gr + (o + 512) // n - (0 if k < GH else W1 // n - GH)))
                        src = bank[h][o // 512][:, o % 512:o % 512 + n]
                        last = act.activation(exps[h][:, o:o + n], src, ACT.Exp, bias=nmax[h][:, k:k + 1], scale=RD ** -0.5)
                    last.then_inc(exp_r.sems[h], 1)
                    if n_step < 2:
                        act.wait_ge(*v_psum(b))
                        for t in range(TB):
                            copy(vals[h][:, t, :, 0:RD], bank[h][3][:, t * D:(t + 1) * D].rearrange("p (a c) -> p a c", c=RD), v_r.sem)
                    if n_step >= 2:
                        turned_out(*steps[n_step - 2])
                        heads_out(*steps[n_step - 2])
                    if n_step == len(steps) - 1:
                        turned_out(*steps[-2])
                        heads_out(*steps[-2])
                    for q in range(3):
                        copy(keptT[h][:, q * 512:(q + 1) * 512], bank[h][q][:, :], kT_r.sems[h], kT_psum(b, 3 * gr + q + 1))
                turned_out(*steps[-1])
                copy(attT[B[0][1]][:, :], bank[B[0][1]][0][:, :], aT_r.sem, aT_psum(B[0]))
                heads_out(*steps[-1])
                copy(attT[B[1][1]][:, :], bank[B[1][1]][0][:, :], aT_r.sem, aT_psum(B[1]))
                for b in B:
                    h = b[1]
                    act.wait_ge(*N5["xt"](b))
                    for c in range(DT):
                        copy(xnT[h][:, c * S:(c + 1) * S], bank[h][2][:, c * S:(c + 1) * S], N5["xts"].sem, scale=g["g_res"][:, c:c + 1])
                for b in B:
                    h = b[1]
                    act.wait_ge(*N6["xt"](b))
                    for c in range(DT):
                        copy(xnT[h][:, c * S:(c + 1) * S], bank[h][0][:, c * S:(c + 1) * S], N6["xts"].sem, accum_out=pooled[h][:, c:c + 1])
                for e, h in EXPERTS:
                    b = B[h]
                    if e == 0:
                        act.wait_ge(*ngt_r(b))
                        act.activation(ge[h][:, :], gl[h][:, :], ACT.Exp, bias=ngt[h][:, 0:1]).then_inc(ge_r.sem, 1)
                    act.wait_ge(*e_psum(b, e + 1))
                    if e >= NH:
                        act.wait_ge(*acc_r(b, e - NH + 1))
                    for o in range(DT):
                        last = act.activation(hid[h][e % NH][:, o * S:(o + 1) * S], bank[h][e % 3][:, o * S:(o + 1) * S], ACT.Gelu,
                                              bias=g["expert_b"][:, e, o:o + 1])
                    last.then_inc(e_r.sems[h], 1)

            with act.Fori(0, PAIRS - 1) as i:
                body(i)
            body(PAIRS - 1)

        @block.tensor
        def _(pe):
            pe.wait_ge(s_cast, 1)
            pe.wait_ge(s_set, 5)

            def turn_rows(b):
                pe.wait_ge(*N4["xn"](b))
                transpose_rows(pe, bank[b[1]][0], xn[b[1]], identf).then_inc(N4["xt"].sem, 1)

            def body(i, last_turn):
                B, after = [(i, 0), (i, 1)], [(i + 1, 0), (i + 1, 1)]

                def scores(b, gr):
                    h = b[1]
                    r0 = 32 * gr
                    if gr == 0:
                        pe.wait_ge(*qkT_r(b))
                    else:
                        pe.wait_ge(*kT_r(b, 3 * gr))
                    for k, (o, n) in enumerate(SPAN):
                        q, t = k % GH, 1 if k < GH else 0
                        out = bank[h][o // 512][:, o % 512:o % 512 + n]
                        pe.matmul(out, qkT[h][r0:r0 + RD, q, 0, t * P:(t + 1) * P], qkT[h][r0:r0 + RD, q, 1, 0:n], start=True, stop=False)
                        last = pe.matmul(bank[h][o // 512][:, o % 512 + n - P:o % 512 + n], identb[:, :], causalb[:, :], start=False, stop=True)
                    last.then_inc(sc_psum.sems[h], 1)

                for b in B:
                    h = b[1]
                    pe.wait_ge(*N4["xts"](b))
                    pe.wait_ge(*y_r(b, 0))
                    for t in range(TB):
                        for k in range(DT):
                            last = pe.matmul(bank[h][2 + t][:, :], xnT[h][:, k * S + t * P:k * S + (t + 1) * P], g["qkv_w"][:, k, 0:512],
                                             start=(k == 0), stop=(k == DT - 1))
                        last.then_inc(qk_psum.sem, 1)
                for b in B:
                    h = b[1]
                    pe.wait_ge(*rope_r(b))
                    for gr in range(NG):
                        for q in range(2):
                            for t in range(TB):
                                last = pe.transpose(bank[h][gr][:, q * S + t * P:q * S + (t + 1) * P],
                                                    roped[h][:, t, q * RH + gr * GH:q * RH + (gr + 1) * GH, :].rearrange("p a c -> p (a c)"),
                                                    identf[:, :])
                        last.then_inc(qkT_psum.sem, 1)
                    scores(b, 0)
                    for t in range(TB):
                        for k in range(DT):
                            last = pe.matmul(bank[h][3][:, t * D:(t + 1) * D], xnT[h][:, k * S + t * P:k * S + (t + 1) * P],
                                             g["qkv_w"][:, k, 512:768], start=(k == 0), stop=(k == DT - 1))
                    last.then_inc(v_psum.sem, 1)

                def weighted(b, gr):
                    h = b[1]
                    pe.wait_ge(*kT_r(b, 3 * gr + 3))
                    if gr == 0:
                        pe.wait_ge(*v_r(b))
                    else:
                        pe.wait_ge(*av_r(b, gr))
                    for s in range(TB):
                        for j in range(GH):
                            last = pe.matmul(bank[h][3][32 * j:32 * j + 32, s * P:S], vals[h][:, s, j * NG + gr, :],
                                             keptT[h][:, (3 * j + 2 * s) * P:(3 * j + 2 + s) * P], start=(s == 0), stop=(s == TB - 1))
                    last.then_inc(oT_psum.sems[h], 1)

                def heads_back(b, gr):
                    h = b[1]
                    pe.wait_ge(*oT_r(b, gr + 1))
                    for t in range(TB):
                        last = pe.transpose(bank[h][3][:, S + t * P:S + (t + 1) * P], outT[h][:, t * P:(t + 1) * P], identf[:, :])
                    last.then_inc(av_psum.sems[h], 1)

                steps = [(b, gr) for gr in range(NG) for b in B]
                for n_step, (b, gr) in enumerate(steps):
                    h = b[1]
                    if n_step == len(steps) - 1:
                        weighted(*steps[-2])
                        heads_back(*steps[-2])
                    for q in range(3 * GH):
                        if q % 4 == 0:
                            pe.wait_ge(*kept_r(b, NT * gr + KEPT_FOR[q // 4]))
                        j, o = q // 3, (W1 + q // 3 * P, q // 3 * S, q // 3 * S + P)[q % 3]
                        last = pe.transpose(bank[h][q // 4][:, (q % 4) * P:(q % 4 + 1) * P], kept[h][:, o:o + P], identf[:, :])
                        if q % 4 == 3:
                            last.then_inc(kT_psum.sems[h], 1)
                    if 1 <= n_step < len(steps) - 1:
                        weighted(*steps[n_step - 1])
                    if gr < NG - 1:
                        scores(b, gr + 1)
                    if 1 <= n_step < len(steps) - 1:
                        heads_back(*steps[n_step - 1])

                def turn_heads(b):
                    pe.wait_ge(*attn_r(b))
                    transpose_rows(pe, bank[b[1]][0], attn[b[1]], identf).then_inc(aT_psum.sem, 1)

                def out_projection(b):
                    h = b[1]
                    pe.wait_ge(*aT_r(b))
                    for t in range(TB):
                        for k in range(DT):
                            last = pe.matmul(bank[h][1][:, t * D:(t + 1) * D], attT[h][:, k * S + t * P:k * S + (t + 1) * P],
                                             g["attn_out_w"][:, k, :], start=(k == 0), stop=(k == DT - 1))
                    last.then_inc(ao_psum.sem, 1)

                def turn_normed(N, b, k):
                    pe.wait_ge(*N["xn"](b))
                    transpose_rows(pe, bank[b[1]][k], xn[b[1]], identf).then_inc(N["xt"].sem, 1)

                def in_projection(b):
                    h = b[1]
                    pe.wait_ge(*N5["xts"](b))
                    for t in range(TB):
                        for k in range(DT):
                            last = pe.matmul(bank[h][1][:, t * D:(t + 1) * D], xnT[h][:, k * S + t * P:k * S + (t + 1) * P],
                                             g["win_w"][:, k, :], start=(k == 0), stop=(k == DT - 1))
                    last.then_inc(win_psum.sem, 1)

                def expert(b, e):
                    h = b[1]
                    if e == 0:
                        pe.wait_ge(*N6["xts"](b))
                    if e >= 3:
                        pe.wait_ge(*e_r(b, e - 2))
                    for o in range(DT):
                        for k in range(DT):
                            last = pe.matmul(bank[h][e % 3][:, o * S:(o + 1) * S], g["expert_w"][:, k, e * D + o * P:e * D + (o + 1) * P],
                                             xnT[h][:, k * S:(k + 1) * S], start=(k == 0), stop=(k == DT - 1))
                    last.then_inc(e_psum.sems[h], 1)

                def gate_logits(b):
                    h = b[1]
                    pe.wait_ge(*pb_r(b))
                    for k in range(DT):
                        last = pe.matmul(bank[h][3][:, 0:NE], pooledb[h][:, k, :], g["gate_w"][:, k, :], start=(k == 0), stop=(k == DT - 1))
                    last.then_inc(gl_psum.sem, 1)

                def turn_back(b):
                    h = b[1]
                    pe.wait_ge(*acc_r(b))
                    for t in range(TB):
                        for o in range(DT):
                            last = pe.transpose(bank[h][3][:, t * D + o * P:t * D + (o + 1) * P], acc[h][:, o * S + t * P:o * S + (t + 1) * P], identf[:, :])
                    last.then_inc(f_psum.sem, 1)

                turn_heads(B[0])
                weighted(*steps[-1])
                heads_back(*steps[-1])
                out_projection(B[0])
                turn_heads(B[1])
                out_projection(B[1])
                turn_normed(N5, B[0], 2)
                in_projection(B[0])
                turn_normed(N5, B[1], 2)
                in_projection(B[1])
                turn_normed(N6, B[0], 0)
                for e, h in EXPERTS:
                    if (e, h) == EXPERTS[2]:
                        turn_normed(N6, B[1], 0)
                    if (e, h) == EXPERTS[-1] and not last_turn:
                        pe.wait_ge(*e_r(B[0]))
                        turn_rows(after[0])
                    expert(B[h], e)
                    if e == 0:
                        gate_logits(B[h])
                turn_back(B[0])
                if not last_turn:
                    pe.wait_ge(*e_r(B[1]))
                    turn_rows(after[1])
                turn_back(B[1])

            for h in range(2):
                turn_rows((0, h))
            with pe.Fori(0, PAIRS - 1) as i:
                body(i, False)
            body(PAIRS - 1, True)

        @block.vector
        def _(dve):

            def xt(b):
                return lambda t: x_all[:, bass.ds(tile_of(b) + t, 1), :].rearrange("p a d -> p (a d)")

            def choices(b):
                h = b[1]
                dve.tensor_copy(rows_i[h][:, :].rearrange("p (t k) -> p t k", k=2), g["choice_row"][:, bass.ds(tile_of(b), TB), :]).then_inc(idx_r.sem, 1)
                dve.tensor_copy(wts[h][:, :, :], g["choice_w"][:, bass.ds(tile_of(b), TB), :]).then_inc(wts_r.sem, 1)

            def combine(b):
                h = b[1]
                dve.wait_ge(*wts_r(b))
                dve.wait_ge(*got_in(b))
                for k in range(2):
                    for t in range(TB):
                        if k:
                            dve.wait_ge(*comb(b, t + 1))
                        dve.scalar_tensor_tensor(xt(b)(t), got[h][:, 2 * t + k, :], wts[h][:, t, k:k + 1], xt(b)(t),
                                                 ALU.mult, ALU.add).then_inc(comb.sem, 1)

            def first_stats(b):
                dve.wait_ge(*comb(b))
                norm_stats(dve, xt(b), stats, mv, var, N4, b)

            def body(i, last_turn):
                B, after = [(i, 0), (i, 1)], [(i + 1, 0), (i + 1, 1)]
                for b in B:
                    h = b[1]
                    for t in range(TB):
                        q2 = qk[h][:, t, :].rearrange("p (a two) -> p a two", two=2)
                        o2 = turned[h][:, t, :].rearrange("p (a two) -> p a two", two=2)
                        s2 = g["rope_sin"][:, t, :].rearrange("p (a two) -> p a two", two=2)
                        heads = roped[h][:, t, :, 0:RD]
                        dve.wait_ge(*qk_r(b, t + 1))
                        for e in range(2):
                            dve.tensor_tensor(o2[:, :, e], q2[:, :, 1 - e], s2[:, :, e], ALU.mult).then_inc(rope_a.sem, 1)
                        dve.tensor_tensor(heads, qk[h][:, t, :].rearrange("p (a c) -> p a c", c=RD),
                                          g["rope_cos"][:, t, :].rearrange("p (a c) -> p a c", c=RD), ALU.mult).then_inc(rope_a.sem, 1)
                        dve.wait_ge(*rope_a(b, 3 * t + 3))
                        dve.tensor_tensor(heads, heads, turned[h][:, t, :].rearrange("p (a c) -> p a c", c=RD), ALU.add).then_inc(rope_r.sem, 1)
                if not last_turn:
                    for b in after:
                        choices(b)
                for gr in range(NG):
                    for b in B:
                        h = b[1]
                        dve.wait_ge(*sc_psum(b, gr + 1))
                        dve.memset(idle_v[:, 2 * gr + h:2 * gr + h + 1], 0.0).then_inc(idle_vr.sem, 1)
                        for k, (o, n) in enumerate(SPAN):
                            dve.max(top1[h][:, k, :], bank[h][o // 512][:, o % 512:o % 512 + n]).then_inc(top1_r.sems[h], 1)
                        for k, (o, n) in enumerate(SPAN):
                            dve.wait_ge(*top1_r(b, NT * gr + k + 1))
                            dve.match_replace(rest[h][:, o:o + n], top1[h][:, k, :], bank[h][o // 512][:, o % 512:o % 512 + n], -3.0e38).then_inc(rest_r.sems[h], 1)
                            if k == 0:
                                dve.wait_ge(*top1_r(b, NT * (gr + 1)))
                                dve.tensor_scalar(nmax[h][:, :], top1[h][:, :, 0], -RD ** -0.5, None, ALU.mult).then_inc(nmax_r.sems[h], 1)
                        for k, (o, n) in enumerate(SPAN):
                            dve.wait_ge(*rest_r(b, NT * gr + k + 1))
                            dve.max(top2[h][:, k, :], rest[h][:, o:o + n]).then_inc(top2_r.sems[h], 1)
                        dve.wait_ge(*exp_r(b, gr + 1))
                        for k in KEEP:
                            o, n = SPAN[k]
                            dve.wait_ge(*top2_r(b, NT * gr + k + 1))
                            dve.scalar_tensor_tensor(kept[h][:, o:o + n], bank[h][o // 512][:, o % 512:o % 512 + n], top2[h][:, k, TOPK - 9:TOPK - 8],
                                                     exps[h][:, o:o + n], ALU.is_ge, ALU.mult).then_inc(kept_r.sems[h], 1)

                def attention_rows(b):
                    h = b[1]
                    dve.wait_ge(*av_r(b))
                    dve.reciprocal(attr[h][:, :, :], att[h][:, :, :, RD]).then_inc(den_r.sem, 1)
                    dve.wait_ge(*den_r(b))
                    dve.tensor_tensor(attn[h][:, :, :].rearrange("p t (a c) -> p t a c", c=RD), att[h][:, :, :, 0:RD],
                                      attr[h][:, :, :].unsqueeze(3).broadcast_to([P, TB, RH, RD]), ALU.mult).then_inc(attn_r.sem, 1)

                def after_attention(b):
                    h = b[1]
                    x = x_all[:, bass.ds(tile_of(b), TB), :]
                    dve.wait_ge(*ao_psum(b))
                    dve.tensor_tensor(x, bank[h][1][:, :].rearrange("p (t d) -> p t d", t=TB), x, ALU.add).then_inc(x4.sem, 1)
                    dve.wait_ge(*x4(b))
                    norm_stats(dve, xt(b), stats, mv, var, N5, b, (1.0 + RMS_EPS, RMS_EPS * LN_EPS))

                def after_patches(b):
                    h = b[1]
                    x = x_all[:, bass.ds(tile_of(b), TB), :]
                    dve.wait_ge(*win_psum(b))
                    dve.wait_ge(*xd(b))
                    dve.tensor_tensor(x, bank[h][1][:, :].rearrange("p (t d) -> p t d", t=TB), x, ALU.add).then_inc(x5.sem, 1)
                    dve.wait_ge(*x5(b))
                    norm_stats(dve, xt(b), stats, mv, var, N6, b)

                def pooled_rows(b):
                    h = b[1]
                    dve.wait_ge(*N6["xts"](b))
                    for c in range(DT):
                        dve.tensor_scalar(pooledb[h][:, c, :], ones[:, :], pooled[h][:, c:c + 1], 1.0 / S, ALU.mult, ALU.mult).then_inc(pb_r.sem, 1)

                def gate(b):
                    h = b[1]
                    dve.wait_ge(*gl_psum(b))
                    dve.tensor_tensor(gl[h][:, :], bank[h][3][:, 0:NE], g["gate_b"][:, :], ALU.add).then_inc(gl_r.sem, 1)
                    dve.wait_ge(*gl_r(b))
                    dve.max(gtop[h][:, :], gl[h][:, :]).then_inc(gtop_r.sem, 1)
                    dve.wait_ge(*gtop_r(b))
                    dve.tensor_scalar(ngt[h][:, :], gtop[h][:, 0:1], -1.0, None, ALU.mult).then_inc(ngt_r.sem, 1)
                    dve.wait_ge(*ge_r(b))
                    dve.scalar_tensor_tensor(gates[h][:, :], gl[h][:, :], gtop[h][:, 1:2], ge[h][:, :], ALU.is_ge, ALU.mult).then_inc(gm_r.sem, 1)
                    dve.wait_ge(*gm_r(b, 1))
                    dve.tensor_reduce(gsum[h][:, :], gates[h][:, :], X, ALU.add).then_inc(gm_r.sem, 1)
                    dve.wait_ge(*gm_r(b, 2))
                    dve.reciprocal(gsum[h][:, :], gsum[h][:, :]).then_inc(gm_r.sem, 1)
                    dve.wait_ge(*gm_r(b, 3))
                    dve.tensor_scalar(gates[h][:, :], gates[h][:, :], gsum[h][:, 0:1], None, ALU.mult).then_inc(gm_r.sem, 1)

                def output(b):
                    h = b[1]
                    dve.wait_ge(*f_psum(b))
                    dve.wait_ge(*y_out(b, 0))
                    dve.tensor_tensor(y[h][:, :, :], bank[h][3][:, :].rearrange("p (t d) -> p t d", t=TB), x_all[:, bass.ds(tile_of(b), TB), :],
                                      ALU.add).then_inc(y_r.sems[h], 1)

                attention_rows(B[0])
                attention_rows(B[1])
                after_attention(B[0])
                norm_apply(dve, xt(B[0]), xn, mv, rstd, N5, B[0])
                after_attention(B[1])
                norm_apply(dve, xt(B[1]), xn, mv, rstd, N5, B[1])
                after_patches(B[0])
                norm_apply(dve, xt(B[0]), xn, mv, rstd, N6, B[0])
                after_patches(B[1])
                pooled_rows(B[0])
                norm_apply(dve, xt(B[1]), xn, mv, rstd, N6, B[1])
                gate(B[0])
                pooled_rows(B[1])
                for n, (e, h) in enumerate(EXPERTS):
                    b = B[h]
                    if (e, h) == (0, 1):
                        gate(b)
                    dve.wait_ge(*e_r(b, e + 1))
                    if e == 0:
                        dve.wait_ge(*gm_r(b))
                        dve.tensor_scalar(acc[h][:, :], hid[h][0][:, :], gates[h][:, 0:1], None, ALU.mult).then_inc(acc_r.sems[h], 1)
                    else:
                        dve.wait_ge(*acc_r(b, e))
                        dve.scalar_tensor_tensor(acc[h][:, :], hid[h][e % NH][:, :], gates[h][:, e:e + 1], acc[h][:, :], ALU.mult, ALU.add).then_inc(acc_r.sems[h], 1)
                    if not last_turn:
                        if n in (4, 6):
                            combine(after[n // 2 - 2])
                        if n in (8, 9):
                            first_stats(after[n - 8])
                        if n in (10, 11):
                            norm_apply(dve, xt(after[n - 10]), xn, mv, rstd, N4, after[n - 10])
                for b in B:
                    output(b)
                finish(dve, dve_own)
                if not last_turn:
                    finish(dve, early_own)

            for h in range(2):
                choices((0, h))
            dve.memset(ones[:, :], 1.0).then_inc(s_set, 1)
            for h in range(2):
                dve.memset(vals[h][:, :, :, RD:32], 0.0).then_inc(s_zero, 1)
                dve.memset(roped[h][:, :, :, RD:32], 0.0).then_inc(s_set, 1)
            dve.wait_ge(s_zero, 2)
            for h in range(2):
                dve.memset(vals[h][:, :, :, RD], 1.0).then_inc(s_set, 1)
            dve.wait_ge(s_set, 5)
            for h in range(2):
                combine((0, h))
            for h in range(2):
                first_stats((0, h))
            for h in range(2):
                norm_apply(dve, xt((0, h)), xn, mv, rstd, N4, (0, h))
            finish(dve, early_own)
            with dve.Fori(0, PAIRS - 1) as i:
                body(i, False)
            body(PAIRS - 1, True)


def constants():
    import numpy as np

    n = np.arange(1, RD // 2 + 1, dtype=np.float64)
    t = 10.0 + 6.0 * n
    for _ in range(60):
        f = t / (2 * np.pi) * np.log(t / (2 * np.pi * np.e)) - (n - 0.875)
        t = t - f / (np.log(t / (2 * np.pi)) / (2 * np.pi))
    z = t / t[0]
    denom = 0.25 + z * z
    w_re = (0.5 / denom).astype(np.float32).astype(np.float64)
    w_im = (-z / denom).astype(np.float32).astype(np.float64)
    pos = np.arange(S, dtype=np.float32)
    K = RD // 2
    phase = pos[:, None] * (10000.0 ** (-np.arange(K, dtype=np.float32) / K))[None, :]
    cos, sin = np.cos(phase).astype(np.float32).astype(np.float64), np.sin(phase).astype(np.float32).astype(np.float64)
    grow = np.sqrt(1.0 + pos.astype(np.float64))[:, None]
    kc = np.stack([cos, cos], -1) * grow[:, :, None]
    ks = np.stack([sin, -sin], -1) * grow[:, :, None]
    qc1 = w_re * cos + w_im * sin
    qs1 = w_re * sin - w_im * cos
    qc = np.stack([qc1, qc1], -1) / grow[:, :, None]
    qs = np.stack([qs1, -qs1], -1) / grow[:, :, None]
    c_cos = np.concatenate([np.tile(qc.reshape(S, RD), (1, RH)), np.tile(kc.reshape(S, RD), (1, RH))], 1).astype(np.float32)
    c_sin = np.concatenate([np.tile(qs.reshape(S, RD), (1, RH)), np.tile(ks.reshape(S, RD), (1, RH))], 1).astype(np.float32)
    logp = np.float32(-0.001)
    dt = -np.log(-np.expm1(logp))
    decay, first = float(np.exp(-dt)), float(np.exp(logp))
    i, j = np.arange(S)[:, None], np.arange(S)[None, :]
    gap = np.where(j >= i, j - i, 0)
    c_decayT = np.where(j >= i, first * decay ** gap, 0.0)
    pi, pj = np.arange(P)[:, None], np.arange(P)[None, :]
    return {
        "c_ident": np.eye(P, dtype=np.float32),
        "c_before": (pi < pj).astype(np.float32),
        "c_causal": np.where(pj > pi, NEG, 0.0).astype(np.float32),
        "c_cos": c_cos, "c_sin": c_sin,
        "c_decayT": c_decayT.astype(np.float32),
        "c_upto": (i <= j).astype(np.float32),
    }


def kernel(**inputs):
    import numpy as np
    import concourse.bacc as bacc
    from concourse.bass_utils import run_bass_kernel_spmd

    v = {k: np.asarray(x) for k, x in inputs.items()}
    cols = lambda x: x.reshape(-1, P).T
    arrays = {
        "x": v["x"].reshape(NB * S, D), "ctx": v["ctx_2048"].reshape(NB * S, DC),
        "ctxT": v["ctx_2048"].transpose(0, 2, 1).reshape(NB * DC, S),
        "mask": v["mask_BxS2_fk1"].reshape(-1), "maskC": cols(v["mask_BxS2_fk1"].reshape(-1)),
        "patch_lens": v["mask_BxS2_if0"].reshape(-1),
        "L0_xattn_W_srcT": v["L0_xattn_W_src"].T, "L0_xattn_W_tgtT": v["L0_xattn_W_tgt"].T,
        "L0_xattn_W_outT": v["L0_xattn_W_out"].T, "L0_xattn_b_srcC": cols(v["L0_xattn_b_src"]),
        "L0_xattn_b_tgtC": cols(v["L0_xattn_b_tgt"]),
        "L0_ffn_w1": v["L0_ffn_w1"].reshape(NE * D, F), "L0_ffn_w2": v["L0_ffn_w2"].reshape(NE * F, D),
        "L0_ffn_b1C": v["L0_ffn_b1"].reshape(NE, FT, P).transpose(0, 2, 1).reshape(NE * P, FT),
        "L0_ffn_b2": v["L0_ffn_b2"].reshape(-1),
        "L1_xattn_g_resC": cols(v["L1_xattn_g_res"]),
        "L1_xattn_W_inT": v["L1_xattn_W_in"].T,
        "L1_ffn_gate_wT": v["L1_ffn_gate_w"].T,
        "L1_ffn_expert_wT": v["L1_ffn_expert_w"].transpose(2, 0, 1).reshape(D, NE * D),
        "L1_ffn_expert_bC": v["L1_ffn_expert_b"].reshape(NE, DT, P).transpose(2, 0, 1),
    }
    for k in ("L0_attn_Wq", "L0_attn_Wk", "L0_attn_Wv", "L0_attn_Wo", "L0_attn_bo", "L0_xattn_b_src", "L0_xattn_b_out",
              "L0_ffn_w_router", "L0_ffn_b_router", "L1_attn_Wq", "L1_attn_Wk", "L1_attn_Wv", "L1_attn_Wo",
              "L1_xattn_b_in", "L1_xattn_g_init", "L1_ffn_gate_b"):
        arrays[k] = v[k]
    arrays.update(constants())
    nc = bacc.Bacc("TRN2", target_bir_lowering=False, num_devices=1)
    a, feed = {}, {}
    for k, x in arrays.items():
        feed[f"in_{k}"] = np.ascontiguousarray(x)
        a[k] = nc.dram_tensor(f"in_{k}", x.shape, mybir.dt.from_np(x.dtype), kind="ExternalInput").ap()
    a["out"] = nc.dram_tensor("y_dram", (NB * S, D), F32, kind="ExternalOutput").ap()
    decoder(nc, a)
    r = run_bass_kernel_spmd(nc, [feed], core_ids=[0])
    return r.results[0]["y_dram"].reshape(NB, S, D)
```
